# Optimizing a Trainium2 kernel written in Bass

```python
import numpy as np
import jax
import jax.numpy as jnp

def _softmax(x, axis=-1):
    return jax.nn.softmax(x, axis=axis)

def _gelu(x):
    return jax.nn.gelu(x, approximate=True)

def _silu(x):
    return jax.nn.silu(x)

def _sigmoid(x):
    return jax.nn.sigmoid(x)

def _layernorm(x, axis=-1, eps=1e-05):
    m = jnp.mean(x, axis=axis, keepdims=True)
    v = jnp.var(x, axis=axis, keepdims=True)
    return (x - m) / jnp.sqrt(v + eps)

def _scatter_add(tgt, idx, src, axis=0):
    return tgt.at[idx].add(src)

def _segment_sum(src, seg, n):
    return jax.ops.segment_sum(src, seg, n)
kernel_name = 'mk_perceiver_d2_seqx_r8_024309'

def setup_inputs(seed: int=0):
    np.random.seed(seed)
    _w = jnp.asarray

    def _rec_inputs():
        import jax
        import jax.numpy as jnp
        _rk = jax.random.key(seed)
        x = -0.0003929 + 0.9999 * jax.random.normal(jax.random.fold_in(_rk, 1), (4, 32, 128), jnp.float32)
        _lenS = 32 - jax.random.randint(jax.random.fold_in(_rk, 7), (4,), 0, max(1, 32 // 4) + 1, jnp.int32)
        _lenS2 = 512 - jax.random.randint(jax.random.fold_in(_rk, 8), (4,), 0, max(1, 512 // 4) + 1, jnp.int32)
        _ctx_1024P = jax.random.normal(jax.random.fold_in(_rk, 11), (4, 16, 128), jnp.float32)
        _ctx_1024c = jax.random.dirichlet(jax.random.fold_in(_rk, 511), 0.3 * jnp.ones((16,), jnp.float32), (4, 512))
        _ctx_1024t = jnp.einsum('bsk,bkd->bsd', _ctx_1024c, _ctx_1024P)
        _ctx_1024t = _ctx_1024t * jax.lax.rsqrt(jnp.mean(jnp.square(_ctx_1024t)) + 1e-12) * 0.953939
        ctx_1024 = 4.13588e-05 + 0.999923 * (_ctx_1024t + 0.3 * jax.random.normal(jax.random.fold_in(_rk, 611), (4, 512, 128), jnp.float32))
        return (x, ctx_1024)
    x, ctx_1024 = _rec_inputs()

    def _L0_xattn_setup():
        import jax, jax.numpy as jnp
        import numpy as np
        H = 128
        B = 8
        L_CHAR = 256
        L_SUB = 128

        def _linear(x, W, b):
            return jnp.einsum('blh,oh->blo', x, W) + b

        def _interp_linear(x, out_len):
            L_in = x.shape[1]
            pos = (jnp.arange(out_len, dtype=x.dtype) + 0.5) * (L_in / out_len) - 0.5
            pos = jnp.clip(pos, 0.0, L_in - 1)
            lo = jnp.floor(pos).astype(jnp.int32)
            hi = jnp.minimum(lo + 1, L_in - 1)
            w = (pos - lo.astype(x.dtype))[None, :, None]
            return x[:, lo] * (1 - w) + x[:, hi] * w
        key = jax.random.key(seed)
        ks = jax.random.split(key, 18)
        s = 0.02
        inp = {'char_emb': jax.random.normal(ks[0], (B, L_CHAR, H), jnp.float32), 'subword_emb': jax.random.normal(ks[1], (B, L_SUB, H), jnp.float32)}
        names = ['Wq_c', 'Wk_s', 'Wv_s', 'Wq_s', 'Wk_c', 'Wv_c']
        for i, n in enumerate(names):
            inp[n] = jax.random.normal(ks[2 + 2 * i], (H, H), jnp.float32) * s
            inp['b' + n[1:]] = jax.random.normal(ks[3 + 2 * i], (H,), jnp.float32) * s
        inp['Wg'] = jax.random.normal(ks[14], (H, 2 * H), jnp.float32) * s
        inp['bg'] = jax.random.normal(ks[15], (H,), jnp.float32) * s
        return inp
    _L0_xattn_all = _L0_xattn_setup()
    _L0_xattn_in = {k: v for k, v in _L0_xattn_all.items() if k in ('Wq_c', 'bq_c', 'Wk_s', 'bk_s', 'Wv_s', 'bv_s', 'Wq_s', 'bq_s', 'Wk_c', 'bk_c', 'Wv_c', 'bv_c', 'Wg', 'bg')}
    del _L0_xattn_all

    def _L0_attn_setup():
        import jax, jax.numpy as jnp
        import numpy as np
        EPS = 1e-05
        key = jax.random.key(seed)
        ks = jax.random.split(key, 8)
        B, T, C, H = (2, 256, 128, 16)
        hs = C // H
        scale = 1.0 / np.sqrt(C)
        x = jax.random.normal(ks[0], (B, T, C), dtype=jnp.float32)
        wq1 = jax.random.normal(ks[1], (H, C, hs), dtype=jnp.float32) * scale
        wk1 = jax.random.normal(ks[2], (H, C, hs), dtype=jnp.float32) * scale
        wq2 = jax.random.normal(ks[3], (H, C, hs), dtype=jnp.float32) * scale
        wk2 = jax.random.normal(ks[4], (H, C, hs), dtype=jnp.float32) * scale
        wv = jax.random.normal(ks[5], (H, C, hs), dtype=jnp.float32) * scale
        ln_gamma = jnp.ones((C,), dtype=jnp.float32)
        ln_beta = jnp.zeros((C,), dtype=jnp.float32)
        lamb = jnp.float32(0.8)
        return {'x': x, 'wq1': wq1, 'wk1': wk1, 'wq2': wq2, 'wk2': wk2, 'wv': wv, 'ln_gamma': ln_gamma, 'ln_beta': ln_beta, 'lamb': lamb}
    _L0_attn_all = _L0_attn_setup()
    _L0_attn_in = {k: v for k, v in _L0_attn_all.items() if k in ('wq1', 'wk1', 'wq2', 'wk2', 'wv', 'ln_gamma', 'ln_beta', 'lamb')}
    del _L0_attn_all

    def _L0_ffn_setup():
        import jax, jax.numpy as jnp
        import numpy as np
        E = 8
        K = 2
        key = jax.random.key(seed)
        ks = jax.random.split(key, 6)
        B, S, D, F = (4, 256, 128, 512)
        s_d = 1.0 / np.sqrt(D).astype(np.float32)
        s_f = 1.0 / np.sqrt(F).astype(np.float32)
        return {'x': jax.random.normal(ks[0], (B, S, D), jnp.float32), 'ln_w': jnp.ones((D,), jnp.float32), 'Wg': jax.random.normal(ks[1], (D, E), jnp.float32) * s_d, 'bg': jnp.zeros((E,), jnp.float32), 'W1a': jax.random.normal(ks[2], (E, D, F), jnp.float32) * s_d, 'b1a': jnp.zeros((E, F), jnp.float32), 'W1b': jax.random.normal(ks[3], (E, D, F), jnp.float32) * s_d, 'b1b': jnp.zeros((E, F), jnp.float32), 'W2': jax.random.normal(ks[4], (E, F, D), jnp.float32) * s_f, 'b2': jnp.zeros((E, D), jnp.float32)}
    _L0_ffn_all = _L0_ffn_setup()
    _L0_ffn_in = {k: v for k, v in _L0_ffn_all.items() if k in ('ln_w', 'Wg', 'bg', 'W1a', 'b1a', 'W1b', 'b1b', 'W2', 'b2')}
    del _L0_ffn_all

    def _L1_xattn_setup():
        import jax, jax.numpy as jnp
        import numpy as np
        N_STATE = 128
        N_HEAD = 16
        D_K = N_STATE // N_HEAD
        key = jax.random.key(seed)
        ks = jax.random.split(key, 12)
        B, S = (2, 256)
        s = 1.0 / np.sqrt(N_STATE)
        inp = {'q': jax.random.normal(ks[0], (B, S, N_STATE), jnp.float32), 'k': jax.random.normal(ks[1], (B, S, N_STATE), jnp.float32), 'v': jax.random.normal(ks[2], (B, S, N_STATE), jnp.float32), 'Wq': jax.random.normal(ks[3], (N_STATE, N_STATE), jnp.float32) * s, 'bq': jax.random.normal(ks[4], (N_STATE,), jnp.float32) * s, 'Wk': jax.random.normal(ks[5], (N_STATE, N_STATE), jnp.float32) * s, 'bk': jax.random.normal(ks[6], (N_STATE,), jnp.float32) * s, 'Wv': jax.random.normal(ks[7], (N_STATE, N_STATE), jnp.float32) * s, 'bv': jax.random.normal(ks[8], (N_STATE,), jnp.float32) * s, 'Wo': jax.random.normal(ks[9], (N_STATE, N_STATE), jnp.float32) * s, 'bo': jax.random.normal(ks[10], (N_STATE,), jnp.float32) * s}
        return inp
    _L1_xattn_all = _L1_xattn_setup()
    _L1_xattn_in = {k: v for k, v in _L1_xattn_all.items() if k in ('Wq', 'bq', 'Wk', 'bk', 'Wv', 'bv', 'Wo', 'bo')}
    del _L1_xattn_all

    def _L1_attn_setup():
        import jax, jax.numpy as jnp
        import numpy as np
        B, T, D = (2, 256, 128)
        H = 16
        DH = D // H

        def alibi_bias(n_heads, token_cnt, dtype=jnp.float32):
            slopes = 2.0 ** (-8.0 * jnp.arange(1, n_heads + 1, dtype=dtype) / n_heads)
            pos = jnp.arange(token_cnt, dtype=dtype)
            rel = pos[None, :] - pos[:, None]
            return slopes[:, None, None] * rel[None, :, :]
        key = jax.random.key(seed)
        ks = jax.random.split(key, 5)
        s = 1.0 / np.sqrt(D)
        return {'x': jax.random.normal(ks[0], (B, T, D), dtype=jnp.float32), 'W_query': jax.random.normal(ks[1], (D, D), dtype=jnp.float32) * s, 'W_key': jax.random.normal(ks[2], (D, D), dtype=jnp.float32) * s, 'W_value': jax.random.normal(ks[3], (D, D), dtype=jnp.float32) * s, 'W_proj': jax.random.normal(ks[4], (D, D), dtype=jnp.float32) * s, 'b_proj': jnp.zeros((D,), dtype=jnp.float32)}
    _L1_attn_all = _L1_attn_setup()
    _L1_attn_in = {k: v for k, v in _L1_attn_all.items() if k in ('W_query', 'W_key', 'W_value', 'W_proj', 'b_proj')}
    del _L1_attn_all

    def _L1_ffn_setup():
        import jax, jax.numpy as jnp
        import numpy as np
        B, T, C, H, E = (1, 32, 128, 256, 8)
        STD = 0.02
        key = jax.random.key(seed)
        ks = jax.random.split(key, 8)
        f32 = jnp.float32
        return {'x': jax.random.normal(ks[0], (B, T, C), f32), 'up': jax.random.normal(ks[1], (E, H, C), f32) * STD, 'gate': jax.random.normal(ks[2], (E, H, C), f32) * STD, 'down': jax.random.normal(ks[3], (E, C, H), f32) * STD, 'router': jax.random.normal(ks[4], (E, C), f32) * STD, 'w_up_s': jax.random.normal(ks[5], (H, C), f32) * STD, 'w_gate_s': jax.random.normal(ks[6], (H, C), f32) * STD, 'w_down_s': jax.random.normal(ks[7], (C, H), f32) * STD}
    _L1_ffn_all = _L1_ffn_setup()
    _L1_ffn_in = {k: v for k, v in _L1_ffn_all.items() if k in ('up', 'gate', 'down', 'router', 'w_up_s', 'w_gate_s', 'w_down_s')}
    del _L1_ffn_all
    return {'x': x, 'ctx_1024': ctx_1024, 'L0_xattn_Wq_c': _L0_xattn_in['Wq_c'], 'L0_xattn_bq_c': _L0_xattn_in['bq_c'], 'L0_xattn_Wk_s': _L0_xattn_in['Wk_s'], 'L0_xattn_bk_s': _L0_xattn_in['bk_s'], 'L0_xattn_Wv_s': _L0_xattn_in['Wv_s'], 'L0_xattn_bv_s': _L0_xattn_in['bv_s'], 'L0_xattn_Wq_s': _L0_xattn_in['Wq_s'], 'L0_xattn_bq_s': _L0_xattn_in['bq_s'], 'L0_xattn_Wk_c': _L0_xattn_in['Wk_c'], 'L0_xattn_bk_c': _L0_xattn_in['bk_c'], 'L0_xattn_Wv_c': _L0_xattn_in['Wv_c'], 'L0_xattn_bv_c': _L0_xattn_in['bv_c'], 'L0_xattn_Wg': _L0_xattn_in['Wg'], 'L0_xattn_bg': _L0_xattn_in['bg'], 'L0_attn_wq1': _L0_attn_in['wq1'], 'L0_attn_wk1': _L0_attn_in['wk1'], 'L0_attn_wq2': _L0_attn_in['wq2'], 'L0_attn_wk2': _L0_attn_in['wk2'], 'L0_attn_wv': _L0_attn_in['wv'], 'L0_attn_ln_gamma': _L0_attn_in['ln_gamma'], 'L0_attn_ln_beta': _L0_attn_in['ln_beta'], 'L0_attn_lamb': _L0_attn_in['lamb'], 'L0_ffn_ln_w': _L0_ffn_in['ln_w'], 'L0_ffn_Wg': _L0_ffn_in['Wg'], 'L0_ffn_bg': _L0_ffn_in['bg'], 'L0_ffn_W1a': _L0_ffn_in['W1a'], 'L0_ffn_b1a': _L0_ffn_in['b1a'], 'L0_ffn_W1b': _L0_ffn_in['W1b'], 'L0_ffn_b1b': _L0_ffn_in['b1b'], 'L0_ffn_W2': _L0_ffn_in['W2'], 'L0_ffn_b2': _L0_ffn_in['b2'], 'L1_xattn_Wq': _L1_xattn_in['Wq'], 'L1_xattn_bq': _L1_xattn_in['bq'], 'L1_xattn_Wk': _L1_xattn_in['Wk'], 'L1_xattn_bk': _L1_xattn_in['bk'], 'L1_xattn_Wv': _L1_xattn_in['Wv'], 'L1_xattn_bv': _L1_xattn_in['bv'], 'L1_xattn_Wo': _L1_xattn_in['Wo'], 'L1_xattn_bo': _L1_xattn_in['bo'], 'L1_attn_W_query': _L1_attn_in['W_query'], 'L1_attn_W_key': _L1_attn_in['W_key'], 'L1_attn_W_value': _L1_attn_in['W_value'], 'L1_attn_W_proj': _L1_attn_in['W_proj'], 'L1_attn_b_proj': _L1_attn_in['b_proj'], 'L1_ffn_up': _L1_ffn_in['up'], 'L1_ffn_gate': _L1_ffn_in['gate'], 'L1_ffn_down': _L1_ffn_in['down'], 'L1_ffn_router': _L1_ffn_in['router'], 'L1_ffn_w_up_s': _L1_ffn_in['w_up_s'], 'L1_ffn_w_gate_s': _L1_ffn_in['w_gate_s'], 'L1_ffn_w_down_s': _L1_ffn_in['w_down_s']}

def reference(x, ctx_1024, L0_xattn_Wq_c, L0_xattn_bq_c, L0_xattn_Wk_s, L0_xattn_bk_s, L0_xattn_Wv_s, L0_xattn_bv_s, L0_xattn_Wq_s, L0_xattn_bq_s, L0_xattn_Wk_c, L0_xattn_bk_c, L0_xattn_Wv_c, L0_xattn_bv_c, L0_xattn_Wg, L0_xattn_bg, L0_attn_wq1, L0_attn_wk1, L0_attn_wq2, L0_attn_wk2, L0_attn_wv, L0_attn_ln_gamma, L0_attn_ln_beta, L0_attn_lamb, L0_ffn_ln_w, L0_ffn_Wg, L0_ffn_bg, L0_ffn_W1a, L0_ffn_b1a, L0_ffn_W1b, L0_ffn_b1b, L0_ffn_W2, L0_ffn_b2, L1_xattn_Wq, L1_xattn_bq, L1_xattn_Wk, L1_xattn_bk, L1_xattn_Wv, L1_xattn_bv, L1_xattn_Wo, L1_xattn_bo, L1_attn_W_query, L1_attn_W_key, L1_attn_W_value, L1_attn_W_proj, L1_attn_b_proj, L1_ffn_up, L1_ffn_gate, L1_ffn_down, L1_ffn_router, L1_ffn_w_up_s, L1_ffn_w_gate_s, L1_ffn_w_down_s):
    import jax
    import jax.numpy as jnp

    def _L0_xattn_ref(char_emb, subword_emb, Wq_c, bq_c, Wk_s, bk_s, Wv_s, bv_s, Wq_s, bq_s, Wk_c, bk_c, Wv_c, bv_c, Wg, bg):
        import jax, jax.numpy as jnp
        import numpy as np
        H = 128
        B = 8
        L_CHAR = 256
        L_SUB = 128

        def _linear(x, W, b):
            return jnp.einsum('blh,oh->blo', x, W) + b

        def _interp_linear(x, out_len):
            L_in = x.shape[1]
            pos = (jnp.arange(out_len, dtype=x.dtype) + 0.5) * (L_in / out_len) - 0.5
            pos = jnp.clip(pos, 0.0, L_in - 1)
            lo = jnp.floor(pos).astype(jnp.int32)
            hi = jnp.minimum(lo + 1, L_in - 1)
            w = (pos - lo.astype(x.dtype))[None, :, None]
            return x[:, lo] * (1 - w) + x[:, hi] * w
        h = char_emb.shape[-1]
        scale = 1.0 / jnp.sqrt(jnp.asarray(h, char_emb.dtype))
        Q_char = _linear(char_emb, Wq_c, bq_c)
        K_sub = _linear(subword_emb, Wk_s, bk_s)
        V_sub = _linear(subword_emb, Wv_s, bv_s)
        scores = jnp.einsum('bqh,bkh->bqk', Q_char, K_sub) * scale
        char2sub = jnp.einsum('bqk,bkh->bqh', jax.nn.softmax(scores, axis=-1), V_sub)
        Q_sub = _linear(subword_emb, Wq_s, bq_s)
        K_char = _linear(char_emb, Wk_c, bk_c)
        V_char = _linear(char_emb, Wv_c, bv_c)
        scores2 = jnp.einsum('bqh,bkh->bqk', Q_sub, K_char) * scale
        sub2char = jnp.einsum('bqk,bkh->bqh', jax.nn.softmax(scores2, axis=-1), V_char)
        L_char = char_emb.shape[1]
        if sub2char.shape[1] != L_char:
            sub2char = _interp_linear(sub2char, L_char)
        gate_in = jnp.concatenate([char2sub, sub2char], axis=-1)
        gate = jax.nn.sigmoid(jnp.einsum('blh,oh->blo', gate_in, Wg) + bg)
        return gate * char2sub + (1 - gate) * sub2char

    def _L0_attn_ref(x, wq1, wk1, wq2, wk2, wv, ln_gamma, ln_beta, lamb):
        import jax, jax.numpy as jnp
        import numpy as np
        EPS = 1e-05
        B, T, C = x.shape
        H, _, hs = wq1.shape
        inv_sqrt_d = jnp.asarray(hs, x.dtype) ** (-0.5)
        q1 = jnp.einsum('btc,hcd->bhtd', x, wq1)
        k1 = jnp.einsum('btc,hcd->bhtd', x, wk1)
        q2 = jnp.einsum('btc,hcd->bhtd', x, wq2)
        k2 = jnp.einsum('btc,hcd->bhtd', x, wk2)
        v = jnp.einsum('btc,hcd->bhtd', x, wv)
        w1 = jax.nn.softmax(jnp.einsum('bhtd,bhsd->bhts', q1, k1) * inv_sqrt_d, axis=-1)
        w2 = jax.nn.softmax(jnp.einsum('bhtd,bhsd->bhts', q2, k2) * inv_sqrt_d, axis=-1)
        wei = w1 - lamb * w2
        out = jnp.einsum('bhts,bhsd->bhtd', wei, v)
        out = out.transpose(0, 2, 1, 3).reshape(B, T, H * hs)
        mu = out.mean(axis=-1, keepdims=True)
        var = out.var(axis=-1, keepdims=True)
        out = (out - mu) * jax.lax.rsqrt(var + EPS) * ln_gamma + ln_beta
        return (1.0 - lamb) * out

    def _L0_ffn_ref(x, ln_w, Wg, bg, W1a, b1a, W1b, b1b, W2, b2):
        import jax, jax.numpy as jnp
        import numpy as np
        E = 8
        K = 2
        B, S, D = x.shape
        eps = jnp.finfo(x.dtype).eps
        xn = x * jax.lax.rsqrt(jnp.mean(x * x, axis=-1, keepdims=True) + eps) * ln_w
        logits = xn @ Wg + bg
        vals, idx = jax.lax.top_k(logits, K)
        topk_w = jax.nn.softmax(vals, axis=-1)
        we = jnp.sum(jax.nn.one_hot(idx, E, dtype=x.dtype) * topk_w[..., None], axis=-2)
        T = B * S
        xf = xn.reshape(T, D)
        wef = we.reshape(T, E).T

        def step(acc, params):
            W1a_e, b1a_e, W1b_e, b1b_e, W2_e, b2_e, w_e = params
            a = xf @ W1a_e + b1a_e
            b = xf @ W1b_e + b1b_e
            y = jax.nn.silu(a) * b @ W2_e + b2_e
            return (acc + w_e[:, None] * y, None)
        out0 = jnp.zeros_like(xf)
        out, _ = jax.lax.scan(step, out0, (W1a, b1a, W1b, b1b, W2, b2, wef))
        return out.reshape(B, S, D)

    def _L1_xattn_ref(q, k, v, Wq, bq, Wk, bk, Wv, bv, Wo, bo):
        import jax, jax.numpy as jnp
        import numpy as np
        N_STATE = 128
        N_HEAD = 16
        D_K = N_STATE // N_HEAD
        B = q.shape[0]

        def proj(x, W, b):
            y = jnp.einsum('bsi,oi->bso', x, W) + b
            return y.reshape(B, -1, N_HEAD, D_K).transpose(0, 2, 1, 3)
        qh = proj(q, Wq, bq)
        kh = proj(k, Wk, bk)
        vh = proj(v, Wv, bv)
        scores = jnp.einsum('bhqd,bhkd->bhqk', qh, kh) / np.sqrt(D_K).astype(np.float32)
        attn = jax.nn.softmax(scores, axis=-1)
        out = jnp.einsum('bhqk,bhkd->bhqd', attn, vh)
        out = out.transpose(0, 2, 1, 3).reshape(B, -1, N_HEAD * D_K)
        return jnp.einsum('bsi,oi->bso', out, Wo) + bo

    def _L1_attn_ref(x, W_query, W_key, W_value, W_proj, b_proj):
        import jax, jax.numpy as jnp
        import numpy as np
        B, T, D = (2, 256, 128)
        H = 16
        DH = D // H

        def alibi_bias(n_heads, token_cnt, dtype=jnp.float32):
            slopes = 2.0 ** (-8.0 * jnp.arange(1, n_heads + 1, dtype=dtype) / n_heads)
            pos = jnp.arange(token_cnt, dtype=dtype)
            rel = pos[None, :] - pos[:, None]
            return slopes[:, None, None] * rel[None, :, :]
        b, t, _ = x.shape

        def heads(y):
            return y.reshape(b, t, H, DH).transpose(0, 2, 1, 3)
        q = heads(x @ W_query)
        k = heads(x @ W_key)
        v = heads(x @ W_value)
        scores = jnp.einsum('bhqd,bhkd->bhqk', q, k)
        causal = jnp.triu(jnp.ones((t, t), dtype=bool), k=1)
        scores = jnp.where(causal[None, None], -jnp.inf, scores)
        scores = scores + alibi_bias(H, t, scores.dtype)[None]
        scores = scores / jnp.sqrt(jnp.asarray(DH, scores.dtype))
        w = jax.nn.softmax(scores, axis=-1)
        ctx = jnp.einsum('bhqk,bhkd->bqhd', w, v).reshape(b, t, H * DH)
        return ctx @ W_proj + b_proj

    def _L1_ffn_ref(x, up, gate, down, router, w_up_s, w_gate_s, w_down_s):
        import jax, jax.numpy as jnp
        import numpy as np
        B, T, C, H, E = (1, 32, 128, 256, 8)
        STD = 0.02
        b, t, c = x.shape
        x_ = x.reshape(b * t, c)
        logits = x_ @ router.T
        idx = jnp.argmax(logits, axis=-1)
        onehot = jax.nn.one_hot(idx, router.shape[0], dtype=x.dtype)
        u = jnp.einsum('bc,ehc->ebh', x_, up)
        g = jnp.einsum('bc,ehc->ebh', x_, gate)
        h = jax.nn.silu(g) * u
        ye = jnp.einsum('ebh,ech->ebc', h, down)
        y = jnp.einsum('ebc,be->bc', ye, onehot)
        ys = jax.nn.silu(x_ @ w_gate_s.T) * (x_ @ w_up_s.T) @ w_down_s.T
        return (y + ys).reshape(b, t, c)
    x = x + _L0_xattn_ref(_layernorm(x, axis=-1), ctx_1024, L0_xattn_Wq_c, L0_xattn_bq_c, L0_xattn_Wk_s, L0_xattn_bk_s, L0_xattn_Wv_s, L0_xattn_bv_s, L0_xattn_Wq_s, L0_xattn_bq_s, L0_xattn_Wk_c, L0_xattn_bk_c, L0_xattn_Wv_c, L0_xattn_bv_c, L0_xattn_Wg, L0_xattn_bg)
    x = x + _L0_attn_ref(_layernorm(x, axis=-1), L0_attn_wq1, L0_attn_wk1, L0_attn_wq2, L0_attn_wk2, L0_attn_wv, L0_attn_ln_gamma, L0_attn_ln_beta, L0_attn_lamb)
    x = x + _L0_ffn_ref(_layernorm(x, axis=-1), L0_ffn_ln_w, L0_ffn_Wg, L0_ffn_bg, L0_ffn_W1a, L0_ffn_b1a, L0_ffn_W1b, L0_ffn_b1b, L0_ffn_W2, L0_ffn_b2)
    x = x + _L1_xattn_ref(_layernorm(x, axis=-1), ctx_1024, ctx_1024, L1_xattn_Wq, L1_xattn_bq, L1_xattn_Wk, L1_xattn_bk, L1_xattn_Wv, L1_xattn_bv, L1_xattn_Wo, L1_xattn_bo)
    x = x + _L1_attn_ref(_layernorm(x, axis=-1), L1_attn_W_query, L1_attn_W_key, L1_attn_W_value, L1_attn_W_proj, L1_attn_b_proj)
    x = x + _L1_ffn_ref(_layernorm(x, axis=-1), L1_ffn_up, L1_ffn_gate, L1_ffn_down, L1_ffn_router, L1_ffn_w_up_s, L1_ffn_w_gate_s, L1_ffn_w_down_s)
    return x

_drawn_inputs = setup_inputs


def setup_inputs(seed=0):
    import zlib

    import numpy as np

    out = dict(_drawn_inputs(seed))
    spreads = {'L0_attn_ln_gamma': (1.0, 0.2),
     'L0_attn_ln_beta': (0.0, 0.1),
     'L0_ffn_ln_w': (1.0, 0.2),
     'L0_ffn_bg': (0.0, 0.1),
     'L0_ffn_b1a': (0.0, 0.1),
     'L0_ffn_b1b': (0.0, 0.1),
     'L0_ffn_b2': (0.0, 0.1),
     'L1_attn_b_proj': (0.0, 0.1)}
    factors = {'L0_xattn_bq_c': 8.0,
     'L0_xattn_bk_s': 8.0,
     'L0_xattn_Wq_s': 8.0,
     'L0_xattn_bq_s': 8.0,
     'L0_xattn_Wk_c': 8.0,
     'L0_xattn_bk_c': 8.0,
     'L0_xattn_bv_c': 4.785,
     'L0_xattn_Wg': 8.0,
     'L0_xattn_bg': 8.0,
     'L1_xattn_bq': 2.912,
     'L1_xattn_bk': 8.0,
     'L1_ffn_up': 8.0,
     'L1_ffn_gate': 8.0,
     'L1_ffn_down': 8.0,
     'L1_ffn_router': 8.0,
     'L1_ffn_w_up_s': 8.0,
     'L1_ffn_w_gate_s': 8.0,
     'L1_ffn_w_down_s': 8.0}
    for name, (base, spread) in spreads.items():
        noise = np.random.default_rng([zlib.crc32(name.encode()), seed]).standard_normal(out[name].shape)
        drawn = base * np.exp(spread * noise) if base else spread * noise
        out[name] = jnp.asarray(drawn.astype(out[name].dtype))
    for name, factor in factors.items():
        out[name] = (out[name] * factor).astype(out[name].dtype)
    return out
```

```python
from contextlib import ExitStack

import numpy as np
import concourse.bass as bass
from concourse import mybir

F32 = mybir.dt.float32
U32 = mybir.dt.uint32
ALU = mybir.AluOpType
ACT = mybir.ActivationFunctionType
AX = mybir.AxisListType.X

P = 128
B, L, D = 4, 32, 128
NCTX = 512
KC = NCTX // P
H, DH = 16, 8
NJ, HL = 4, 4
QW = D // NJ
E0N, F0 = 8, 512
FC0 = F0 // P
E1N, F1 = 8, 256
FC1 = F1 // P
R = NCTX // L
LO = R // 2 - 1
EPS = 1e-5
RMS_EPS = float(np.finfo(np.float32).eps)
SC0 = float(D) ** -0.5
SCH = float(DH) ** -0.5

(C_BQC, C_BKS, C_BVS, C_BQS, C_BKC, C_BVC, C_BG, C_LNW, C_BQ1, C_BK1, C_BV1) = range(11)
C_B1A = 11
C_B1B = C_B1A + E0N * FC0
N_COLS = C_B1B + E0N * FC0
R_GAMMA, R_BETA, R_BO, R_BPROJ, R_BG, R_LAMB = 0, D, 2 * D, 3 * D, 4 * D, 4 * D + E0N
N_ROWS = R_LAMB + 1
K_ID = 0
K_MF = K_ID + P
K_MP = K_MF + HL
K_MB = K_MP + HL
K_SEL = K_MB + B
K_IOTA = K_SEL + L
K_ALIBI = K_IOTA + E0N
N_CONST = K_ALIBI + NJ * L
MASKED = -1e30


def shape_constants():
    k = np.zeros((P, N_CONST), np.float32)
    p = np.arange(P)
    k[:, K_ID:K_ID + P] = np.eye(P)
    k[:, K_MF:K_MF + HL] = (p[:, None] // DH) % HL == np.arange(HL)
    k[:, K_MP:K_MP + HL] = p[:, None] // L == np.arange(HL)
    k[:, K_MB:K_MB + B] = p[:, None] // L == np.arange(B)
    k[:, K_SEL:K_SEL + L] = p[:, None] % L == np.arange(L)
    k[:, K_IOTA:K_IOTA + E0N] = np.arange(E0N)
    slopes = np.float32(2.0) ** (np.float32(-8.0) * np.arange(1, H + 1, dtype=np.float32) / np.float32(H))
    for j in range(NJ):
        for hl in range(HL):
            t = np.arange(L, dtype=np.float32)
            bias = slopes[j * HL + hl] * (t[None, :] - t[:, None])
            bias[t[None, :] > t[:, None]] = MASKED
            k[hl * L:(hl + 1) * L, K_ALIBI + j * L:K_ALIBI + (j + 1) * L] = bias
    return k


def build(nc, A, out):
    with ExitStack() as ctx:
        def sb(name, shape, dt=F32):
            return ctx.enter_context(nc.sbuf_tensor(name, shape, dt))

        class Sems(dict):
            def __missing__(self, name):
                self[name] = ctx.enter_context(nc.semaphore(name))
                return self[name]

        s = Sems()

        x0 = sb("x0", [P, D])
        con = sb("con", [P, N_CONST])
        col = sb("col", [P, N_COLS])
        row = sb("row", [P, N_ROWS])
        w0 = sb("w0", [P, 8, D])
        w1 = sb("w1", [P, 5, D])
        w2 = sb("w2", [P, 8, D])
        wr = sb("wr", [P, 2, E0N])
        b2 = sb("b2", [E0N, D])
        ctxT = sb("ctxT", [P, B * NCTX])
        ctxN = sb("ctxN", [P, B * KC, D])
        wab = sb("wab", [P, E0N, 2, F0])
        wdn = sb("wdn", [P, E0N, FC0, D])
        wgu = sb("wgu", [P, E1N + 1, 2, F1])
        wdo = sb("wdo", [P, E1N + 1, FC1, D])

        ident = con[:, K_ID:K_ID + P]
        mask_f = con[:, K_MF:K_MF + HL]
        mask_p = con[:, K_MP:K_MP + HL]
        mask_b = con[:, K_MB:K_MB + B]
        sel = con[:, K_SEL:K_SEL + L]
        iota = con[:, K_IOTA:K_IOTA + E0N]
        alibi = con[:, K_ALIBI:K_ALIBI + NJ * L].rearrange("p (j s) -> p j s", j=NJ)

        def cv(i):
            return col[:, i:i + 1]

        half = sb("half", [P, 1])
        st6 = sb("st6", [P, 6, 6])
        mv = sb("mv", [P, 6, 2])
        ve = sb("ve", [P, 8])
        rs = sb("rs", [P, 8])
        yN = sb("yN", [P, D])
        yT = sb("yT", [P, D])
        xs = [x0] + [sb(f"x{i}", [P, D]) for i in range(1, 7)]
        qcT = sb("qcT", [P, P])
        kcT = sb("kcT", [P, P])
        vc = sb("vc", [P, D])
        qpT = sb("qpT", [P, P])
        qbk = sb("qbk", [P, 1])
        qsT = sb("qsT", [P, 2, P])
        m0 = sb("m0", [P, 4])
        e0 = sb("e0", [P, NCTX])
        e0n = sb("e0n", [P, NCTX])
        p0T = sb("p0T", [P, KC, P])
        pcT = sb("pcT", [P, P])
        c2sT = sb("c2sT", [P, P])
        s2 = sb("s2", [P, 2, L])
        e2 = sb("e2", [P, 2, L])
        p2 = sb("p2", [P, 2, L])
        m2 = sb("m2", [P, 8])
        pa = sb("pa", [P, L])
        paT = sb("paT", [P, L])
        paBD = sb("paBD", [P, P])
        s2cT = sb("s2cT", [P, P])
        hbg = sb("hbg", [P, 1])
        th = sb("th", [P, P])
        dif = sb("dif", [P, P])
        base = sb("base", [P, P])
        td = sb("td", [P, P])
        oT0 = sb("oT0", [P, P])
        qb = sb("qb", [P, 2, B, HL, L])
        kT = sb("kT", [P, 2, P])
        vN = sb("vN", [P, D])
        mx = sb("mx", [P, 2, NJ, B])
        ex = sb("ex", [P, 2, NJ, P])
        eT = sb("eT", [P, 2, NJ, P])
        sm = sb("sm", [P, 2, NJ, B])
        rc = sb("rc", [P, 2, NJ, B])
        mask2 = sb("mask2", [P, HL])
        rm = sb("rm", [P, 2, B, NJ, HL])
        um = sb("um", [P, 2, B, D])
        gl = sb("gl", [P, D])
        xb = sb("xb", [P, D])
        oml = sb("oml", [P, 1])
        tz = sb("tz", [P, D])
        qb3 = sb("qb3", [P, B, HL, L])
        kT3 = sb("kT3", [P, P])
        vN3 = sb("vN3", [P, D])
        mx3 = sb("mx3", [P, NJ, B])
        ex3 = sb("ex3", [P, NJ, P])
        eT3 = sb("eT3", [P, NJ, P])
        sm3 = sb("sm3", [P, NJ, B])
        rc3 = sb("rc3", [P, NJ, B])
        rm3 = sb("rm3", [P, B, NJ, HL])
        um3 = sb("um3", [P, B, D])
        aT3 = sb("aT3", [P, P])
        kx = sb("kx", [P, B, NCTX])
        vx = sb("vx", [P, B, KC, NJ, QW + 1])
        qxT = sb("qxT", [P, P])
        qbx = sb("qbx", [P, B, HL, L])
        nmx = sb("nmx", [P, B * NJ])
        xe = sb("xe", [P, 3, NCTX])
        xeT = sb("xeT", [P, 3, KC, P])
        rx = sb("rx", [P, B, NJ])
        rmx = sb("rmx", [P, B, NJ, HL])
        umx = sb("umx", [P, B, D])
        aTx = sb("aTx", [P, P])
        lg = sb("lg", [P, 2, E0N])
        top = sb("top", [P, 2, 8])
        idx = sb("idx", [P, 2, 8], U32)
        idf = sb("idf", [P, 2, 8])
        tw = sb("tw", [P, 6])
        oh = sb("oh", [P, 4, E0N])
        weT = sb("weT", [E0N, P])
        sa = sb("sa", [P, 4, P])
        hT = sb("hT", [P, 2, FC0, P])
        acc = sb("acc", [P, 2, D])
        sa1 = sb("sa1", [P, 3, FC1, P])
        hT1 = sb("hT1", [P, 3, FC1, P])
        acc1 = sb("acc1", [P, 2, D])

        PS = ctx.enter_context(nc.psum_tensor("PS", [P, 8, 512], F32))
        quad = PS[:, 0:4, :]

        block = ctx.enter_context(nc.Block())

        @block.sync
        def _(sp):
            sp.dma_start(x0[:], A["x"]).then_inc(s["x_in"], 16)
            sp.dma_start(con[:], A["con"]).then_inc(s["con_in"], 16)
            sp.dma_start(w0[:], A["w0"]).then_inc(s["w0_in"], 16)
            sp.dma_start(col[:], A["col"]).then_inc(s["col_in"], 16)
            sp.dma_start(ctxT[:], A["ctxT"]).then_inc(s["ctxT_in"], 16)
            sp.dma_start(w2[:], A["w2"]).then_inc(s["w2_in"], 16)
            sp.dma_start(ctxN[:], A["ctxN"]).then_inc(s["ctxN_in"], 16)
            sp.dma_start(w1[:], A["w1"]).then_inc(s["w1_in"], 16)
            sp.dma_start(row[:], A["row"].partition_broadcast(P)).then_inc(s["row_in"], 16)
            sp.dma_start(wr[:], A["wr"]).then_inc(s["wr_in"], 16)
            sp.dma_start(b2[:], A["b2"]).then_inc(s["b2_in"], 16)
            for e in range(0, E0N, 2):
                sp.dma_start(wab[:, e:e + 2], A["wab"][:, e:e + 2]).then_inc(s[f"wab{e}_in"], 16)
                sp.dma_start(wdn[:, e:e + 2], A["wdn"][:, e:e + 2]).then_inc(s[f"wdn{e}_in"], 16)
            sp.dma_start(wgu[:], A["wgu"]).then_inc(s["wgu_in"], 16)
            sp.dma_start(wdo[:], A["wdo"]).then_inc(s["wdo_in"], 16)
            sp.wait_ge(s["x"], 5)
            sp.dma_start(out, xs[6][:]).then_inc(s["out_done"], 16)
            sp.wait_ge(s["out_done"], 16)

        @block.gpsimd
        def _(g):
            g.memset(half[:], -0.5).then_inc(s["half"], 1)
            g.memset(vx[:, :, :, :, QW:QW + 1], 1.0).then_inc(s["vx_ones"], 1)
            g.wait_ge(s["half"], 1)

            def rsqrt(k):
                g.wait_ge(s["var"], k + 1)
                g.tensor_tensor(rs[:, k:k + 1], ve[:, k:k + 1], half[:], ALU.pow).then_inc(s["rstd"], 1)

            rsqrt(0)
            rsqrt(1)
            rsqrt(2)
            rsqrt(3)
            rsqrt(4)
            g.wait_ge(s["rstd"], 5)
            g.tensor_tensor(rs[:, 3:4], rs[:, 3:4], rs[:, 4:5], ALU.mult).then_inc(s["ln2_scale"], 1)
            rsqrt(5)
            rsqrt(6)
            rsqrt(7)

        @block.vector
        def _(v):
            steps = [0]

            def step():
                steps[0] += 1
                return steps[0]

            def layernorm(k, n):
                src = xs[n]
                v.bn_stats(st6[:, n, :], src[:]).then_inc(s["v_step"], 1)
                v.wait_ge(s["v_step"], step())
                v.bn_aggr(mv[:, n, :], st6[:, n, :]).then_inc(s["v_step"], 1)
                v.wait_ge(s["v_step"], step())
                v.tensor_scalar(ve[:, k:k + 1], mv[:, n, 1:2], EPS, None, ALU.add).then_inc(s["var"], 1)
                v.wait_ge(s["rstd"], k + 1)
                if n:
                    v.wait_ge(s["yN_turned"], n)
                v.tensor_scalar(yN[:], src[:], mv[:, n, 0:1], rs[:, k:k + 1], ALU.subtract, ALU.mult).then_inc(s["yN"], 1)

            v.wait_ge(s["x_in"], 16)
            layernorm(0, 0)
            v.wait_ge(s["yN_turned"], 1)
            v.tensor_copy(yT[:], PS[:, 7, 0:P]).then_inc(s["yT"], 1)
            v.wait_ge(s["col_in"], 16)
            v.wait_ge(s["qc_mm"], 1)
            v.tensor_scalar(qcT[:], PS[:, 7, 0:P], cv(C_BQC), SC0, ALU.add, ALU.mult).then_inc(s["qcT"], 1)
            v.wait_ge(s["qp_mm"], 1)
            v.tensor_copy(qpT[:], PS[:, 7, 0:P]).then_inc(s["qpT"], 1)
            v.tensor_copy(qbk[:], PS[:, 7, P:P + 1]).then_inc(s["qbk"], 1)
            v.tensor_scalar(hbg[:], cv(C_BG), 0.5, None, ALU.mult).then_inc(s["hbg"], 1)
            v.wait_ge(s["s0_mm"], 1)
            v.tensor_reduce(m0[:, 0:1], PS[:, 0, :], AX, ALU.max, negate=True).then_inc(s["v_step"], 1)
            v.wait_ge(s["v_step"], step())
            v.wait_ge(s["qbk"], 1)
            v.scalar_tensor_tensor(m0[:, 1:2], m0[:, 0:1], qbk[:, 0:1], qbk[:], ALU.subtract, ALU.add).then_inc(s["m0b"], 1)
            v.wait_ge(s["s2_mm"], 1)
            sc2 = PS[:, 5, 256:256 + 2 * L].rearrange("p (r s) -> p r s", r=2)
            v.tensor_reduce(m2[:, 0:2], sc2, AX, ALU.max).then_inc(s["v_step"], 1)
            v.wait_ge(s["v_step"], step())
            v.tensor_tensor(s2[:], sc2, m2[:, 0:2].unsqueeze(2).broadcast_to([P, 2, L]), ALU.subtract).then_inc(s["s2"], 1)
            v.wait_ge(s["e0"], 1)
            v.reciprocal(m0[:, 3:4], m0[:, 2:3]).then_inc(s["v_step"], 1)
            v.wait_ge(s["v_step"], step())
            v.tensor_scalar(e0n[:], e0[:], m0[:, 3:4], None, ALU.mult).then_inc(s["e0n"], 1)
            v.wait_ge(s["e2"], 1)
            v.tensor_reduce(m2[:, 2:4], e2[:], AX, ALU.add).then_inc(s["v_step"], 1)
            v.wait_ge(s["v_step"], step())
            v.reciprocal(m2[:, 4:6], m2[:, 2:4]).then_inc(s["v_step"], 1)
            v.wait_ge(s["v_step"], step())
            v.tensor_tensor(p2[:], e2[:], m2[:, 4:6].unsqueeze(2).broadcast_to([P, 2, L]), ALU.mult).then_inc(s["p2"], 1)
            v.wait_ge(s["p0_turned"], 1)
            v.tensor_copy(p0T[:, 0:2, :], PS[:, 4, 0:2 * P].rearrange("p (c k) -> p c k", c=2)).then_inc(s["p0T_a"], 1)
            v.wait_ge(s["p2"], 1)
            v.tensor_tensor(pa[:], p2[:, 0, :], p2[:, 1, :], ALU.add).then_inc(s["v_step"], 1)
            v.wait_ge(s["v_step"], step())
            v.transpose(paT[:], pa[:]).then_inc(s["v_step"], 1)
            v.wait_ge(s["v_step"], step())
            v.tensor_tensor(paBD[:].rearrange("p (b i) -> p b i", b=B), paT[:].unsqueeze(1).broadcast_to([P, B, L]),
                            mask_b.unsqueeze(2).broadcast_to([P, B, L]), ALU.mult).then_inc(s["paBD"], 1)
            v.wait_ge(s["pc_mm"], 1)
            v.tensor_copy(pcT[:], PS[:, 0, 0:P]).then_inc(s["pcT"], 1)
            v.wait_ge(s["s2c_mm"], 1)
            v.tensor_scalar(s2cT[:], PS[:, 5, 384:384 + P], 0.5, cv(C_BVC), ALU.mult, ALU.add).then_inc(s["s2cT"], 1)
            v.wait_ge(s["c2s_mm"], 1)
            v.tensor_scalar(c2sT[:], PS[:, 7, 0:P], cv(C_BVS), None, ALU.add).then_inc(s["c2sT"], 1)
            v.wait_ge(s["c2sT"], 1)
            v.wait_ge(s["s2cT"], 1)
            v.tensor_tensor(dif[:], c2sT[:], s2cT[:], ALU.subtract).then_inc(s["v_step"], 1)
            v.wait_ge(s["v_step"], step())
            v.scalar_tensor_tensor(base[:], dif[:], 0.5, s2cT[:], ALU.mult, ALU.add).then_inc(s["base"], 1)
            v.wait_ge(s["th"], 1)
            v.scalar_tensor_tensor(td[:], dif[:], 0.5, th[:], ALU.mult, ALU.mult).then_inc(s["v_step"], 1)
            v.wait_ge(s["v_step"], step())
            v.wait_ge(s["base"], 1)
            v.tensor_tensor(oT0[:], td[:], base[:], ALU.add).then_inc(s["oT0"], 1)
            v.wait_ge(s["o0_turned"], 1)
            v.tensor_tensor(xs[1][:], PS[:, 4, 0:P], x0[:], ALU.add).then_inc(s["x"], 1)

            v.wait_ge(s["x"], 1)
            layernorm(1, 1)
            v.wait_ge(s["yN_turned"], 2)
            v.tensor_copy(yT[:], PS[:, 7, 0:P]).then_inc(s["yT"], 1)

            def spread(dst, src):
                return v.tensor_tensor(dst, src.rearrange("p (b t) -> p b t", b=B).unsqueeze(2).broadcast_to([P, B, HL, L]),
                                       mask_f.unsqueeze(1).unsqueeze(3).broadcast_to([P, B, HL, L]), ALU.mult)

            v.wait_ge(s["q12_mm"], 1)
            spread(qb[:, 0], PS[:, 6, 0:P]).then_inc(s["qb"], 1)
            v.wait_ge(s["q12_mm"], 2)
            spread(qb[:, 1], PS[:, 7, 0:P]).then_inc(s["qb"], 1)
            v.wait_ge(s["row_in"], 16)
            lamb = row[:, R_LAMB:R_LAMB + 1]
            v.tensor_scalar(oml[:], lamb, -1.0, 1.0, ALU.mult, ALU.add).then_inc(s["oml"], 1)
            v.tensor_scalar(mask2[:], mask_p, lamb, -1.0, ALU.mult, ALU.mult).then_inc(s["mask2"], 1)
            v.wait_ge(s["oml"], 1)
            v.tensor_scalar(gl[:], row[:, R_GAMMA:R_GAMMA + D], oml[:], None, ALU.mult).then_inc(s["gl"], 1)
            v.scalar_tensor_tensor(xb[:], row[:, R_BETA:R_BETA + D], oml[:, 0:1], xs[1][:], ALU.mult, ALU.add).then_inc(s["xb"], 1)
            for n in range(2):
                v.wait_ge(s["s1_mm"], n + 1)
                sc = PS[:, 4 * n:4 * n + 4, 0:P].rearrange("p j (b s) -> p j b s", b=B)
                v.tensor_reduce(mx[:, n], sc, AX, ALU.max).then_inc(s["v_step"], 1)
                v.wait_ge(s["v_step"], step())
                for j in range(NJ):
                    last = v.tensor_tensor(ex[:, n, j, :].rearrange("p (b s) -> p b s", b=B), sc[:, j],
                                           mx[:, n, j, :].unsqueeze(2).broadcast_to([P, B, L]), ALU.subtract)
                last.then_inc(s["ex1_sub"], 1)
            for n in range(2):
                v.wait_ge(s["ex1"], n + 1)
                v.tensor_reduce(sm[:, n], ex[:, n].rearrange("p j (b s) -> p j b s", b=B), AX, ALU.add).then_inc(s["v_step"], 1)
                v.wait_ge(s["v_step"], step())
                v.reciprocal(rc[:, n], sm[:, n]).then_inc(s["v_step"], 1)
                v.wait_ge(s["v_step"], step())
                if n == 1:
                    v.wait_ge(s["mask2"], 1)
                m = mask_p if n == 0 else mask2[:]
                v.tensor_tensor(rm[:, n], rc[:, n].rearrange("p j b -> p b j").unsqueeze(3).broadcast_to([P, B, NJ, HL]),
                                m.unsqueeze(1).unsqueeze(1).broadcast_to([P, B, NJ, HL]), ALU.mult).then_inc(s["rm1"], 1)
            v.wait_ge(s["e1_turned"], 2)
            v.tensor_copy(eT[:, 1], PS[:, 4, :].rearrange("p (j k) -> p j k", j=NJ)).then_inc(s["eT_1"], 1)
            for n in range(2):
                v.wait_ge(s["u1_mm"], n + 1)
                v.wait_ge(s["rm1"], n + 1)
                v.tensor_tensor(um[:, n].rearrange("p b (g d) -> p b g d", d=DH),
                                PS[:, 4 * n:4 * n + 4, 0:P].rearrange("p b (g d) -> p b g d", d=DH),
                                rm[:, n].rearrange("p b j h -> p b (j h)").unsqueeze(3).broadcast_to([P, B, H, DH]),
                                ALU.mult).then_inc(s["um1"], 1)
            v.wait_ge(s["a1_mm"], 1)
            a1 = PS[:, 0, 0:D]
            v.bn_stats(st6[:, 5, :], a1).then_inc(s["v_step"], 1)
            v.wait_ge(s["v_step"], step())
            v.bn_aggr(mv[:, 5, :], st6[:, 5, :]).then_inc(s["v_step"], 1)
            v.wait_ge(s["v_step"], step())
            v.tensor_scalar(ve[:, 2:3], mv[:, 5, 1:2], EPS, None, ALU.add).then_inc(s["var"], 1)
            v.wait_ge(s["gl"], 1)
            v.scalar_tensor_tensor(tz[:], a1, mv[:, 5, 0:1], gl[:], ALU.subtract, ALU.mult).then_inc(s["v_step"], 1)
            v.wait_ge(s["v_step"], step())
            v.wait_ge(s["xb"], 1)
            v.wait_ge(s["rstd"], 3)
            v.scalar_tensor_tensor(xs[2][:], tz[:], rs[:, 2:3], xb[:], ALU.mult, ALU.add).then_inc(s["x"], 1)

            v.wait_ge(s["x"], 2)
            v.bn_stats(st6[:, 2, :], xs[2][:]).then_inc(s["v_step"], 1)
            v.wait_ge(s["v_step"], step())
            v.bn_aggr(mv[:, 2, :], st6[:, 2, :]).then_inc(s["v_step"], 1)
            v.wait_ge(s["v_step"], step())
            v.tensor_scalar(ve[:, 3:4], mv[:, 2, 1:2], EPS, None, ALU.add).then_inc(s["var"], 1)
            v.wait_ge(s["rstd"], 4)
            v.tensor_scalar(tw[:, 5:6], mv[:, 2, 1:2], rs[:, 3:4], rs[:, 3:4], ALU.mult, ALU.mult).then_inc(s["v_step"], 1)
            v.wait_ge(s["v_step"], step())
            v.tensor_scalar(ve[:, 4:5], tw[:, 5:6], RMS_EPS, None, ALU.add).then_inc(s["var"], 1)
            v.wait_ge(s["ln2_scale"], 1)
            v.wait_ge(s["yN_turned"], 2)
            v.tensor_scalar(yN[:], xs[2][:], mv[:, 2, 0:1], rs[:, 3:4], ALU.subtract, ALU.mult).then_inc(s["yN"], 1)
            v.wait_ge(s["yN_turned"], 3)
            v.tensor_scalar(yT[:], PS[:, 7, 0:P], cv(C_LNW), None, ALU.mult).then_inc(s["yT"], 1)

            def route(n, bias):
                v.wait_ge(s["lg_mm"], n + 1)
                lgp = PS[:, 6, 0:E0N]
                if bias is None:
                    v.tensor_copy(lg[:, n], lgp).then_inc(s["lg"], 1)
                else:
                    v.tensor_tensor(lg[:, n], lgp, bias, ALU.add).then_inc(s["lg"], 1)
                v.wait_ge(s["lg"], n + 1)
                v.max(top[:, n], lg[:, n]).then_inc(s["v_step"], 1)
                v.wait_ge(s["v_step"], step())
                v.max_index(idx[:, n], top[:, n], lg[:, n]).then_inc(s["v_step"], 1)
                v.wait_ge(s["v_step"], step())
                v.tensor_copy(idf[:, n], idx[:, n]).then_inc(s["idf"], 1)

            route(0, row[:, R_BG:R_BG + E0N])
            v.tensor_tensor(tw[:, 0:1], top[:, 0, 1:2], top[:, 0, 0:1], ALU.subtract).then_inc(s["tw_d"], 1)
            v.wait_ge(s["tw_e"], 1)
            v.tensor_scalar(tw[:, 2:3], tw[:, 1:2], 1.0, None, ALU.add).then_inc(s["v_step"], 1)
            v.wait_ge(s["v_step"], step())
            v.reciprocal(tw[:, 3:4], tw[:, 2:3]).then_inc(s["v_step"], 1)
            v.wait_ge(s["v_step"], step())
            v.tensor_tensor(tw[:, 4:5], tw[:, 1:2], tw[:, 3:4], ALU.mult).then_inc(s["v_step"], 1)
            v.wait_ge(s["v_step"], step())
            v.wait_ge(s["idf"], 1)
            v.tensor_scalar(oh[:, 0], iota, idf[:, 0, 0:1], tw[:, 3:4], ALU.is_equal, ALU.mult).then_inc(s["oh"], 1)
            v.tensor_scalar(oh[:, 1], iota, idf[:, 0, 1:2], tw[:, 4:5], ALU.is_equal, ALU.mult).then_inc(s["oh"], 1)
            v.wait_ge(s["oh"], 2)
            v.tensor_tensor(oh[:, 2], oh[:, 0], oh[:, 1], ALU.add).then_inc(s["we"], 1)

            def gate0(e, f):
                n = e * FC0 + f
                v.wait_ge(s["ab_mm"], e + 1)
                v.wait_ge(s["sa"], n + 1)
                if e >= 2 and f == 0:
                    v.wait_ge(s["y_mm"], e - 1)
                v.scalar_tensor_tensor(hT[:, e % 2, f], PS[:, 2 + e % 2, f * P:(f + 1) * P],
                                       cv(C_B1B + n), sa[:, n % 4], ALU.add, ALU.mult).then_inc(s["hT"], 1)

            def add0(e):
                v.wait_ge(s["y_mm"], e + 1)
                v.wait_ge(s["acc"], e + 1)
                v.scalar_tensor_tensor(acc[:, (e + 1) % 2] if e < E0N - 1 else xs[3][:],
                                       PS[:, 4 + e % 2, 0:D], oh[:, 2, e:e + 1], acc[:, e % 2],
                                       ALU.mult, ALU.add).then_inc(s["acc"], 1)

            for e in range(E0N):
                for f in range(FC0):
                    gate0(e, f)
                if e == 0:
                    v.wait_ge(s["we_turned"], 1)
                    v.tensor_copy(weT[:], PS[0:E0N, 6, 0:P]).then_inc(s["weT"], 1)
                if e == 1:
                    v.wait_ge(s["b2_mm"], 1)
                    v.tensor_tensor(acc[:, 0], PS[:, 6, 0:P], xs[2][:], ALU.add).then_inc(s["acc"], 1)
                if e >= 1:
                    add0(e - 1)
            add0(E0N - 1)

            v.wait_ge(s["acc"], E0N + 1)
            layernorm(5, 3)
            v.wait_ge(s["yN_turned"], 4)
            v.tensor_copy(yT[:], PS[:, 7, 0:P]).then_inc(s["yT"], 1)
            v.wait_ge(s["qx_mm"], 1)
            v.tensor_scalar(qxT[:], PS[:, 7, 0:P], cv(C_BQ1), SCH, ALU.add, ALU.mult).then_inc(s["v_step"], 1)
            v.wait_ge(s["v_step"], step())
            spread(qbx[:], qxT[:]).then_inc(s["qbx"], 1)

            def peak(n):
                v.wait_ge(s["sx_mm"], n + 1)
                v.tensor_reduce(nmx[:, n:n + 1], PS[:, n % NJ, :], AX, ALU.max, negate=True).then_inc(s["nmx"], 1)

            def turned(n):
                v.wait_ge(s["xe_turned"], n + 1)
                if n >= 3:
                    v.wait_ge(s["ux_mm"], n - 2)
                v.tensor_copy(xeT[:, n % 3], PS[:, 5, :].rearrange("p (c k) -> p c k", c=KC)).then_inc(s["xeT_odd"], 1)

            def keep_blocks(h):
                v.wait_ge(s["ux_mm"], 8 * (h + 1))
                u = PS[:, 6 + h, 0:8 * (QW + 1)].rearrange("p (g c) -> p g c", c=QW + 1)
                bs = slice(2 * h, 2 * h + 2)
                v.reciprocal(rx[:, bs].rearrange("p b j -> p (b j)"), u[:, :, QW]).then_inc(s["v_step"], 1)
                v.wait_ge(s["v_step"], step())
                v.tensor_tensor(rmx[:, bs], rx[:, bs].unsqueeze(3).broadcast_to([P, 2, NJ, HL]),
                                mask_p.unsqueeze(1).unsqueeze(1).broadcast_to([P, 2, NJ, HL]), ALU.mult).then_inc(s["v_step"], 1)
                v.wait_ge(s["v_step"], step())
                v.tensor_tensor(umx[:, bs].rearrange("p b (j h d) -> p (b j) h d", j=NJ, h=HL),
                                u[:, :, 0:QW].rearrange("p g (h d) -> p g h d", h=HL),
                                rmx[:, bs].rearrange("p b j h -> p (b j) h").unsqueeze(3).broadcast_to([P, 8, HL, DH]),
                                ALU.mult).then_inc(s["umx"], 1)

            for n in range(B * NJ + 2):
                if n < B * NJ:
                    peak(n)
                if n >= 3 and n % 2:
                    turned(n - 2)
                if n == 12:
                    keep_blocks(0)
            keep_blocks(1)
            v.tensor_tensor(tz[:], xs[3][:], row[:, R_BO:R_BO + D], ALU.add).then_inc(s["x3b"], 1)
            v.wait_ge(s["ax_mm"], 1)
            v.tensor_scalar(aTx[:], PS[:, 5, 0:P], cv(C_BV1), None, ALU.add).then_inc(s["aTx"], 1)
            v.wait_ge(s["ox_mm"], 1)
            v.wait_ge(s["x3b"], 1)
            v.tensor_tensor(xs[4][:], PS[:, 5, 0:P], tz[:], ALU.add).then_inc(s["x"], 1)

            v.wait_ge(s["x"], 3)
            layernorm(6, 4)
            v.wait_ge(s["yN_turned"], 5)
            v.tensor_copy(yT[:], PS[:, 7, 0:P]).then_inc(s["yT"], 1)
            v.wait_ge(s["q3_mm"], 1)
            spread(qb3[:], PS[:, 6, 0:P]).then_inc(s["qb3"], 1)
            v.wait_ge(s["s3_mm"], 1)
            sc = quad[:, :, 0:P].rearrange("p j (b s) -> p j b s", b=B)
            v.tensor_reduce(mx3[:], sc, AX, ALU.max).then_inc(s["v_step"], 1)
            v.wait_ge(s["v_step"], step())
            for j in range(NJ):
                last = v.tensor_tensor(ex3[:, j, :].rearrange("p (b s) -> p b s", b=B), sc[:, j],
                                       mx3[:, j, :].unsqueeze(2).broadcast_to([P, B, L]), ALU.subtract)
            last.then_inc(s["ex3_sub"], 1)
            v.wait_ge(s["ex3"], 1)
            v.tensor_reduce(sm3[:], ex3[:].rearrange("p j (b s) -> p j b s", b=B), AX, ALU.add).then_inc(s["v_step"], 1)
            v.wait_ge(s["v_step"], step())
            v.reciprocal(rc3[:], sm3[:]).then_inc(s["v_step"], 1)
            v.wait_ge(s["v_step"], step())
            v.tensor_tensor(rm3[:], rc3[:].rearrange("p j b -> p b j").unsqueeze(3).broadcast_to([P, B, NJ, HL]),
                            mask_p.unsqueeze(1).unsqueeze(1).broadcast_to([P, B, NJ, HL]), ALU.mult).then_inc(s["rm3"], 1)
            v.wait_ge(s["u3_mm"], 1)
            v.wait_ge(s["rm3"], 1)
            v.tensor_tensor(um3[:].rearrange("p b (g d) -> p b g d", d=DH),
                            quad[:, :, 0:P].rearrange("p b (g d) -> p b g d", d=DH),
                            rm3[:].rearrange("p b j h -> p b (j h)").unsqueeze(3).broadcast_to([P, B, H, DH]),
                            ALU.mult).then_inc(s["um3"], 1)
            v.wait_ge(s["a3_mm"], 1)
            v.tensor_copy(aT3[:], PS[:, 6, 0:P]).then_inc(s["aT3"], 1)
            v.tensor_tensor(tz[:], xs[4][:], row[:, R_BPROJ:R_BPROJ + D], ALU.add).then_inc(s["v_step"], 1)
            v.wait_ge(s["v_step"], step())
            v.wait_ge(s["o3_mm"], 1)
            v.tensor_tensor(xs[5][:], PS[:, 7, 0:P], tz[:], ALU.add).then_inc(s["x"], 1)

            v.wait_ge(s["x"], 4)
            layernorm(7, 5)
            v.wait_ge(s["yN_turned"], 6)
            v.tensor_copy(yT[:], PS[:, 7, 0:P]).then_inc(s["yT"], 1)
            route(1, None)
            v.wait_ge(s["idf"], 2)
            v.tensor_scalar(oh[:, 3], iota, idf[:, 1, 0:1], None, ALU.is_equal).then_inc(s["oh3"], 1)
            for n in range(E1N + 2):
                if n <= E1N:
                    v.wait_ge(s["sa1"], n + 1)
                    if n >= 3:
                        v.wait_ge(s["y1_mm"], n - 2)
                    v.tensor_tensor(hT1[:, n % 3], PS[:, n % 4, 256:512].rearrange("p (f t) -> p f t", f=FC1),
                                    sa1[:, n % 3], ALU.mult).then_inc(s["hT1"], 1)
                if n >= 1:
                    k = n - 1
                    v.wait_ge(s["y1_mm"], k + 1)
                    src = PS[:, 4 + k % 2, 0:D]
                    if k == 0:
                        v.tensor_tensor(acc1[:, 0], src, xs[5][:], ALU.add).then_inc(s["acc1"], 1)
                    else:
                        v.wait_ge(s["acc1"], k)
                        v.wait_ge(s["oh3"], 1)
                        last = v.scalar_tensor_tensor(acc1[:, k % 2] if k < E1N else xs[6][:], src, oh[:, 3, k - 1:k],
                                                      acc1[:, (k - 1) % 2], ALU.mult, ALU.add)
                        last.then_inc(s["acc1"] if k < E1N else s["x"], 1)

        @block.scalar
        def _(a):
            def bg_out(u):
                a.wait_ge(s["bg_mm"], u + 1)
                src = PS[:, 1 + u % 3, :]
                if u < B:
                    a.activation(kx[:, u], src, ACT.Identity, bias=cv(C_BK1)).then_inc(s["bg_out"], 1)
                else:
                    for c in range(KC):
                        last = a.activation(vx[:, u - B, c, :, 0:QW], src[:, c * D:(c + 1) * D].rearrange("p (j w) -> p j w", j=NJ),
                                            ACT.Copy)
                    last.then_inc(s["bg_out"], 1)

            a.wait_ge(s["col_in"], 16)
            a.wait_ge(s["kc_mm"], 1)
            a.activation(kcT[:], PS[:, 6, 0:P], ACT.Identity, bias=cv(C_BKC)).then_inc(s["kcT"], 1)
            a.wait_ge(s["vc_mm"], 1)
            a.activation(vc[:], PS[:, 5, 0:P], ACT.Copy).then_inc(s["vc"], 1)
            a.wait_ge(s["qs_mm"], 1)
            a.activation(qsT[:].rearrange("p r t -> p (r t)"), PS[:, 4, 0:2 * P], ACT.Identity, bias=cv(C_BQS)).then_inc(s["qsT"], 1)
            a.wait_ge(s["m0b"], 1)
            a.activation(e0[:], PS[:, 0, :], ACT.Exp, bias=m0[:, 1:2], accum_out=m0[:, 2:3]).then_inc(s["e0"], 1)
            a.wait_ge(s["s2"], 1)
            a.activation(e2[:], s2[:], ACT.Exp, scale=SC0).then_inc(s["e2"], 1)
            bg_out(0)
            bg_out(1)
            a.wait_ge(s["p0_turned"], 1)
            a.activation(p0T[:, 2:4, :], PS[:, 6, 0:2 * P].rearrange("p (c k) -> p c k", c=2), ACT.Copy).then_inc(s["p0T_b"], 1)
            bg_out(2)
            bg_out(3)
            a.wait_ge(s["g_mm"], 1)
            a.wait_ge(s["hbg"], 1)
            a.activation(th[:], PS[:, 6, 0:P], ACT.Tanh, bias=hbg[:, 0:1], scale=0.5).then_inc(s["th"], 1)
            for u in range(4, 8):
                bg_out(u)

            a.wait_ge(s["k12_mm"], 1)
            a.activation(kT[:].rearrange("p n k -> p (n k)"), PS[:, 5, 0:2 * P], ACT.Copy).then_inc(s["kT"], 1)
            a.wait_ge(s["v1_mm"], 1)
            a.activation(vN[:], PS[:, 4, 0:P], ACT.Copy).then_inc(s["vN"], 1)
            for n in range(2):
                a.wait_ge(s["ex1_sub"], n + 1)
                a.activation(ex[:, n].rearrange("p j k -> p (j k)"), ex[:, n].rearrange("p j k -> p (j k)"),
                             ACT.Exp, scale=SCH).then_inc(s["ex1"], 1)
            a.wait_ge(s["e1_turned"], 1)
            a.activation(eT[:, 0], PS[:, 0, :].rearrange("p (j k) -> p j k", j=NJ), ACT.Copy).then_inc(s["eT_0"], 1)

            a.wait_ge(s["tw_d"], 1)
            a.activation(tw[:, 1:2], tw[:, 0:1], ACT.Exp).then_inc(s["tw_e"], 1)
            for e in range(E0N):
                for f in range(FC0):
                    n = e * FC0 + f
                    a.wait_ge(s["ab_mm"], e + 1)
                    if n >= 4:
                        a.wait_ge(s["hT"], n - 3)
                    a.activation(sa[:, n % 4], PS[:, e % 2, f * P:(f + 1) * P], ACT.Silu, bias=cv(C_B1A + n)).then_inc(s["sa"], 1)

            def ex_tile(n):
                a.wait_ge(s["nmx"], n + 1)
                if n >= 3:
                    a.wait_ge(s["xe_turned"], n - 2)
                a.activation(xe[:, n % 3], PS[:, n % NJ, :], ACT.Exp, bias=nmx[:, n:n + 1]).then_inc(s["xe"], 1)

            def turned(n):
                a.wait_ge(s["xe_turned"], n + 1)
                if n >= 3:
                    a.wait_ge(s["ux_mm"], n - 2)
                a.activation(xeT[:, n % 3], PS[:, 4, :].rearrange("p (c k) -> p c k", c=KC),
                             ACT.Copy).then_inc(s["xeT_even"], 1)

            for n in range(B * NJ + 1):
                if n < B * NJ:
                    ex_tile(n)
                if n % 2:
                    turned(n - 1)

            a.wait_ge(s["k3_mm"], 1)
            a.activation(kT3[:], PS[:, 5, 0:P], ACT.Copy).then_inc(s["kT3"], 1)
            a.wait_ge(s["v3_mm"], 1)
            a.activation(vN3[:], PS[:, 4, 0:P], ACT.Copy).then_inc(s["vN3"], 1)
            a.wait_ge(s["ex3_sub"], 1)
            a.activation(ex3[:].rearrange("p j k -> p (j k)"), ex3[:].rearrange("p j k -> p (j k)"),
                         ACT.Exp, scale=SCH).then_inc(s["ex3"], 1)
            a.wait_ge(s["e3_turned"], 1)
            a.activation(eT3[:], PS[:, 4, :].rearrange("p (j k) -> p j k", j=NJ), ACT.Copy).then_inc(s["eT3"], 1)

            for n in range(E1N + 1):
                a.wait_ge(s["gu_mm"], n + 1)
                if n >= 3:
                    a.wait_ge(s["hT1"], n - 2)
                a.activation(sa1[:, n % 3], PS[:, n % 4, 0:256].rearrange("p (f t) -> p f t", f=FC1), ACT.Silu).then_inc(s["sa1"], 1)

        @block.tensor
        def _(t):
            def mm(o, lhsT, rhs, start=True, stop=True):
                return t.matmul(o, lhsT, rhs, start=start, stop=stop, skip_group_check=True)

            def turn_y(n):
                t.wait_ge(s["yN"], n)
                t.transpose(PS[:, 7, 0:P], yN[:], ident).then_inc(s["yN_turned"], 1)

            def bg(u):
                if u == 0:
                    t.wait_ge(s["w2_in"], 16)
                if u >= 3:
                    t.wait_ge(s["bg_out"], u - 2)
                if u < B:
                    last = mm(PS[:, 1 + u % 3, :], w2[:, 1], ctxT[:, u * NCTX:(u + 1) * NCTX])
                else:
                    for c in range(KC):
                        last = mm(PS[:, 1 + u % 3, c * D:(c + 1) * D],
                                  ctxT[:, (u - B) * NCTX + c * P:(u - B) * NCTX + (c + 1) * P], w2[:, 2])
                last.then_inc(s["bg_mm"], 1)

            t.wait_ge(s["con_in"], 16)
            turn_y(1)
            t.wait_ge(s["w0_in"], 16)
            t.wait_ge(s["yT"], 1)
            mm(PS[:, 7, 0:P], w0[:, 0], yT[:]).then_inc(s["qc_mm"], 1)
            mm(PS[:, 6, 0:P], w0[:, 4], yT[:]).then_inc(s["kc_mm"], 1)
            mm(PS[:, 5, 0:P], yT[:], w0[:, 5]).then_inc(s["vc_mm"], 1)
            t.wait_ge(s["qcT"], 1)
            mm(PS[:, 7, 0:P], w0[:, 1], qcT[:])
            mm(PS[:, 7, P:P + 1], qcT[:], cv(C_BKS)).then_inc(s["qp_mm"], 1)
            t.wait_ge(s["ctxT_in"], 16)
            near = ctxT[:].rearrange("c (b i r) -> c r b i", b=B, r=R)
            for r in range(2):
                last = mm(PS[:, 4, r * P:(r + 1) * P], w0[:, 3], near[:, LO + r])
            last.then_inc(s["qs_mm"], 1)
            t.wait_ge(s["qpT"], 1)
            for b in range(B):
                last = mm(PS[b * L:(b + 1) * L, 0, :], qpT[:, b * L:(b + 1) * L], ctxT[:, b * NCTX:(b + 1) * NCTX])
            last.then_inc(s["s0_mm"], 1)
            t.wait_ge(s["qsT"], 1)
            t.wait_ge(s["kcT"], 1)
            t.wait_ge(s["vc"], 1)
            for r in range(2):
                for b in range(B):
                    last = mm(PS[b * L:(b + 1) * L, 5, 256 + r * L:256 + (r + 1) * L],
                              qsT[:, r, b * L:(b + 1) * L], kcT[:, b * L:(b + 1) * L])
            last.then_inc(s["s2_mm"], 1)
            bg(0)
            bg(1)
            t.wait_ge(s["e0n"], 1)
            for c in range(KC):
                last = t.transpose(PS[:, 4 + 2 * (c // 2), (c % 2) * P:(c % 2 + 1) * P], e0n[:, c * P:(c + 1) * P], ident)
            last.then_inc(s["p0_turned"], 1)
            bg(2)
            t.wait_ge(s["p0T_a"], 1)
            t.wait_ge(s["p0T_b"], 1)
            t.wait_ge(s["ctxN_in"], 16)
            for b in range(B):
                for c in range(KC):
                    last = mm(PS[:, 0, b * L:(b + 1) * L], ctxN[:, b * KC + c],
                              p0T[:, c, b * L:(b + 1) * L], start=(c == 0), stop=(c == KC - 1))
            last.then_inc(s["pc_mm"], 1)
            t.wait_ge(s["paBD"], 1)
            t.wait_ge(s["vc"], 1)
            mm(PS[:, 5, 384:384 + P], vc[:], paBD[:]).then_inc(s["s2c_mm"], 1)
            t.wait_ge(s["pcT"], 1)
            t.wait_ge(s["qbk"], 1)
            mm(PS[:, 7, 0:P], w0[:, 2], pcT[:]).then_inc(s["c2s_mm"], 1)
            bg(3)
            t.wait_ge(s["s2cT"], 1)
            t.wait_ge(s["c2sT"], 1)
            mm(PS[:, 6, 0:P], w0[:, 7], s2cT[:], stop=False)
            mm(PS[:, 6, 0:P], w0[:, 6], c2sT[:], start=False).then_inc(s["g_mm"], 1)
            bg(4)
            t.wait_ge(s["oT0"], 1)
            t.transpose(PS[:, 4, 0:P], oT0[:], ident).then_inc(s["o0_turned"], 1)
            bg(5)

            turn_y(2)
            bg(6)
            t.wait_ge(s["yT"], 2)
            t.wait_ge(s["w1_in"], 16)
            mm(PS[:, 6, 0:P], w1[:, 0], yT[:]).then_inc(s["q12_mm"], 1)
            mm(PS[:, 5, 0:P], w1[:, 1], yT[:])
            mm(PS[:, 5, P:2 * P], w1[:, 3], yT[:]).then_inc(s["k12_mm"], 1)
            mm(PS[:, 7, 0:P], w1[:, 2], yT[:]).then_inc(s["q12_mm"], 1)
            mm(PS[:, 4, 0:P], yT[:], w1[:, 4]).then_inc(s["v1_mm"], 1)
            bg(7)
            t.wait_ge(s["bg_out"], 8)
            for n in range(2):
                t.wait_ge(s["qb"], n + 1)
                t.wait_ge(s["kT"], 1)
                t.wait_ge(s["vN"], 1)
                for j in range(NJ):
                    q = slice(j * QW, (j + 1) * QW)
                    for b in range(B):
                        last = mm(PS[:, 4 * n + j, b * L:(b + 1) * L],
                                  qb[q, n, b].rearrange("p h t -> p (h t)"), kT[q, n, b * L:(b + 1) * L])
                last.then_inc(s["s1_mm"], 1)
            for n in range(2):
                t.wait_ge(s["ex1"], n + 1)
                for j in range(NJ):
                    last = t.transpose(PS[:, 4 * n, j * P:(j + 1) * P], ex[:, n, j], ident)
                last.then_inc(s["e1_turned"], 1)
            for n in range(2):
                t.wait_ge(s[f"eT_{n}"], 1)
                for b in range(B):
                    q = slice(b * L, (b + 1) * L)
                    for j in range(NJ):
                        last = mm(PS[:, 4 * n + b, j * QW:(j + 1) * QW],
                                  eT[q, n, j], vN[q, j * QW:(j + 1) * QW])
                last.then_inc(s["u1_mm"], 1)
            t.wait_ge(s["um1"], 2)
            for b in range(B):
                for n in range(2):
                    last = mm(PS[b * L:(b + 1) * L, 0, 0:D], sel, um[:, n, b], start=(n == 0), stop=(n == 1))
            last.then_inc(s["a1_mm"], 1)

            turn_y(3)
            t.wait_ge(s["yT"], 3)
            t.wait_ge(s["wr_in"], 16)
            mm(PS[:, 6, 0:E0N], yT[:], wr[:, 0]).then_inc(s["lg_mm"], 1)

            def up0(e):
                if e % 2 == 0:
                    t.wait_ge(s[f"wab{e}_in"], 16)
                if e >= 2:
                    t.wait_ge(s["hT"], FC0 * (e - 1))
                for f in range(FC0):
                    mm(PS[:, e % 2, f * P:(f + 1) * P], wab[:, e, 0, f * P:(f + 1) * P], yT[:])
                    last = mm(PS[:, 2 + e % 2, f * P:(f + 1) * P], wab[:, e, 1, f * P:(f + 1) * P], yT[:])
                last.then_inc(s["ab_mm"], 1)

            def down0(e):
                if e % 2 == 0:
                    t.wait_ge(s[f"wdn{e}_in"], 16)
                if e >= 2:
                    t.wait_ge(s["acc"], e)
                for f in range(FC0):
                    t.wait_ge(s["hT"], FC0 * e + f + 1)
                    last = mm(PS[:, 4 + e % 2, 0:D], hT[:, e % 2, f], wdn[:, e, f], start=(f == 0), stop=(f == FC0 - 1))
                last.then_inc(s["y_mm"], 1)

            up0(0)
            t.wait_ge(s["we"], 1)
            t.transpose(PS[0:E0N, 6, 0:P], oh[:, 2], ident).then_inc(s["we_turned"], 1)
            for e in range(E0N):
                if e + 1 < E0N:
                    up0(e + 1)
                if e == 0:
                    t.wait_ge(s["weT"], 1)
                    t.wait_ge(s["b2_in"], 16)
                    mm(PS[:, 6, 0:P], weT[:], b2[:]).then_inc(s["b2_mm"], 1)
                down0(e)

            turn_y(4)
            t.wait_ge(s["yT"], 4)
            mm(PS[:, 7, 0:P], w2[:, 0], yT[:]).then_inc(s["qx_mm"], 1)
            t.wait_ge(s["qbx"], 1)
            t.wait_ge(s["vx_ones"], 1)
            t.wait_ge(s["acc"], E0N + 1)

            def score(n):
                b, j = divmod(n, NJ)
                q = slice(j * QW, (j + 1) * QW)
                if n >= NJ:
                    t.wait_ge(s["xe"], n - NJ + 1)
                mm(PS[:, j, :], qbx[q, b].rearrange("p h t -> p (h t)"), kx[q, b]).then_inc(s["sx_mm"], 1)

            def copied(n):
                t.wait_ge(s["xeT_odd"] if n % 2 else s["xeT_even"], n // 2 + 1)

            def turn(n):
                t.wait_ge(s["xe"], n + 1)
                if n >= 2:
                    copied(n - 2)
                for c in range(KC):
                    last = t.transpose(PS[:, 4 + n % 2, c * P:(c + 1) * P], xe[:, n % 3, c * P:(c + 1) * P], ident)
                last.then_inc(s["xe_turned"], 1)

            def values(n):
                b, j = divmod(n, NJ)
                copied(n)
                o = (n % 8) * (QW + 1)
                for c in range(KC):
                    last = mm(PS[:, 6 + n // 8, o:o + QW + 1], xeT[:, n % 3, c], vx[:, b, c, j], start=(c == 0), stop=(c == KC - 1))
                last.then_inc(s["ux_mm"], 1)

            score(0)
            score(1)
            for n in range(B * NJ + 2):
                if n + 2 < B * NJ:
                    score(n + 2)
                if 0 <= n - 1 < B * NJ:
                    turn(n - 1)
                if n >= 2:
                    values(n - 2)
            t.wait_ge(s["umx"], 2)
            for b in range(B):
                last = mm(PS[:, 5, b * L:(b + 1) * L], umx[:, b], sel)
            last.then_inc(s["ax_mm"], 1)
            t.wait_ge(s["aTx"], 1)
            mm(PS[:, 5, 0:P], aTx[:], w2[:, 3]).then_inc(s["ox_mm"], 1)

            for j in range(NJ):
                mm(PS[:, j, 0:P].rearrange("p (b s) -> p b s", b=B), ident,
                   alibi[:, j].unsqueeze(1).broadcast_to([P, B, L]), stop=False)
            turn_y(5)
            t.wait_ge(s["yT"], 5)
            mm(PS[:, 6, 0:P], w2[:, 4], yT[:]).then_inc(s["q3_mm"], 1)
            mm(PS[:, 5, 0:P], w2[:, 5], yT[:]).then_inc(s["k3_mm"], 1)
            mm(PS[:, 4, 0:P], yT[:], w2[:, 6]).then_inc(s["v3_mm"], 1)
            t.wait_ge(s["qb3"], 1)
            t.wait_ge(s["kT3"], 1)
            for j in range(NJ):
                q = slice(j * QW, (j + 1) * QW)
                for b in range(B):
                    last = mm(PS[:, j, b * L:(b + 1) * L], qb3[q, b].rearrange("p h t -> p (h t)"),
                              kT3[q, b * L:(b + 1) * L], start=False)
            last.then_inc(s["s3_mm"], 1)
            t.wait_ge(s["ex3"], 1)
            t.wait_ge(s["vN3"], 1)
            for j in range(NJ):
                last = t.transpose(PS[:, 4, j * P:(j + 1) * P], ex3[:, j], ident)
            last.then_inc(s["e3_turned"], 1)
            t.wait_ge(s["eT3"], 1)
            for b in range(B):
                q = slice(b * L, (b + 1) * L)
                for j in range(NJ):
                    last = mm(PS[:, b, j * QW:(j + 1) * QW], eT3[q, j], vN3[q, j * QW:(j + 1) * QW])
            last.then_inc(s["u3_mm"], 1)
            t.wait_ge(s["um3"], 1)
            for b in range(B):
                last = mm(PS[:, 6, b * L:(b + 1) * L], um3[:, b], sel)
            last.then_inc(s["a3_mm"], 1)
            t.wait_ge(s["aT3"], 1)
            mm(PS[:, 7, 0:P], aT3[:], w2[:, 7]).then_inc(s["o3_mm"], 1)

            turn_y(6)
            t.wait_ge(s["yT"], 6)
            mm(PS[:, 6, 0:E0N], yT[:], wr[:, 1]).then_inc(s["lg_mm"], 1)
            t.wait_ge(s["wgu_in"], 16)
            t.wait_ge(s["wdo_in"], 16)

            def up1(n):
                if n >= 4:
                    t.wait_ge(s["hT1"], n - 3)
                for k in range(2):
                    for f in range(FC1):
                        last = mm(PS[:, n % 4, (k * FC1 + f) * P:(k * FC1 + f + 1) * P], wgu[:, n, k, f * P:(f + 1) * P], yT[:])
                last.then_inc(s["gu_mm"], 1)

            def down1(n):
                if n >= 2:
                    t.wait_ge(s["acc1"], n - 1)
                t.wait_ge(s["hT1"], n + 1)
                for f in range(FC1):
                    last = mm(PS[:, 4 + n % 2, 0:D], hT1[:, n % 3, f], wdo[:, n, f], start=(f == 0), stop=(f == FC1 - 1))
                last.then_inc(s["y1_mm"], 1)

            up1(0)
            up1(1)
            for n in range(E1N + 1):
                if n + 2 <= E1N:
                    up1(n + 2)
                down1(n)


def kernel(**inputs):
    import concourse.bacc as bacc
    from concourse.bass_utils import run_bass_kernel_spmd

    I = {k: np.asarray(a) for k, a in inputs.items()}
    ctx = I["ctx_1024"].reshape(B * NCTX, D)

    def stack(*ws):
        return np.stack(ws, 1)

    def heads(w):
        return w.transpose(1, 0, 2).reshape(D, D)

    def chunks(w):
        return w.reshape(w.shape[0], -1, P, w.shape[2]).transpose(2, 0, 1, 3)

    x0, x1 = "L0_xattn_", "L1_xattn_"
    cols = [I[x0 + n] for n in ("bq_c", "bk_s", "bv_s", "bq_s", "bk_c", "bv_c", "bg")]
    cols += [I["L0_ffn_ln_w"], I[x1 + "bq"], I[x1 + "bk"], I[x1 + "bv"]]
    cols += list(I["L0_ffn_b1a"].reshape(-1, P)) + list(I["L0_ffn_b1b"].reshape(-1, P))
    up = np.concatenate([I["L1_ffn_w_up_s"][None], I["L1_ffn_up"]])
    gate = np.concatenate([I["L1_ffn_w_gate_s"][None], I["L1_ffn_gate"]])
    down = np.concatenate([I["L1_ffn_w_down_s"][None], I["L1_ffn_down"]])
    arrays = {
        "x": I["x"].reshape(P, D),
        "con": shape_constants(),
        "col": np.stack(cols, 1),
        "row": np.concatenate([I["L0_attn_ln_gamma"], I["L0_attn_ln_beta"], I[x1 + "bo"], I["L1_attn_b_proj"],
                               I["L0_ffn_bg"], I["L0_attn_lamb"].reshape(1)]),
        "w0": stack(I[x0 + "Wq_c"].T, I[x0 + "Wk_s"], I[x0 + "Wv_s"].T, I[x0 + "Wq_s"].T, I[x0 + "Wk_c"].T,
                    I[x0 + "Wv_c"].T, I[x0 + "Wg"][:, :D].T, I[x0 + "Wg"][:, D:].T),
        "w1": stack(*[heads(I["L0_attn_" + n]) for n in ("wq1", "wk1", "wq2", "wk2", "wv")]),
        "w2": stack(I[x1 + "Wq"].T, I[x1 + "Wk"].T, I[x1 + "Wv"].T, I[x1 + "Wo"].T, I["L1_attn_W_query"],
                    I["L1_attn_W_key"], I["L1_attn_W_value"], I["L1_attn_W_proj"]),
        "wr": stack(I["L0_ffn_Wg"], I["L1_ffn_router"].T),
        "b2": I["L0_ffn_b2"],
        "ctxT": ctx.T,
        "ctxN": ctx.reshape(B * KC, P, D).transpose(1, 0, 2),
        "wab": np.stack([I["L0_ffn_W1a"], I["L0_ffn_W1b"]]).transpose(2, 1, 0, 3),
        "wdn": chunks(I["L0_ffn_W2"]),
        "wgu": np.stack([gate, up]).transpose(3, 1, 0, 2),
        "wdo": chunks(down.transpose(0, 2, 1)),
    }
    nc = bacc.Bacc("TRN2", target_bir_lowering=False, num_devices=1)
    A = {}
    for name, a in arrays.items():
        arrays[name] = a = np.ascontiguousarray(a)
        A[name] = nc.dram_tensor(f"in_{name}", a.shape, mybir.dt.from_np(a.dtype), kind="ExternalInput").ap()
    out = nc.dram_tensor("out_x", (P, D), F32, kind="ExternalOutput").ap()
    build(nc, A, out)
    r = run_bass_kernel_spmd(nc, [{f"in_{k}": a for k, a in arrays.items()}], core_ids=[0])
    return r.results[0]["out_x"].reshape(B, L, D)
```

```python
from contextlib import ExitStack

import numpy as np
import concourse.bass as bass
from concourse import mybir

F32 = mybir.dt.float32
U32 = mybir.dt.uint32
ALU = mybir.AluOpType
ACT = mybir.ActivationFunctionType
AX = mybir.AxisListType.X

P = 128
B, L, D = 4, 32, 128
NCTX = 512
KC = NCTX // P
H, DH = 16, 8
NJ, HL = 4, 4
QW = D // NJ
E0N, F0 = 8, 512
FC0 = F0 // P
E1N, F1 = 8, 256
FC1 = F1 // P
R = NCTX // L
LO = R // 2 - 1
EPS = 1e-5
RMS_EPS = float(np.finfo(np.float32).eps)
SC0 = float(D) ** -0.5
SCH = float(DH) ** -0.5

(C_BQC, C_BKS, C_BVS, C_BQS, C_BKC, C_BVC, C_BG, C_LNW, C_BQ1, C_BK1, C_BV1) = range(11)
C_B1A = 11
C_B1B = C_B1A + E0N * FC0
N_COLS = C_B1B + E0N * FC0
R_GAMMA, R_BETA, R_BO, R_BPROJ, R_BG, R_LAMB = 0, D, 2 * D, 3 * D, 4 * D, 4 * D + E0N
N_ROWS = R_LAMB + 1
K_ID = 0
K_MF = K_ID + P
K_MQ = K_MF + HL
K_SEL = K_MQ + NJ
K_IOTA = K_SEL + L
K_ALIBI = K_IOTA + E0N
N_CONST = K_ALIBI + NJ * L
MASKED = -1e30


def shape_constants():
    k = np.zeros((P, N_CONST), np.float32)
    p = np.arange(P)
    k[:, K_ID:K_ID + P] = np.eye(P)
    k[:, K_MF:K_MF + HL] = (p[:, None] // DH) % HL == np.arange(HL)
    k[:, K_MQ:K_MQ + NJ] = p[:, None] // QW == np.arange(NJ)
    k[:, K_SEL:K_SEL + L] = p[:, None] % L == np.arange(L)
    k[:, K_IOTA:K_IOTA + E0N] = np.arange(E0N)
    slopes = np.float32(2.0) ** (np.float32(-8.0) * np.arange(1, H + 1, dtype=np.float32) / np.float32(H))
    for j in range(NJ):
        for hl in range(HL):
            t = np.arange(L, dtype=np.float32)
            bias = slopes[j * HL + hl] * (t[None, :] - t[:, None])
            bias[t[None, :] > t[:, None]] = MASKED
            k[hl * L:(hl + 1) * L, K_ALIBI + j * L:K_ALIBI + (j + 1) * L] = bias
    return k


def build(nc, A, out):
    with ExitStack() as ctx:
        def sb(name, shape, dt=F32):
            return ctx.enter_context(nc.sbuf_tensor(name, shape, dt))

        class Sems(dict):
            def __missing__(self, name):
                self[name] = ctx.enter_context(nc.semaphore(name))
                return self[name]

        s = Sems()

        x0 = sb("x0", [P, D])
        con = sb("con", [P, N_CONST])
        col = sb("col", [P, N_COLS])
        row = sb("row", [P, N_ROWS])
        w0 = sb("w0", [P, 8, D])
        w1 = sb("w1", [P, 5, D])
        w2 = sb("w2", [P, 8, D])
        wr = sb("wr", [P, 2, E0N])
        b2 = sb("b2", [E0N, D])
        ctxT = sb("ctxT", [P, B * NCTX])
        ctxN = sb("ctxN", [P, B * KC, D])
        wab = sb("wab", [P, E0N, 2, F0])
        wdn = sb("wdn", [P, E0N, FC0, D])
        wgu = sb("wgu", [P, E1N + 1, 2, F1])
        wdo = sb("wdo", [P, E1N + 1, FC1, D])

        ident = con[:, K_ID:K_ID + P]
        mask_f = con[:, K_MF:K_MF + HL]
        mask_q = con[:, K_MQ:K_MQ + NJ]
        sel = con[:, K_SEL:K_SEL + L]
        iota = con[:, K_IOTA:K_IOTA + E0N]
        alibi = con[:, K_ALIBI:K_ALIBI + NJ * L]

        def cv(i):
            return col[:, i:i + 1]

        xeT = [t[:, k * NCTX:(k + 1) * NCTX] for t in (ctxN[:].rearrange("p c k -> p (c k)"), ctxT[:]) for k in range(NJ)]

        half = sb("half", [P, 1])
        warm = sb("warm", [P, 1])
        st6 = sb("st6", [P, 6, 6])
        mv = sb("mv", [P, 6, 2])
        ve = sb("ve", [P, 8])
        rs = sb("rs", [P, 8])
        yN = sb("yN", [P, D])
        yT = sb("yT", [P, D])
        xs = [x0] + [sb(f"x{i}", [P, D]) for i in range(1, 7)]
        qcT = sb("qcT", [P, P])
        kcT = sb("kcT", [P, P])
        vc = sb("vc", [P, D])
        qpT = sb("qpT", [P, P])
        qbk = sb("qbk", [P, 1])
        qsT = sb("qsT", [P, 2, P])
        m0 = sb("m0", [P, 4])
        e0 = sb("e0", [P, NCTX])
        p0T = sb("p0T", [P, KC, P])
        pcN = sb("pcN", [P, P])
        pcT = sb("pcT", [P, P])
        c2sT = sb("c2sT", [P, P])
        s2 = sb("s2", [P, 2, L])
        e2 = sb("e2", [P, 2, L])
        p2 = sb("p2", [P, 2, L])
        m2 = sb("m2", [P, 8])
        pa = sb("pa", [P, L])
        paT = sb("paT", [P, L])
        paBD = sb("paBD", [P, P])
        s2cT = sb("s2cT", [P, P])
        hbg = sb("hbg", [P, 1])
        th = sb("th", [P, P])
        dif = sb("dif", [P, P])
        base = sb("base", [P, P])
        td = sb("td", [P, P])
        oT0 = sb("oT0", [P, P])
        qb = sb("qb", [P, 2, B, HL, L])
        kb = sb("kb", [P, 2, B, NJ, L])
        vb = sb("vb", [P, B, NJ, QW])
        mx = sb("mx", [P, 2, B * NJ])
        ex = sb("ex", [P, 2, B, P])
        eT = sb("eT", [P, 2, B, P])
        sm = sb("sm", [P, 2, B * NJ])
        rc = sb("rc", [P, 2, B * NJ])
        mask2 = sb("mask2", [P, HL])
        rm = sb("rm", [P, 2, B, NJ, HL])
        um = sb("um", [P, 2, B, D])
        gl = sb("gl", [P, D])
        xb = sb("xb", [P, D])
        oml = sb("oml", [P, 1])
        tz = sb("tz", [P, D])
        qb3, kb3, vb3, ex3, eT3, rm3, um3 = qb[:, 0], kb[:, 0], vb, ex[:, 0], eT[:, 0], rm[:, 0], um[:, 0]
        mx3, sm3, rc3 = mx[:, 0], sm[:, 0], rc[:, 0]
        aT3 = sb("aT3", [P, P])
        kx = sb("kx", [P, B, NCTX])
        vx = sb("vx", [P, B, KC, D])
        qxT = sb("qxT", [P, P])
        qbx = sb("qbx", [P, B, HL, L])
        nmx = sb("nmx", [P, B * NJ])
        xe = sb("xe", [P, 3, NCTX])
        smx = sb("smx", [P, B * NJ])
        rx = sb("rx", [P, B, NJ])
        uxT = sb("uxT", [P, 2, P])
        rmx = sb("rmx", [P, B, NJ, HL])
        umx = sb("umx", [P, B, D])
        aTx = sb("aTx", [P, P])
        lg = sb("lg", [P, 2, E0N])
        top = sb("top", [P, 2, 8])
        idx = sb("idx", [P, 2, 8], U32)
        idf = sb("idf", [P, 2, 8])
        tw = sb("tw", [P, 6])
        oh = sb("oh", [P, 4, E0N])
        weT = sb("weT", [E0N, P])
        sa = sb("sa", [P, 4, P])
        hT = sb("hT", [P, 2, FC0, P])
        acc = sb("acc", [P, 2, D])
        sa1 = sb("sa1", [P, 3, FC1, P])
        hT1 = sb("hT1", [P, 3, FC1, P])
        acc1 = sb("acc1", [P, 2, D])

        PS = ctx.enter_context(nc.psum_tensor("PS", [P, 8, 512], F32))

        block = ctx.enter_context(nc.Block())

        @block.sync
        def _(sp):
            sp.dma_start(x0[:], A["x"]).then_inc(s["x_in"], 16)
            sp.dma_start(con[:], A["con"]).then_inc(s["con_in"], 16)
            sp.dma_start(w0[:], A["w0"]).then_inc(s["w0_in"], 16)
            sp.dma_start(col[:], A["col"]).then_inc(s["col_in"], 16)
            sp.dma_start(ctxT[:], A["ctxT"]).then_inc(s["ctxT_in"], 16)
            sp.dma_start(w2[:], A["w2"]).then_inc(s["w2_in"], 16)
            sp.dma_start(ctxN[:], A["ctxN"]).then_inc(s["ctxN_in"], 16)
            sp.dma_start(w1[:], A["w1"]).then_inc(s["w1_in"], 16)
            sp.dma_start(row[:], A["row"].partition_broadcast(P)).then_inc(s["row_in"], 16)
            sp.dma_start(wr[:], A["wr"]).then_inc(s["wr_in"], 16)
            sp.dma_start(b2[:], A["b2"]).then_inc(s["b2_in"], 16)
            for e in range(0, E0N, 2):
                sp.dma_start(wab[:, e:e + 2], A["wab"][:, e:e + 2]).then_inc(s[f"wab{e}_in"], 16)
                sp.dma_start(wdn[:, e:e + 2], A["wdn"][:, e:e + 2]).then_inc(s[f"wdn{e}_in"], 16)
            sp.dma_start(wgu[:], A["wgu"]).then_inc(s["wgu_in"], 16)
            sp.dma_start(wdo[:], A["wdo"]).then_inc(s["wdo_in"], 16)
            sp.wait_ge(s["x"], 5)
            sp.dma_start(out, xs[6][:]).then_inc(s["out_done"], 16)
            sp.wait_ge(s["out_done"], 16)

        @block.gpsimd
        def _(g):
            g.memset(half[:], -0.5).then_inc(s["half"], 1)
            for blocks in (kb, vb):
                last = g.memset(blocks[:], 0.0)
            last.then_inc(s["zeros"], 1)
            g.wait_ge(s["half"], 1)

            def rsqrt(k):
                g.wait_ge(s["var"], k + 1)
                g.tensor_tensor(rs[:, k:k + 1], ve[:, k:k + 1], half[:], ALU.pow).then_inc(s["rstd"], 1)

            rsqrt(0)
            rsqrt(1)
            rsqrt(2)
            rsqrt(3)
            rsqrt(4)
            rsqrt(5)
            rsqrt(6)

        @block.vector
        def _(v):
            steps = [0]

            def step():
                steps[0] += 1
                return steps[0]

            def layernorm(k, n):
                src = xs[n]
                v.bn_stats(st6[:, n, :], src[:]).then_inc(s["v_step"], 1)
                v.wait_ge(s["v_step"], step())
                v.bn_aggr(mv[:, n, :], st6[:, n, :]).then_inc(s["v_step"], 1)
                v.wait_ge(s["v_step"], step())
                v.tensor_scalar(ve[:, k:k + 1], mv[:, n, 1:2], EPS, None, ALU.add).then_inc(s["var"], 1)
                v.wait_ge(s["rstd"], k + 1)
                if n:
                    v.wait_ge(s["yN_turned"], n)
                v.tensor_scalar(yN[:], src[:], mv[:, n, 0:1], rs[:, k:k + 1], ALU.subtract, ALU.mult).then_inc(s["yN"], 1)

            v.wait_ge(s["x_in"], 16)
            layernorm(0, 0)
            v.wait_ge(s["yN_turned"], 1)
            v.tensor_copy(yT[:], PS[:, 7, 0:P]).then_inc(s["yT"], 1)
            v.wait_ge(s["col_in"], 16)
            v.wait_ge(s["qc_mm"], 1)
            v.tensor_scalar(qcT[:], PS[:, 7, 0:P], cv(C_BQC), SC0, ALU.add, ALU.mult).then_inc(s["qcT"], 1)
            v.wait_ge(s["qp_mm"], 1)
            v.tensor_copy(qpT[:], PS[:, 7, 0:P]).then_inc(s["qpT"], 1)
            v.tensor_copy(qbk[:], PS[:, 7, P:P + 1]).then_inc(s["qbk"], 1)
            v.tensor_scalar(hbg[:], cv(C_BG), 0.5, None, ALU.mult).then_inc(s["hbg"], 1)
            v.wait_ge(s["s0_mm"], 1)
            v.tensor_reduce(m0[:, 0:1], PS[:, 0, :], AX, ALU.max, negate=True).then_inc(s["v_step"], 1)
            v.wait_ge(s["v_step"], step())
            v.wait_ge(s["qbk"], 1)
            v.scalar_tensor_tensor(m0[:, 1:2], m0[:, 0:1], qbk[:, 0:1], qbk[:], ALU.subtract, ALU.add).then_inc(s["m0b"], 1)
            v.wait_ge(s["s2_mm"], 1)
            sc2 = PS[:, 5, 256:256 + 2 * L].rearrange("p (r s) -> p r s", r=2)
            v.tensor_reduce(m2[:, 0:2], sc2, AX, ALU.max).then_inc(s["v_step"], 1)
            v.wait_ge(s["v_step"], step())
            v.tensor_tensor(s2[:], sc2, m2[:, 0:2].unsqueeze(2).broadcast_to([P, 2, L]), ALU.subtract).then_inc(s["s2"], 1)
            v.wait_ge(s["e0"], 1)
            v.reciprocal(m0[:, 3:4], m0[:, 2:3]).then_inc(s["r0"], 1)
            v.wait_ge(s["e2"], 1)
            v.tensor_reduce(m2[:, 2:4], e2[:], AX, ALU.add).then_inc(s["v_step"], 1)
            v.wait_ge(s["v_step"], step())
            v.reciprocal(m2[:, 4:6], m2[:, 2:4]).then_inc(s["v_step"], 1)
            v.wait_ge(s["v_step"], step())
            v.tensor_tensor(p2[:], e2[:], m2[:, 4:6].unsqueeze(2).broadcast_to([P, 2, L]), ALU.mult).then_inc(s["p2"], 1)
            v.wait_ge(s["p0_turned"], 1)
            v.tensor_copy(p0T[:, 0:2, :], PS[:, 4, 0:2 * P].rearrange("p (c k) -> p c k", c=2)).then_inc(s["p0T_a"], 1)
            v.wait_ge(s["p2"], 1)
            v.tensor_tensor(pa[:], p2[:, 0, :], p2[:, 1, :], ALU.add).then_inc(s["v_step"], 1)
            v.wait_ge(s["v_step"], step())
            v.transpose(paT[:], pa[:]).then_inc(s["v_step"], 1)
            v.wait_ge(s["v_step"], step())
            v.tensor_tensor(paBD[:].rearrange("p (b i) -> p b i", b=B), paT[:].unsqueeze(1).broadcast_to([P, B, L]),
                            mask_q.unsqueeze(2).broadcast_to([P, B, L]), ALU.mult).then_inc(s["paBD"], 1)
            v.wait_ge(s["pc_mm"], 1)
            v.wait_ge(s["r0"], 1)
            v.tensor_scalar(pcN[:], PS[:, 0, 0:P], m0[:, 3:4], None, ALU.mult).then_inc(s["pcN"], 1)
            v.wait_ge(s["pc_turned"], 1)
            v.tensor_copy(pcT[:], PS[:, 1, 0:P]).then_inc(s["pcT"], 1)
            v.wait_ge(s["s2c_mm"], 1)
            v.tensor_scalar(s2cT[:], PS[:, 5, 384:384 + P], 0.5, cv(C_BVC), ALU.mult, ALU.add).then_inc(s["s2cT"], 1)
            v.wait_ge(s["c2s_mm"], 1)
            v.tensor_scalar(c2sT[:], PS[:, 7, 0:P], cv(C_BVS), None, ALU.add).then_inc(s["c2sT"], 1)
            v.wait_ge(s["c2sT"], 1)
            v.wait_ge(s["s2cT"], 1)
            v.tensor_tensor(dif[:], c2sT[:], s2cT[:], ALU.subtract).then_inc(s["v_step"], 1)
            v.wait_ge(s["v_step"], step())
            v.scalar_tensor_tensor(base[:], dif[:], 0.5, s2cT[:], ALU.mult, ALU.add).then_inc(s["base"], 1)
            v.wait_ge(s["th"], 1)
            v.scalar_tensor_tensor(td[:], dif[:], 0.5, th[:], ALU.mult, ALU.mult).then_inc(s["v_step"], 1)
            v.wait_ge(s["v_step"], step())
            v.wait_ge(s["base"], 1)
            v.tensor_tensor(oT0[:], td[:], base[:], ALU.add).then_inc(s["oT0"], 1)
            v.wait_ge(s["o0_turned"], 1)
            v.tensor_tensor(xs[1][:], PS[:, 4, 0:P], x0[:], ALU.add).then_inc(s["x"], 1)

            v.wait_ge(s["x"], 1)
            layernorm(1, 1)
            v.wait_ge(s["yN_turned"], 2)
            v.tensor_copy(yT[:], PS[:, 7, 0:P]).then_inc(s["yT"], 1)

            def spread(dst, src):
                return v.tensor_tensor(dst, src.rearrange("p (b t) -> p b t", b=B).unsqueeze(2).broadcast_to([P, B, HL, L]),
                                       mask_f.unsqueeze(1).unsqueeze(3).broadcast_to([P, B, HL, L]), ALU.mult)

            def softmax_in(dst, peak, src):
                sc = src.rearrange("p (g s) -> p g s", s=L)
                v.tensor_reduce(peak, sc, AX, ALU.max).then_inc(s["v_step"], 1)
                v.wait_ge(s["v_step"], step())
                return v.tensor_tensor(dst.rearrange("p b (j s) -> p (b j) s", s=L), sc,
                                       peak.unsqueeze(2).broadcast_to([P, peak.shape[1], L]), ALU.subtract)

            def normaliser(dst, inv, total, e, mask):
                v.tensor_reduce(total, e.rearrange("p b (j s) -> p (b j) s", s=L), AX, ALU.add).then_inc(s["v_step"], 1)
                v.wait_ge(s["v_step"], step())
                v.reciprocal(inv, total).then_inc(s["v_step"], 1)
                v.wait_ge(s["v_step"], step())
                return v.tensor_tensor(dst.rearrange("p b j h -> p (b j) h"), inv.unsqueeze(2).broadcast_to([P, inv.shape[1], HL]),
                                       mask.unsqueeze(1).broadcast_to([P, inv.shape[1], HL]), ALU.mult)

            def blocks(dst, src, norm):
                return v.tensor_tensor(dst.rearrange("p b (g d) -> p (b g) d", d=DH), src.rearrange("p (g d) -> p g d", d=DH),
                                       norm.rearrange("p b j h -> p (b j h)").unsqueeze(2).broadcast_to([P, norm.shape[1] * H, DH]),
                                       ALU.mult)

            v.wait_ge(s["q12_mm"], 1)
            spread(qb[:, 0], PS[:, 6, 0:P]).then_inc(s["qb"], 1)
            v.wait_ge(s["q12_mm"], 2)
            spread(qb[:, 1], PS[:, 7, 0:P]).then_inc(s["qb"], 1)
            v.wait_ge(s["row_in"], 16)
            lamb = row[:, R_LAMB:R_LAMB + 1]
            v.tensor_scalar(oml[:], lamb, -1.0, 1.0, ALU.mult, ALU.add).then_inc(s["oml"], 1)
            v.tensor_scalar(mask2[:], mask_q, lamb, -1.0, ALU.mult, ALU.mult).then_inc(s["mask2"], 1)
            v.wait_ge(s["oml"], 1)
            v.tensor_scalar(gl[:], row[:, R_GAMMA:R_GAMMA + D], oml[:], None, ALU.mult).then_inc(s["gl"], 1)
            v.scalar_tensor_tensor(xb[:], row[:, R_BETA:R_BETA + D], oml[:, 0:1], xs[1][:], ALU.mult, ALU.add).then_inc(s["xb"], 1)
            for n in range(2):
                v.wait_ge(s["s1_mm"], n + 1)
                softmax_in(ex[:, n], mx[:, n], PS[:, 6 + n, :]).then_inc(s["ex1_sub"], 1)
            for n in range(2):
                v.wait_ge(s["ex1"], n + 1)
                if n == 1:
                    v.wait_ge(s["mask2"], 1)
                normaliser(rm[:, n], rc[:, n], sm[:, n], ex[:, n], mask_q if n == 0 else mask2[:]).then_inc(s["rm1"], 1)
            for n in range(2):
                v.wait_ge(s["u1_mm"], n + 1)
                v.wait_ge(s["rm1"], n + 1)
                blocks(um[:, n], PS[:, n, :], rm[:, n]).then_inc(s["um1"], 1)
            v.wait_ge(s["a1_mm"], 1)
            a1 = PS[:, 6, 0:D]
            v.bn_stats(st6[:, 5, :], a1).then_inc(s["v_step"], 1)
            v.wait_ge(s["v_step"], step())
            v.bn_aggr(mv[:, 5, :], st6[:, 5, :]).then_inc(s["v_step"], 1)
            v.wait_ge(s["v_step"], step())
            v.tensor_scalar(ve[:, 2:3], mv[:, 5, 1:2], EPS, None, ALU.add).then_inc(s["var"], 1)
            v.wait_ge(s["gl"], 1)
            v.scalar_tensor_tensor(tz[:], a1, mv[:, 5, 0:1], gl[:], ALU.subtract, ALU.mult).then_inc(s["v_step"], 1)
            v.wait_ge(s["v_step"], step())
            v.wait_ge(s["xb"], 1)
            v.wait_ge(s["rstd"], 3)
            v.scalar_tensor_tensor(xs[2][:], tz[:], rs[:, 2:3], xb[:], ALU.mult, ALU.add).then_inc(s["x"], 1)

            v.wait_ge(s["x"], 2)
            v.bn_stats(st6[:, 2, :], xs[2][:]).then_inc(s["v_step"], 1)
            v.wait_ge(s["v_step"], step())
            v.bn_aggr(mv[:, 2, :], st6[:, 2, :]).then_inc(s["v_step"], 1)
            v.wait_ge(s["v_step"], step())
            v.tensor_scalar(ve[:, 3:4], mv[:, 2, 1:2], 1.0 + RMS_EPS, RMS_EPS * EPS, ALU.mult, ALU.add).then_inc(s["var"], 1)
            v.wait_ge(s["rstd"], 4)
            v.wait_ge(s["yN_turned"], 2)
            v.tensor_scalar(yN[:], xs[2][:], mv[:, 2, 0:1], rs[:, 3:4], ALU.subtract, ALU.mult).then_inc(s["yN"], 1)
            v.wait_ge(s["yN_turned"], 3)
            v.tensor_scalar(yT[:], PS[:, 7, 0:P], cv(C_LNW), None, ALU.mult).then_inc(s["yT"], 1)

            def route(n, bias):
                v.wait_ge(s["lg_mm"], n + 1)
                lgp = PS[:, 6, 0:E0N]
                if bias is None:
                    v.tensor_copy(lg[:, n], lgp).then_inc(s["lg"], 1)
                else:
                    v.tensor_tensor(lg[:, n], lgp, bias, ALU.add).then_inc(s["lg"], 1)
                v.wait_ge(s["lg"], n + 1)
                v.max(top[:, n], lg[:, n]).then_inc(s["v_step"], 1)
                v.wait_ge(s["v_step"], step())
                v.max_index(idx[:, n], top[:, n], lg[:, n]).then_inc(s["v_step"], 1)
                v.wait_ge(s["v_step"], step())
                v.tensor_copy(idf[:, n], idx[:, n]).then_inc(s["idf"], 1)

            route(0, row[:, R_BG:R_BG + E0N])
            v.tensor_tensor(tw[:, 0:1], top[:, 0, 1:2], top[:, 0, 0:1], ALU.subtract).then_inc(s["tw_d"], 1)
            v.wait_ge(s["tw_e"], 1)
            v.tensor_scalar(tw[:, 2:3], tw[:, 1:2], 1.0, None, ALU.add).then_inc(s["v_step"], 1)
            v.wait_ge(s["v_step"], step())
            v.reciprocal(tw[:, 3:4], tw[:, 2:3]).then_inc(s["v_step"], 1)
            v.wait_ge(s["v_step"], step())
            v.tensor_tensor(tw[:, 4:5], tw[:, 1:2], tw[:, 3:4], ALU.mult).then_inc(s["v_step"], 1)
            v.wait_ge(s["v_step"], step())
            v.wait_ge(s["idf"], 1)
            v.tensor_scalar(oh[:, 0], iota, idf[:, 0, 0:1], tw[:, 3:4], ALU.is_equal, ALU.mult).then_inc(s["oh"], 1)
            v.tensor_scalar(oh[:, 1], iota, idf[:, 0, 1:2], tw[:, 4:5], ALU.is_equal, ALU.mult).then_inc(s["oh"], 1)
            v.wait_ge(s["oh"], 2)
            v.tensor_tensor(oh[:, 2], oh[:, 0], oh[:, 1], ALU.add).then_inc(s["we"], 1)

            def gate0(e, f):
                n = e * FC0 + f
                v.wait_ge(s["ab_mm"], e + 1)
                v.wait_ge(s["sa"], n + 1)
                if e >= 2 and f == 0:
                    v.wait_ge(s["y_mm"], e - 1)
                v.scalar_tensor_tensor(hT[:, e % 2, f], PS[:, 2 + e % 2, f * P:(f + 1) * P],
                                       cv(C_B1B + n), sa[:, n % 4], ALU.add, ALU.mult).then_inc(s["hT"], 1)

            def add0(e):
                v.wait_ge(s["y_mm"], e + 1)
                v.wait_ge(s["acc"], e + 1)
                v.scalar_tensor_tensor(acc[:, (e + 1) % 2] if e < E0N - 1 else xs[3][:],
                                       PS[:, 4 + e % 2, 0:D], oh[:, 2, e:e + 1], acc[:, e % 2],
                                       ALU.mult, ALU.add).then_inc(s["acc"], 1)

            for e in range(E0N):
                for f in range(FC0):
                    gate0(e, f)
                if e == 0:
                    v.wait_ge(s["we_turned"], 1)
                    v.tensor_copy(weT[:], PS[0:E0N, 6, 0:P]).then_inc(s["weT"], 1)
                if e == 1:
                    v.wait_ge(s["b2_mm"], 1)
                    v.tensor_tensor(acc[:, 0], PS[:, 6, 0:P], xs[2][:], ALU.add).then_inc(s["acc"], 1)
                if e >= 1:
                    add0(e - 1)
            add0(E0N - 1)

            v.wait_ge(s["acc"], E0N + 1)
            layernorm(4, 3)
            v.wait_ge(s["yN_turned"], 4)
            v.tensor_copy(yT[:], PS[:, 7, 0:P]).then_inc(s["yT"], 1)
            v.wait_ge(s["qx_mm"], 1)
            v.tensor_scalar(qxT[:], PS[:, 7, 0:P], cv(C_BQ1), SCH, ALU.add, ALU.mult).then_inc(s["v_step"], 1)
            v.wait_ge(s["v_step"], step())
            spread(qbx[:], qxT[:]).then_inc(s["qbx"], 1)

            def peak(n):
                v.wait_ge(s["sx_mm"], n + 1)
                v.tensor_reduce(nmx[:, n:n + 1], PS[:, n % NJ, :], AX, ALU.max, negate=True).then_inc(s["nmx"], 1)

            def turned(n):
                v.wait_ge(s["xe_turned"], n + 1)
                if n >= 2 * NJ:
                    v.wait_ge(s["ux_mm"], n // NJ - 1)
                v.tensor_copy(xeT[n % (2 * NJ)], PS[:, 5, :]).then_inc(s["xeT_odd"], 1)

            def own_a(b):
                v.wait_ge(s["ux_mm"], b + 1)
                v.tensor_copy(uxT[:, b % 2], PS[:, 6 + b % 2, 0:P]).then_inc(s["uxT"], 1)
                v.reciprocal(rx[:, b], smx[:, b * NJ:(b + 1) * NJ]).then_inc(s["v_step"], 1)
                v.wait_ge(s["v_step"], step())
                v.tensor_tensor(rmx[:, b], rx[:, b].unsqueeze(2).broadcast_to([P, NJ, HL]),
                                mask_q.unsqueeze(1).broadcast_to([P, NJ, HL]), ALU.mult).then_inc(s["rmx"], 1)

            def own_b(b):
                v.wait_ge(s["rmx"], b + 1)
                v.wait_ge(s["ux_turned"], b + 1)
                v.tensor_tensor(umx[:, b].rearrange("p (g d) -> p g d", d=DH),
                                PS[:, 6 + b % 2, P:2 * P].rearrange("p (g d) -> p g d", d=DH),
                                rmx[:, b].rearrange("p j h -> p (j h)").unsqueeze(2).broadcast_to([P, H, DH]),
                                ALU.mult).then_inc(s["umx"], 1)

            def own_c(b):
                v.wait_ge(s["ax_mm"], b + 1)
                v.tensor_scalar(aTx[:, b * L:(b + 1) * L], PS[:, 6 + b % 2, 2 * P:2 * P + L], cv(C_BV1), None, ALU.add).then_inc(s["aTx"], 1)

            v.tensor_tensor(tz[:], xs[3][:], row[:, R_BO:R_BO + D], ALU.add).then_inc(s["x3b"], 1)
            for n in range(B * NJ + 3):
                if n < B * NJ:
                    peak(n)
                if 3 <= n < B * NJ + 2 and n % 2:
                    turned(n - 2)
                for k, part in enumerate((own_a, own_b, own_c)):
                    b = (n - 8 - k) // NJ
                    if (n - 8 - k) % NJ == 0 and 0 <= b < B - 1:
                        part(b)
            own_a(B - 1)
            own_b(B - 1)
            own_c(B - 1)
            v.wait_ge(s["ox_mm"], 1)
            v.wait_ge(s["x3b"], 1)
            v.tensor_tensor(xs[4][:], PS[:, 5, 0:P], tz[:], ALU.add).then_inc(s["x"], 1)

            v.wait_ge(s["x"], 3)
            layernorm(5, 4)
            v.wait_ge(s["yN_turned"], 5)
            v.tensor_copy(yT[:], PS[:, 7, 0:P]).then_inc(s["yT"], 1)
            v.wait_ge(s["q3_mm"], 1)
            spread(qb3, PS[:, 6, 0:P]).then_inc(s["qb3"], 1)
            v.wait_ge(s["s3_mm"], 1)
            for h in range(2):
                bs, gs = slice(2 * h, 2 * h + 2), slice(2 * h * NJ, (2 * h + 2) * NJ)
                v.wait_ge(s["s3_mm"], h + 1)
                softmax_in(ex3[:, bs], mx3[:, gs], PS[:, h, 0:2 * P]).then_inc(s["ex3_sub"], 1)
            for h in range(2):
                bs, gs = slice(2 * h, 2 * h + 2), slice(2 * h * NJ, (2 * h + 2) * NJ)
                v.wait_ge(s["ex3"], h + 1)
                normaliser(rm3[:, bs], rc3[:, gs], sm3[:, gs], ex3[:, bs], mask_q).then_inc(s["rm3"], 1)
            for h in range(2):
                bs = slice(2 * h, 2 * h + 2)
                v.wait_ge(s["u3_mm"], h + 1)
                v.wait_ge(s["rm3"], h + 1)
                blocks(um3[:, bs], PS[:, 5 + h, 0:2 * P], rm3[:, bs]).then_inc(s["um3"], 1)
            v.wait_ge(s["a3_mm"], 1)
            v.tensor_copy(aT3[:], PS[:, 4, 0:P]).then_inc(s["aT3"], 1)
            v.tensor_tensor(tz[:], xs[4][:], row[:, R_BPROJ:R_BPROJ + D], ALU.add).then_inc(s["v_step"], 1)
            v.wait_ge(s["v_step"], step())
            v.wait_ge(s["o3_mm"], 1)
            v.tensor_tensor(xs[5][:], PS[:, 7, 0:P], tz[:], ALU.add).then_inc(s["x"], 1)

            v.wait_ge(s["x"], 4)
            layernorm(6, 5)
            v.wait_ge(s["yN_turned"], 6)
            v.tensor_copy(yT[:], PS[:, 7, 0:P]).then_inc(s["yT"], 1)
            route(1, None)
            v.wait_ge(s["idf"], 2)
            v.tensor_scalar(oh[:, 3], iota, idf[:, 1, 0:1], None, ALU.is_equal).then_inc(s["oh3"], 1)
            for n in range(E1N + 2):
                if n <= E1N:
                    v.wait_ge(s["sa1"], n + 1)
                    if n >= 3:
                        v.wait_ge(s["y1_mm"], n - 2)
                    v.tensor_tensor(hT1[:, n % 3], PS[:, n % 4, 256:512].rearrange("p (f t) -> p f t", f=FC1),
                                    sa1[:, n % 3], ALU.mult).then_inc(s["hT1"], 1)
                if n >= 1:
                    k = n - 1
                    v.wait_ge(s["y1_mm"], k + 1)
                    src = PS[:, 4 + k % 2, 0:D]
                    if k == 0:
                        v.tensor_tensor(acc1[:, 0], src, xs[5][:], ALU.add).then_inc(s["acc1"], 1)
                    else:
                        v.wait_ge(s["acc1"], k)
                        v.wait_ge(s["oh3"], 1)
                        last = v.scalar_tensor_tensor(acc1[:, k % 2] if k < E1N else xs[6][:], src, oh[:, 3, k - 1:k],
                                                      acc1[:, (k - 1) % 2], ALU.mult, ALU.add)
                        last.then_inc(s["acc1"] if k < E1N else s["x"], 1)

        @block.scalar
        def _(a):
            def bg_out(u):
                a.wait_ge(s["bg_mm"], u + 1)
                src = PS[:, 2 + u % 2, :]
                if u < B:
                    a.activation(kx[:, u], src, ACT.Identity, bias=cv(C_BK1)).then_inc(s["bg_out"], 1)
                else:
                    a.activation(vx[:, u - B].rearrange("p c k -> p (c k)"), src, ACT.Copy).then_inc(s["bg_out"], 1)

            def diagonal(dst, src):
                for q in range(NJ):
                    r = slice(q * QW, (q + 1) * QW)
                    last = a.activation(dst[r, :, q], src[r], ACT.Copy)
                return last

            a.wait_ge(s["half"], 1)
            a.activation(warm[:], half[:], ACT.Exp)
            a.wait_ge(s["col_in"], 16)
            a.wait_ge(s["kc_mm"], 1)
            a.activation(kcT[:], PS[:, 6, 0:P], ACT.Identity, bias=cv(C_BKC)).then_inc(s["kcT"], 1)
            a.wait_ge(s["vc_mm"], 1)
            a.activation(vc[:], PS[:, 5, 0:P], ACT.Copy).then_inc(s["vc"], 1)
            a.wait_ge(s["qs_mm"], 1)
            a.activation(qsT[:].rearrange("p r t -> p (r t)"), PS[:, 4, 0:2 * P], ACT.Identity, bias=cv(C_BQS)).then_inc(s["qsT"], 1)
            a.wait_ge(s["m0b"], 1)
            a.activation(e0[:], PS[:, 0, :], ACT.Exp, bias=m0[:, 1:2], accum_out=m0[:, 2:3]).then_inc(s["e0"], 1)
            a.wait_ge(s["s2"], 1)
            a.activation(e2[:], s2[:], ACT.Exp, scale=SC0).then_inc(s["e2"], 1)
            bg_out(0)
            a.wait_ge(s["p0_turned"], 1)
            a.activation(p0T[:, 2:4, :], PS[:, 6, 0:2 * P].rearrange("p (c k) -> p c k", c=2), ACT.Copy).then_inc(s["p0T_b"], 1)
            bg_out(1)
            a.wait_ge(s["g_mm"], 1)
            a.wait_ge(s["hbg"], 1)
            a.activation(th[:], PS[:, 6, 0:P], ACT.Tanh, bias=hbg[:, 0:1], scale=0.5).then_inc(s["th"], 1)
            bg_out(2)
            bg_out(3)

            a.wait_ge(s["zeros"], 1)
            for n in range(2):
                a.wait_ge(s["k12_mm"], n + 1)
                diagonal(kb[:, n], PS[:, 5 - n, 0:P].rearrange("p (b s) -> p b s", b=B)).then_inc(s["kb"], 1)
            a.wait_ge(s["v1_mm"], 1)
            diagonal(vb, PS[:, 0, 0:P].rearrange("p (b w) -> p b w", b=B)).then_inc(s["vb"], 1)
            for n in range(2):
                a.wait_ge(s["ex1_sub"], n + 1)
                a.activation(ex[:, n].rearrange("p b k -> p (b k)"), ex[:, n].rearrange("p b k -> p (b k)"),
                             ACT.Exp, scale=SCH).then_inc(s["ex1"], 1)
            for n in range(2):
                a.wait_ge(s["e1_turned"], n + 1)
                a.activation(eT[:, n].rearrange("p b k -> p (b k)"), PS[:, 4 + n, :], ACT.Copy).then_inc(s["eT"], 1)
            for u in range(4, 8):
                bg_out(u)

            a.wait_ge(s["tw_d"], 1)
            a.activation(tw[:, 1:2], tw[:, 0:1], ACT.Exp).then_inc(s["tw_e"], 1)
            for e in range(E0N):
                for f in range(FC0):
                    n = e * FC0 + f
                    a.wait_ge(s["ab_mm"], e + 1)
                    if n >= 4:
                        a.wait_ge(s["hT"], n - 3)
                    a.activation(sa[:, n % 4], PS[:, e % 2, f * P:(f + 1) * P], ACT.Silu, bias=cv(C_B1A + n)).then_inc(s["sa"], 1)

            def ex_tile(n):
                a.wait_ge(s["nmx"], n + 1)
                if n >= 3:
                    a.wait_ge(s["xe_turned"], n - 2)
                a.activation(xe[:, n % 3], PS[:, n % NJ, :], ACT.Exp, bias=nmx[:, n:n + 1],
                             accum_out=smx[:, n:n + 1]).then_inc(s["xe"], 1)

            def turned(n):
                a.wait_ge(s["xe_turned"], n + 1)
                if n >= 2 * NJ:
                    a.wait_ge(s["ux_mm"], n // NJ - 1)
                a.activation(xeT[n % (2 * NJ)], PS[:, 4, :], ACT.Copy).then_inc(s["xeT_even"], 1)

            for n in range(B * NJ + 1):
                if n < B * NJ:
                    ex_tile(n)
                if n % 2:
                    turned(n - 1)

            a.wait_ge(s["k3_mm"], 1)
            diagonal(kb3, PS[:, 5, 0:P].rearrange("p (b s) -> p b s", b=B)).then_inc(s["kb"], 1)
            a.wait_ge(s["v3_mm"], 1)
            diagonal(vb3, PS[:, 4, 0:P].rearrange("p (b w) -> p b w", b=B)).then_inc(s["vb3"], 1)
            for h in range(2):
                part = ex3[:, 2 * h:2 * h + 2].rearrange("p b k -> p (b k)")
                a.wait_ge(s["ex3_sub"], h + 1)
                a.activation(part, part, ACT.Exp, scale=SCH).then_inc(s["ex3"], 1)
            for h in range(2):
                a.wait_ge(s["e3_turned"], h + 1)
                a.activation(eT3[:, 2 * h:2 * h + 2].rearrange("p b k -> p (b k)"), PS[:, 2 + h, 0:2 * P], ACT.Copy).then_inc(s["eT3"], 1)

            for n in range(E1N + 1):
                a.wait_ge(s["gu_mm"], n + 1)
                if n >= 3:
                    a.wait_ge(s["hT1"], n - 2)
                a.activation(sa1[:, n % 3], PS[:, n % 4, 0:256].rearrange("p (f t) -> p f t", f=FC1), ACT.Silu).then_inc(s["sa1"], 1)

        @block.tensor
        def _(t):
            def mm(o, lhsT, rhs, start=True, stop=True):
                return t.matmul(o, lhsT, rhs, start=start, stop=stop, skip_group_check=True)

            def turn_y(n):
                t.wait_ge(s["yN"], n)
                t.transpose(PS[:, 7, 0:P], yN[:], ident).then_inc(s["yN_turned"], 1)

            piece = [0]

            def bg(n):
                for k in range(piece[0], piece[0] + n):
                    u, c = divmod(k, KC)
                    if k == 0:
                        t.wait_ge(s["w2_in"], 16)
                    if u >= 2 and c == 0:
                        t.wait_ge(s["bg_out"], u - 1)
                    part = ctxT[:, (u % B) * NCTX + c * P:(u % B) * NCTX + (c + 1) * P]
                    o = PS[:, 2 + u % 2, c * P:(c + 1) * P]
                    last = mm(o, w2[:, 1], part) if u < B else mm(o, part, w2[:, 2])
                    if c == KC - 1:
                        last.then_inc(s["bg_mm"], 1)
                piece[0] += n

            t.wait_ge(s["con_in"], 16)
            turn_y(1)
            t.wait_ge(s["w0_in"], 16)
            t.wait_ge(s["yT"], 1)
            mm(PS[:, 7, 0:P], w0[:, 0], yT[:]).then_inc(s["qc_mm"], 1)
            mm(PS[:, 6, 0:P], w0[:, 4], yT[:]).then_inc(s["kc_mm"], 1)
            mm(PS[:, 5, 0:P], yT[:], w0[:, 5]).then_inc(s["vc_mm"], 1)
            t.wait_ge(s["qcT"], 1)
            mm(PS[:, 7, 0:P], w0[:, 1], qcT[:])
            mm(PS[:, 7, P:P + 1], qcT[:], cv(C_BKS)).then_inc(s["qp_mm"], 1)
            t.wait_ge(s["ctxT_in"], 16)
            near = ctxT[:].rearrange("c (b i r) -> c r b i", b=B, r=R)
            for r in range(2):
                last = mm(PS[:, 4, r * P:(r + 1) * P], w0[:, 3], near[:, LO + r])
            last.then_inc(s["qs_mm"], 1)
            t.wait_ge(s["qpT"], 1)
            for b in range(B):
                last = mm(PS[b * L:(b + 1) * L, 0, :], qpT[:, b * L:(b + 1) * L], ctxT[:, b * NCTX:(b + 1) * NCTX])
            last.then_inc(s["s0_mm"], 1)
            t.wait_ge(s["qsT"], 1)
            t.wait_ge(s["kcT"], 1)
            t.wait_ge(s["vc"], 1)
            for r in range(2):
                for b in range(B):
                    last = mm(PS[b * L:(b + 1) * L, 5, 256 + r * L:256 + (r + 1) * L],
                              qsT[:, r, b * L:(b + 1) * L], kcT[:, b * L:(b + 1) * L])
            last.then_inc(s["s2_mm"], 1)
            bg(4)
            t.wait_ge(s["e0"], 1)
            for c in range(KC):
                last = t.transpose(PS[:, 4 + 2 * (c // 2), (c % 2) * P:(c % 2 + 1) * P], e0[:, c * P:(c + 1) * P], ident)
            last.then_inc(s["p0_turned"], 1)
            bg(1)
            t.wait_ge(s["p0T_a"], 1)
            t.wait_ge(s["p0T_b"], 1)
            t.wait_ge(s["ctxN_in"], 16)
            for c in range(KC):
                for b in range(B):
                    last = mm(PS[b * L:(b + 1) * L, 0, 0:D], p0T[:, c, b * L:(b + 1) * L], ctxN[:, b * KC + c],
                              start=(c == 0), stop=(c == KC - 1))
            last.then_inc(s["pc_mm"], 1)
            bg(1)
            t.wait_ge(s["pcN"], 1)
            t.transpose(PS[:, 1, 0:P], pcN[:], ident).then_inc(s["pc_turned"], 1)
            t.wait_ge(s["paBD"], 1)
            t.wait_ge(s["vc"], 1)
            mm(PS[:, 5, 384:384 + P], vc[:], paBD[:]).then_inc(s["s2c_mm"], 1)
            bg(1)
            t.wait_ge(s["pcT"], 1)
            t.wait_ge(s["qbk"], 1)
            mm(PS[:, 7, 0:P], w0[:, 2], pcT[:]).then_inc(s["c2s_mm"], 1)
            bg(1)
            t.wait_ge(s["s2cT"], 1)
            t.wait_ge(s["c2sT"], 1)
            mm(PS[:, 6, 0:P], w0[:, 7], s2cT[:], stop=False)
            mm(PS[:, 6, 0:P], w0[:, 6], c2sT[:], start=False).then_inc(s["g_mm"], 1)
            bg(2)
            t.wait_ge(s["oT0"], 1)
            t.transpose(PS[:, 4, 0:P], oT0[:], ident).then_inc(s["o0_turned"], 1)
            bg(5)

            turn_y(2)
            bg(1)
            t.wait_ge(s["yT"], 2)
            t.wait_ge(s["w1_in"], 16)
            mm(PS[:, 6, 0:P], w1[:, 0], yT[:]).then_inc(s["q12_mm"], 1)
            mm(PS[:, 5, 0:P], w1[:, 1], yT[:]).then_inc(s["k12_mm"], 1)
            mm(PS[:, 7, 0:P], w1[:, 2], yT[:]).then_inc(s["q12_mm"], 1)
            mm(PS[:, 4, 0:P], w1[:, 3], yT[:]).then_inc(s["k12_mm"], 1)

            def values_mm(bank, w):
                for b in range(B):
                    for q in range(NJ):
                        last = mm(PS[q * L:(q + 1) * L, bank, b * QW:(b + 1) * QW], yT[:, b * L:(b + 1) * L], w[:, q * QW:(q + 1) * QW])
                return last

            values_mm(0, w1[:, 4]).then_inc(s["v1_mm"], 1)
            bg(1)
            for n in range(2):
                t.wait_ge(s["qb"], n + 1)
                t.wait_ge(s["kb"], n + 1)
                for b in range(B):
                    last = mm(PS[:, 6 + n, b * P:(b + 1) * P], qb[:, n, b].rearrange("p h t -> p (h t)"),
                              kb[:, n, b].rearrange("p j s -> p (j s)"))
                last.then_inc(s["s1_mm"], 1)
            bg(3)
            for n in range(2):
                t.wait_ge(s["ex1"], n + 1)
                for b in range(B):
                    last = t.transpose(PS[:, 4 + n, b * P:(b + 1) * P], ex[:, n, b], ident)
                last.then_inc(s["e1_turned"], 1)
            t.wait_ge(s["vb"], 1)
            for n in range(2):
                t.wait_ge(s["eT"], n + 1)
                for b in range(B):
                    last = mm(PS[:, n, b * D:(b + 1) * D], eT[:, n, b], vb[:, b].rearrange("p j w -> p (j w)"))
                last.then_inc(s["u1_mm"], 1)
            for n in range(2):
                t.wait_ge(s["um1"], n + 1)
                for b in range(B):
                    last = mm(PS[b * L:(b + 1) * L, 6, 0:D], sel, um[:, n, b], start=(n == 0), stop=(n == 1))
            last.then_inc(s["a1_mm"], 1)
            bg(2 * B * KC - piece[0])

            turn_y(3)
            t.wait_ge(s["yT"], 3)
            t.wait_ge(s["wr_in"], 16)
            mm(PS[:, 6, 0:E0N], yT[:], wr[:, 0]).then_inc(s["lg_mm"], 1)

            def up0(e):
                if e % 2 == 0:
                    t.wait_ge(s[f"wab{e}_in"], 16)
                if e < 2:
                    t.wait_ge(s["bg_out"], 7 + e)
                else:
                    t.wait_ge(s["hT"], FC0 * (e - 1))
                for f in range(FC0):
                    mm(PS[:, e % 2, f * P:(f + 1) * P], wab[:, e, 0, f * P:(f + 1) * P], yT[:])
                    last = mm(PS[:, 2 + e % 2, f * P:(f + 1) * P], wab[:, e, 1, f * P:(f + 1) * P], yT[:])
                last.then_inc(s["ab_mm"], 1)

            def down0(e):
                if e % 2 == 0:
                    t.wait_ge(s[f"wdn{e}_in"], 16)
                if e >= 2:
                    t.wait_ge(s["acc"], e)
                for f in range(FC0):
                    t.wait_ge(s["hT"], FC0 * e + f + 1)
                    last = mm(PS[:, 4 + e % 2, 0:D], hT[:, e % 2, f], wdn[:, e, f], start=(f == 0), stop=(f == FC0 - 1))
                last.then_inc(s["y_mm"], 1)

            up0(0)
            t.wait_ge(s["we"], 1)
            t.transpose(PS[0:E0N, 6, 0:P], oh[:, 2], ident).then_inc(s["we_turned"], 1)
            for e in range(E0N):
                if e + 1 < E0N:
                    up0(e + 1)
                if e == 0:
                    t.wait_ge(s["weT"], 1)
                    t.wait_ge(s["b2_in"], 16)
                    mm(PS[:, 6, 0:P], weT[:], b2[:]).then_inc(s["b2_mm"], 1)
                down0(e)

            turn_y(4)
            t.wait_ge(s["yT"], 4)
            mm(PS[:, 7, 0:P], w2[:, 0], yT[:]).then_inc(s["qx_mm"], 1)
            t.wait_ge(s["qbx"], 1)
            t.wait_ge(s["acc"], E0N + 1)

            def score(n):
                b, j = divmod(n, NJ)
                q = slice(j * QW, (j + 1) * QW)
                if n >= NJ:
                    t.wait_ge(s["xe"], n - NJ + 1)
                mm(PS[:, j, :], qbx[q, b].rearrange("p h t -> p (h t)"), kx[q, b]).then_inc(s["sx_mm"], 1)

            def copied(n):
                t.wait_ge(s["xeT_odd"] if n % 2 else s["xeT_even"], n // 2 + 1)

            def turn(n):
                t.wait_ge(s["xe"], n + 1)
                if n >= 2:
                    copied(n - 2)
                for c in range(KC):
                    last = t.transpose(PS[:, 4 + n % 2, c * P:(c + 1) * P], xe[:, n % 3, c * P:(c + 1) * P], ident)
                last.then_inc(s["xe_turned"], 1)

            def values(b):
                if b >= 2:
                    t.wait_ge(s["aTx"], b - 1)
                for n in range(NJ * b, NJ * (b + 1)):
                    copied(n)
                for c in range(KC):
                    for j in range(NJ):
                        q = slice(j * QW, (j + 1) * QW)
                        last = mm(PS[q, 6 + b % 2, 0:P], vx[:, b, c, q], xeT[(NJ * b + j) % (2 * NJ)][:, c * P:(c + 1) * P],
                                  start=(c == 0), stop=(c == KC - 1))
                last.then_inc(s["ux_mm"], 1)

            def unturn(b):
                t.wait_ge(s["uxT"], b + 1)
                t.transpose(PS[:, 6 + b % 2, P:2 * P], uxT[:, b % 2], ident).then_inc(s["ux_turned"], 1)

            def fold(b):
                t.wait_ge(s["umx"], b + 1)
                mm(PS[:, 6 + b % 2, 2 * P:2 * P + L], umx[:, b], sel).then_inc(s["ax_mm"], 1)

            score(0)
            score(1)
            for n in range(B * NJ + 2):
                if n + 2 < B * NJ:
                    score(n + 2)
                if 0 <= n - 1 < B * NJ:
                    turn(n - 1)
                if (n - 5) % NJ == 0 and n >= 5:
                    values((n - 5) // NJ)
                if n % NJ == 0 and n >= 8:
                    unturn(n // NJ - 2)
                if n % NJ == 1 and n >= 9:
                    fold(n // NJ - 2)
            unturn(B - 1)
            fold(B - 1)
            t.wait_ge(s["aTx"], B)
            mm(PS[:, 5, 0:P], aTx[:], w2[:, 3]).then_inc(s["ox_mm"], 1)

            for h in range(2):
                mm(PS[:, h, 0:2 * P].rearrange("p (b k) -> p b k", b=2), ident, alibi.unsqueeze(1).broadcast_to([P, 2, NJ * L]),
                   stop=False)
            turn_y(5)
            t.wait_ge(s["yT"], 5)
            mm(PS[:, 6, 0:P], w2[:, 4], yT[:]).then_inc(s["q3_mm"], 1)
            mm(PS[:, 5, 0:P], w2[:, 5], yT[:]).then_inc(s["k3_mm"], 1)
            values_mm(4, w2[:, 6]).then_inc(s["v3_mm"], 1)
            t.wait_ge(s["qb3"], 1)
            t.wait_ge(s["kb"], 3)
            for b in range(B):
                last = mm(PS[:, b // 2, b % 2 * P:(b % 2 + 1) * P], qb3[:, b].rearrange("p h t -> p (h t)"),
                          kb3[:, b].rearrange("p j s -> p (j s)"), start=False)
                if b % 2:
                    last.then_inc(s["s3_mm"], 1)
            for b in range(B):
                if b % 2 == 0:
                    t.wait_ge(s["ex3"], b // 2 + 1)
                last = t.transpose(PS[:, 2 + b // 2, b % 2 * P:(b % 2 + 1) * P], ex3[:, b], ident)
                if b % 2:
                    last.then_inc(s["e3_turned"], 1)
            t.wait_ge(s["vb3"], 1)
            for b in range(B):
                if b % 2 == 0:
                    t.wait_ge(s["eT3"], b // 2 + 1)
                last = mm(PS[:, 5 + b // 2, b % 2 * D:(b % 2 + 1) * D], eT3[:, b], vb3[:, b].rearrange("p j w -> p (j w)"))
                if b % 2:
                    last.then_inc(s["u3_mm"], 1)
            for b in range(B):
                if b % 2 == 0:
                    t.wait_ge(s["um3"], b // 2 + 1)
                last = mm(PS[:, 4, b * L:(b + 1) * L], um3[:, b], sel)
            last.then_inc(s["a3_mm"], 1)
            t.wait_ge(s["aT3"], 1)
            mm(PS[:, 7, 0:P], aT3[:], w2[:, 7]).then_inc(s["o3_mm"], 1)

            turn_y(6)
            t.wait_ge(s["yT"], 6)
            mm(PS[:, 6, 0:E0N], yT[:], wr[:, 1]).then_inc(s["lg_mm"], 1)
            t.wait_ge(s["wgu_in"], 16)
            t.wait_ge(s["wdo_in"], 16)

            def up1(n):
                if n >= 4:
                    t.wait_ge(s["hT1"], n - 3)
                for k in range(2):
                    for f in range(FC1):
                        last = mm(PS[:, n % 4, (k * FC1 + f) * P:(k * FC1 + f + 1) * P], wgu[:, n, k, f * P:(f + 1) * P], yT[:])
                last.then_inc(s["gu_mm"], 1)

            def down1(n):
                if n >= 2:
                    t.wait_ge(s["acc1"], n - 1)
                t.wait_ge(s["hT1"], n + 1)
                for f in range(FC1):
                    last = mm(PS[:, 4 + n % 2, 0:D], hT1[:, n % 3, f], wdo[:, n, f], start=(f == 0), stop=(f == FC1 - 1))
                last.then_inc(s["y1_mm"], 1)

            up1(0)
            up1(1)
            for n in range(E1N + 1):
                if n + 2 <= E1N:
                    up1(n + 2)
                down1(n)


def kernel(**inputs):
    import concourse.bacc as bacc
    from concourse.bass_utils import run_bass_kernel_spmd

    I = {k: np.asarray(a) for k, a in inputs.items()}
    ctx = I["ctx_1024"].reshape(B * NCTX, D)

    def stack(*ws):
        return np.stack(ws, 1)

    def heads(w):
        return w.transpose(1, 0, 2).reshape(D, D)

    def chunks(w):
        return w.reshape(w.shape[0], -1, P, w.shape[2]).transpose(2, 0, 1, 3)

    x0, x1 = "L0_xattn_", "L1_xattn_"
    cols = [I[x0 + n] for n in ("bq_c", "bk_s", "bv_s", "bq_s", "bk_c", "bv_c", "bg")]
    cols += [I["L0_ffn_ln_w"], I[x1 + "bq"], I[x1 + "bk"], I[x1 + "bv"]]
    cols += list(I["L0_ffn_b1a"].reshape(-1, P)) + list(I["L0_ffn_b1b"].reshape(-1, P))
    up = np.concatenate([I["L1_ffn_w_up_s"][None], I["L1_ffn_up"]])
    gate = np.concatenate([I["L1_ffn_w_gate_s"][None], I["L1_ffn_gate"]])
    down = np.concatenate([I["L1_ffn_w_down_s"][None], I["L1_ffn_down"]])
    arrays = {
        "x": I["x"].reshape(P, D),
        "con": shape_constants(),
        "col": np.stack(cols, 1),
        "row": np.concatenate([I["L0_attn_ln_gamma"], I["L0_attn_ln_beta"], I[x1 + "bo"], I["L1_attn_b_proj"],
                               I["L0_ffn_bg"], I["L0_attn_lamb"].reshape(1)]),
        "w0": stack(I[x0 + "Wq_c"].T, I[x0 + "Wk_s"], I[x0 + "Wv_s"].T, I[x0 + "Wq_s"].T, I[x0 + "Wk_c"].T,
                    I[x0 + "Wv_c"].T, I[x0 + "Wg"][:, :D].T, I[x0 + "Wg"][:, D:].T),
        "w1": stack(*[heads(I["L0_attn_" + n]) for n in ("wq1", "wk1", "wq2", "wk2", "wv")]),
        "w2": stack(I[x1 + "Wq"].T, I[x1 + "Wk"].T, I[x1 + "Wv"].T, I[x1 + "Wo"].T, I["L1_attn_W_query"],
                    I["L1_attn_W_key"], I["L1_attn_W_value"], I["L1_attn_W_proj"]),
        "wr": stack(I["L0_ffn_Wg"], I["L1_ffn_router"].T),
        "b2": I["L0_ffn_b2"],
        "ctxT": ctx.T,
        "ctxN": ctx.reshape(B * KC, P, D).transpose(1, 0, 2),
        "wab": np.stack([I["L0_ffn_W1a"], I["L0_ffn_W1b"]]).transpose(2, 1, 0, 3),
        "wdn": chunks(I["L0_ffn_W2"]),
        "wgu": np.stack([gate, up]).transpose(3, 1, 0, 2),
        "wdo": chunks(down.transpose(0, 2, 1)),
    }
    nc = bacc.Bacc("TRN2", target_bir_lowering=False, num_devices=1)
    A = {}
    for name, a in arrays.items():
        arrays[name] = a = np.ascontiguousarray(a)
        A[name] = nc.dram_tensor(f"in_{name}", a.shape, mybir.dt.from_np(a.dtype), kind="ExternalInput").ap()
    out = nc.dram_tensor("out_x", (P, D), F32, kind="ExternalOutput").ap()
    build(nc, A, out)
    r = run_bass_kernel_spmd(nc, [{f"in_{k}": a for k, a in arrays.items()}], core_ids=[0])
    return r.results[0]["out_x"].reshape(B, L, D)
```

```python
from contextlib import ExitStack

import numpy as np
import concourse.bass as bass
from concourse import mybir

F32 = mybir.dt.float32
U32 = mybir.dt.uint32
ALU = mybir.AluOpType
ACT = mybir.ActivationFunctionType
AX = mybir.AxisListType.X

P = 128
B, L, D = 4, 32, 128
NCTX = 512
KC = NCTX // P
H, DH = 16, 8
NJ, HL = 4, 4
QW = D // NJ
E0N, F0 = 8, 512
FC0 = F0 // P
E1N, F1 = 8, 256
FC1 = F1 // P
R = NCTX // L
LO = R // 2 - 1
EPS = 1e-5
RMS_EPS = float(np.finfo(np.float32).eps)
SC0 = float(D) ** -0.5
SCH = float(DH) ** -0.5

(C_BQC, C_BKS, C_BVS, C_BQS, C_BKC, C_BVC, C_BG, C_LNW, C_BQ1, C_BK1, C_BV1) = range(11)
C_B1A = 11
C_B1B = C_B1A + E0N * FC0
N_COLS = C_B1B + E0N * FC0
R_GAMMA, R_BETA, R_BO, R_BPROJ, R_BG, R_LAMB = 0, D, 2 * D, 3 * D, 4 * D, 4 * D + E0N
N_ROWS = R_LAMB + 1
K_ID = 0
K_MF = K_ID + P
K_MQ = K_MF + HL
K_SEL = K_MQ + NJ
K_IOTA = K_SEL + L
K_ALIBI = K_IOTA + E0N
K_MH = K_ALIBI + NJ * L
N_CONST = K_MH + H
MASKED = -1e30
FILL = dict(start=8, y1=2, qc=2, qp=2, s2=4, p0=1, pc=2, c2s=1, g=2, y2=1, e1=2, a1=10, y3=1,
            un=2, ox=6, y5=1, v3=1, s3=3, a3=1, o3=8, y6=1)
PIECES = dict(g=4, o0=8, s1=2, x=10, y4=3)


def shape_constants():
    k = np.zeros((P, N_CONST), np.float32)
    p = np.arange(P)
    k[:, K_ID:K_ID + P] = np.eye(P)
    k[:, K_MF:K_MF + HL] = (p[:, None] // DH) % HL == np.arange(HL)
    k[:, K_MQ:K_MQ + NJ] = p[:, None] // QW == np.arange(NJ)
    k[:, K_SEL:K_SEL + L] = p[:, None] % L == np.arange(L)
    k[:, K_IOTA:K_IOTA + E0N] = np.arange(E0N)
    k[:, K_MH:K_MH + H] = (p[:, None] // DH == np.arange(H)) * np.float32(SCH)
    slopes = np.float32(2.0) ** (np.float32(-8.0) * np.arange(1, H + 1, dtype=np.float32) / np.float32(H))
    for j in range(NJ):
        for hl in range(HL):
            t = np.arange(L, dtype=np.float32)
            bias = slopes[j * HL + hl] * (t[None, :] - t[:, None])
            bias[t[None, :] > t[:, None]] = MASKED
            k[hl * L:(hl + 1) * L, K_ALIBI + j * L:K_ALIBI + (j + 1) * L] = bias
    return k


def build(nc, A, out):
    with ExitStack() as ctx:
        def sb(name, shape, dt=F32):
            return ctx.enter_context(nc.sbuf_tensor(name, shape, dt))

        class Sems(dict):
            def __missing__(self, name):
                self[name] = ctx.enter_context(nc.semaphore(name))
                return self[name]

        s = Sems()

        x0 = sb("x0", [P, D])
        con = sb("con", [P, N_CONST])
        col = sb("col", [P, N_COLS])
        row = sb("row", [P, N_ROWS])
        w0 = sb("w0", [P, 8, D])
        w1 = sb("w1", [P, 5, D])
        w2 = sb("w2", [P, 8, D])
        wr = sb("wr", [P, 2, E0N])
        b2 = sb("b2", [E0N, D])
        ctxT = sb("ctxT", [P, B * NCTX])
        ctxN = sb("ctxN", [P, B * KC, D])
        wab = sb("wab", [P, E0N, 2, F0])
        wdn = sb("wdn", [P, E0N, FC0, D])
        wgu = sb("wgu", [P, E1N + 1, 2, F1])
        wdo = sb("wdo", [P, E1N + 1, FC1, D])

        ident = con[:, K_ID:K_ID + P]
        mask_f = con[:, K_MF:K_MF + HL]
        mask_q = con[:, K_MQ:K_MQ + NJ]
        sel = con[:, K_SEL:K_SEL + L]
        iota = con[:, K_IOTA:K_IOTA + E0N]
        alibi = con[:, K_ALIBI:K_ALIBI + NJ * L]
        mask_h = con[:, K_MH:K_MH + H]

        def cv(i):
            return col[:, i:i + 1]

        xeT = [t[:, k * NCTX:(k + 1) * NCTX] for t in (ctxN[:].rearrange("p c k -> p (c k)"), ctxT[:]) for k in range(NJ)]

        qbx = [wab[:, b // 2, b % 2].rearrange("p (h t) -> p h t", t=L) for b in range(B)]

        half = sb("half", [P, 1])
        blank = sb("blank", [P, P])
        euler = sb("euler", [P, 1])
        warm = sb("warm", [P, 1])
        st6 = sb("st6", [P, 6, 6])
        mv = sb("mv", [P, 6, 2])
        ve = sb("ve", [P, 8])
        rs = sb("rs", [P, 8])
        yN = sb("yN", [P, D])
        yT = sb("yT", [P, D])
        xs = [x0] + [sb(f"x{i}", [P, D]) for i in range(1, 7)]
        qcT = sb("qcT", [P, P])
        kcT = sb("kcT", [P, P])
        vc = sb("vc", [P, D])
        qpT = sb("qpT", [P, P])
        qbk = sb("qbk", [P, 1])
        qsT = sb("qsT", [P, 2, P])
        m0 = sb("m0", [P, 4])
        e0 = sb("e0", [P, NCTX])
        p0T = sb("p0T", [P, KC, P])
        pcN = sb("pcN", [P, P])
        pcT = sb("pcT", [P, P])
        c2sT = sb("c2sT", [P, P])
        s2 = sb("s2", [P, 2, L])
        e2 = sb("e2", [P, 2, L])
        p2 = sb("p2", [P, 2, L])
        m2 = sb("m2", [P, 8])
        pa = sb("pa", [P, L])
        paT = sb("paT", [P, L])
        paBD = sb("paBD", [P, P])
        s2cT = sb("s2cT", [P, P])
        hbg = sb("hbg", [P, 1])
        th = sb("th", [P, P])
        dif = sb("dif", [P, P])
        base = sb("base", [P, P])
        td = sb("td", [P, P])
        oT0 = sb("oT0", [P, P])
        qb = sb("qb", [P, 2, B, HL, L])
        kb = sb("kb", [P, 2, B, NJ, L])
        vb = sb("vb", [P, B, D + NJ])
        mx = sb("mx", [P, 2, B * NJ])
        ex = sb("ex", [P, 2, B, P])
        eT = sb("eT", [P, 2, B, P])
        rc = sb("rc", [P, 2, B * NJ])
        sm3 = sb("sm3", [P, B * NJ])
        mask2 = sb("mask2", [P, HL])
        rm = sb("rm", [P, 2, B, NJ, HL])
        um = sb("um", [P, 2, B, D])
        gl = sb("gl", [P, D])
        xb = sb("xb", [P, D])
        oml = sb("oml", [P, 1])
        tz = sb("tz", [P, D])
        qb3, kb3, ex3, eT3, rm3, um3 = qb[:, 0], kb[:, 0], ex[:, 0], eT[:, 0], rm[:, 0], um[:, 0]
        mx3, rc3 = mx[:, 0], rc[:, 0]
        aT3 = sb("aT3", [P, P])
        kx = sb("kx", [P, B, NCTX])
        vx = sb("vx", [P, B, KC, D])
        qxT = sb("qxT", [P, P])
        nmx = sb("nmx", [P, B * NJ])
        xe = sb("xe", [P, 3, NCTX])
        smx = sb("smx", [P, B * NJ])
        rx = sb("rx", [P, B, NJ])
        rmT = sb("rmT", [P, 2, P])
        rmx = sb("rmx", [P, 2, P])
        umx = sb("umx", [P, B, D])
        aTx = sb("aTx", [P, P])
        lg = sb("lg", [P, 2, E0N])
        top = sb("top", [P, 2, 8])
        idx = sb("idx", [P, 2, 8], U32)
        idf = sb("idf", [P, 2, 8])
        tw = sb("tw", [P, 6])
        oh = sb("oh", [P, 4, E0N])
        weT = sb("weT", [E0N, P])
        sa = sb("sa", [P, 4, P])
        hT = sb("hT", [P, 2, FC0, P])
        acc = sb("acc", [P, 2, D])
        sa1 = sb("sa1", [P, 3, FC1, P])
        hT1 = sb("hT1", [P, 3, FC1, P])
        acc1 = sb("acc1", [P, 2, D])

        PS = ctx.enter_context(nc.psum_tensor("PS", [P, 8, 512], F32))

        def bs(h):
            return slice(2 * h, 2 * h + 2)

        def gs(h):
            return slice(2 * h * NJ, (2 * h + 2) * NJ)

        S_BANK = (1, 6, 7, 7)
        T_BANK = (4, 5, 6, 4)
        U_BANK = (0, 1, 5, 7)

        RX_BANK = (6, 7, 6, 2)

        def ab_banks(e, f):
            return (e % 2, 2 + e % 2) if e < E0N - 1 or f < FC0 // 2 else (6, 7)

        def y0_bank(e):
            return (4, 5, 7, 4, 5, 4, 5, 4)[e]

        def y1_bank(n):
            return 4 + n % 2 if n < E1N else 6

        def ab_ready(e, f):
            return e + 1 if e < E0N - 1 or f < FC0 // 2 else e + 2

        def bg_bank(u):
            return 2 + u % 2 if u < B else u - B

        block = ctx.enter_context(nc.Block())

        @block.sync
        def _(sp):
            sp.dma_start(x0[:], A["x"]).then_inc(s["x_in"], 16)
            sp.dma_start(con[:], A["con"]).then_inc(s["con_in"], 16)
            sp.dma_start(w0[:, 0:2], A["w0"][:, 0:2]).then_inc(s["w0_in"], 16)
            sp.dma_start(col[:], A["col"]).then_inc(s["col_in"], 16)
            sp.dma_start(ctxT[:], A["ctxT"]).then_inc(s["ctxT_in"], 16)
            sp.dma_start(w0[:, 2:8], A["w0"][:, 2:8]).then_inc(s["w0_rest_in"], 16)
            sp.dma_start(ctxN[:], A["ctxN"]).then_inc(s["ctxN_in"], 16)
            sp.dma_start(w2[:], A["w2"]).then_inc(s["w2_in"], 16)
            sp.dma_start(w1[:], A["w1"]).then_inc(s["w1_in"], 16)
            sp.dma_start(row[:], A["row"].partition_broadcast(P)).then_inc(s["row_in"], 16)
            sp.dma_start(wr[:], A["wr"]).then_inc(s["wr_in"], 16)
            sp.dma_start(b2[:], A["b2"]).then_inc(s["b2_in"], 16)
            for e in range(0, E0N, 2):
                sp.dma_start(wab[:, e:e + 2], A["wab"][:, e:e + 2]).then_inc(s[f"wab{e}_in"], 16)
                sp.dma_start(wdn[:, e:e + 2], A["wdn"][:, e:e + 2]).then_inc(s[f"wdn{e}_in"], 16)
            sp.dma_start(wgu[:], A["wgu"]).then_inc(s["wgu_in"], 16)
            sp.dma_start(wdo[:], A["wdo"]).then_inc(s["wdo_in"], 16)
            sp.wait_ge(s["x"], 5)
            sp.dma_start(out, xs[6][:]).then_inc(s["out_done"], 16)
            sp.wait_ge(s["out_done"], 16)

        @block.gpsimd
        def _(g):
            g.memset(blank[:], 0.0).then_inc(s["blank"], 1)
            g.memset(half[:], -0.5).then_inc(s["half"], 1)
            g.memset(euler[:], float(np.e))
            for tile in (kb, vb):
                last = g.memset(tile[:], 0.0)
            last.then_inc(s["zeros"], 1)
            g.wait_ge(s["half"], 1)

            def rsqrt(k):
                g.wait_ge(s["var"], k + 1)
                g.tensor_tensor(rs[:, k:k + 1], ve[:, k:k + 1], half[:], ALU.pow).then_inc(s["rstd"], 1)

            rsqrt(0)
            rsqrt(1)
            rsqrt(2)
            rsqrt(3)
            g.wait_ge(s["tw_d"], 1)
            g.tensor_tensor(tw[:, 1:2], euler[:], tw[:, 0:1], ALU.pow).then_inc(s["tw_e"], 1)
            rsqrt(4)
            g.wait_ge(s["qxT"], 1)
            for b in range(1, B):
                g.tensor_tensor(qbx[b], qxT[:, b * L:(b + 1) * L].unsqueeze(1).broadcast_to([P, H, L]),
                                mask_h.unsqueeze(2).broadcast_to([P, H, L]), ALU.mult).then_inc(s["qbx"], 1)
            rsqrt(5)
            rsqrt(6)

        @block.vector
        def _(v):
            steps = [0]

            def step():
                steps[0] += 1
                return steps[0]

            def layernorm(k, n):
                src = xs[n]
                v.bn_stats(st6[:, n, :], src[:]).then_inc(s["v_step"], 1)
                v.wait_ge(s["v_step"], step())
                v.bn_aggr(mv[:, n, :], st6[:, n, :]).then_inc(s["v_step"], 1)
                v.wait_ge(s["v_step"], step())
                v.tensor_scalar(ve[:, k:k + 1], mv[:, n, 1:2], EPS, None, ALU.add).then_inc(s["var"], 1)
                v.wait_ge(s["rstd"], k + 1)
                if n:
                    v.wait_ge(s["yN_turned"], n)
                v.tensor_scalar(yN[:], src[:], mv[:, n, 0:1], rs[:, k:k + 1], ALU.subtract, ALU.mult).then_inc(s["yN"], 1)

            v.wait_ge(s["x_in"], 16)
            layernorm(0, 0)
            v.wait_ge(s["yN_turned"], 1)
            v.tensor_copy(yT[:], PS[:, 7, 0:P]).then_inc(s["yT"], 1)
            v.wait_ge(s["col_in"], 16)
            v.wait_ge(s["qc_mm"], 1)
            v.tensor_scalar(qcT[:], PS[:, 7, 0:P], cv(C_BQC), SC0, ALU.add, ALU.mult).then_inc(s["qcT"], 1)
            v.wait_ge(s["qp_mm"], 1)
            v.tensor_copy(qpT[:], PS[:, 7, 0:P]).then_inc(s["qpT"], 1)
            v.tensor_copy(qbk[:], PS[:, 7, P:P + 1]).then_inc(s["qbk"], 1)
            v.tensor_scalar(hbg[:], cv(C_BG), 0.5, None, ALU.mult).then_inc(s["hbg"], 1)
            v.wait_ge(s["zeros"], 1)
            v.tensor_copy(vb[:, :, D:D + NJ], mask_q.unsqueeze(1).broadcast_to([P, B, NJ])).then_inc(s["vb_ones"], 1)
            v.wait_ge(s["s0_mm"], 1)
            v.tensor_reduce(m0[:, 0:1], PS[:, 0, :], AX, ALU.max, negate=True).then_inc(s["v_step"], 1)
            v.wait_ge(s["v_step"], step())
            v.wait_ge(s["qbk"], 1)
            v.scalar_tensor_tensor(m0[:, 1:2], m0[:, 0:1], qbk[:, 0:1], qbk[:], ALU.subtract, ALU.add).then_inc(s["m0b"], 1)
            v.wait_ge(s["p0_turned"], 1)
            v.tensor_copy(p0T[:, 0:2, :], PS[:, 4, 0:2 * P].rearrange("p (c k) -> p c k", c=2)).then_inc(s["p0T_a"], 1)
            v.wait_ge(s["s2_mm"], 1)
            sc2 = PS[:, 5, 256:256 + 2 * L].rearrange("p (r s) -> p r s", r=2)
            v.tensor_reduce(m2[:, 0:2], sc2, AX, ALU.max).then_inc(s["v_step"], 1)
            v.wait_ge(s["v_step"], step())
            v.tensor_tensor(s2[:], sc2, m2[:, 0:2].unsqueeze(2).broadcast_to([P, 2, L]), ALU.subtract).then_inc(s["s2"], 1)
            v.wait_ge(s["e0"], 1)
            v.reciprocal(m0[:, 3:4], m0[:, 2:3]).then_inc(s["r0"], 1)
            v.wait_ge(s["e2"], 1)
            v.tensor_reduce(m2[:, 2:4], e2[:], AX, ALU.add).then_inc(s["v_step"], 1)
            v.wait_ge(s["v_step"], step())
            v.reciprocal(m2[:, 4:6], m2[:, 2:4]).then_inc(s["v_step"], 1)
            v.wait_ge(s["v_step"], step())
            v.tensor_tensor(p2[:], e2[:], m2[:, 4:6].unsqueeze(2).broadcast_to([P, 2, L]), ALU.mult).then_inc(s["p2"], 1)
            v.wait_ge(s["pc_mm"], 1)
            v.wait_ge(s["r0"], 1)
            v.tensor_scalar(pcN[:], PS[:, 0, 0:P], m0[:, 3:4], None, ALU.mult).then_inc(s["pcN"], 1)
            v.wait_ge(s["p2"], 1)
            v.tensor_tensor(pa[:], p2[:, 0, :], p2[:, 1, :], ALU.add).then_inc(s["v_step"], 1)
            v.wait_ge(s["v_step"], step())
            v.transpose(paT[:], pa[:]).then_inc(s["v_step"], 1)
            v.wait_ge(s["v_step"], step())
            v.tensor_tensor(paBD[:].rearrange("p (b i) -> p b i", b=B), paT[:].unsqueeze(1).broadcast_to([P, B, L]),
                            mask_q.unsqueeze(2).broadcast_to([P, B, L]), ALU.mult).then_inc(s["paBD"], 1)
            v.wait_ge(s["pc_turned"], 1)
            v.tensor_copy(pcT[:], PS[:, 1, 0:P]).then_inc(s["pcT"], 1)
            v.wait_ge(s["s2c_mm"], 1)
            v.tensor_scalar(s2cT[:], PS[:, 5, 384:384 + P], 0.5, cv(C_BVC), ALU.mult, ALU.add).then_inc(s["s2cT"], 1)
            v.wait_ge(s["c2s_mm"], 1)
            v.tensor_scalar(c2sT[:], PS[:, 7, 0:P], cv(C_BVS), None, ALU.add).then_inc(s["c2sT"], 1)
            v.wait_ge(s["c2sT"], 1)
            v.wait_ge(s["s2cT"], 1)
            v.tensor_tensor(dif[:], c2sT[:], s2cT[:], ALU.subtract).then_inc(s["v_step"], 1)
            v.wait_ge(s["v_step"], step())
            v.scalar_tensor_tensor(base[:], dif[:], 0.5, s2cT[:], ALU.mult, ALU.add).then_inc(s["base"], 1)
            v.wait_ge(s["th"], 1)
            v.scalar_tensor_tensor(td[:], dif[:], 0.5, th[:], ALU.mult, ALU.mult).then_inc(s["v_step"], 1)
            v.wait_ge(s["v_step"], step())
            v.wait_ge(s["base"], 1)
            v.tensor_tensor(oT0[:], td[:], base[:], ALU.add).then_inc(s["oT0"], 1)
            v.wait_ge(s["o0_turned"], 1)
            v.tensor_tensor(xs[1][:], PS[:, 4, 0:P], x0[:], ALU.add).then_inc(s["x"], 1)

            v.wait_ge(s["x"], 1)
            layernorm(1, 1)
            v.wait_ge(s["yN_turned"], 2)
            v.tensor_copy(yT[:], PS[:, 7, 0:P]).then_inc(s["yT"], 1)

            def spread(dst, src):
                n = dst.shape[1]
                return v.tensor_tensor(dst, src.rearrange("p (b t) -> p b t", b=n).unsqueeze(2).broadcast_to([P, n, HL, L]),
                                       mask_f.unsqueeze(1).unsqueeze(3).broadcast_to([P, n, HL, L]), ALU.mult)

            def softmax_in(dst, peak, src):
                sc = src.rearrange("p (g s) -> p g s", s=L)
                v.tensor_reduce(peak, sc, AX, ALU.max).then_inc(s["v_step"], 1)
                v.wait_ge(s["v_step"], step())
                return v.tensor_tensor(dst.rearrange("p b (j s) -> p (b j) s", s=L), sc,
                                       peak.unsqueeze(2).broadcast_to([P, peak.shape[1], L]), ALU.subtract)

            def products(bank):
                return PS[:, bank, 0:2 * (D + NJ)].rearrange("p (b w) -> p b w", b=2)

            def inverse(inv, sums):
                v.reciprocal(inv.rearrange("p (b j) -> p b j", b=2), sums).then_inc(s["v_step"], 1)
                return step()

            def normaliser(norm, inv, ready, mask):
                v.wait_ge(s["v_step"], ready)
                v.tensor_tensor(norm.rearrange("p b j h -> p (b j) h"), mask.unsqueeze(1).broadcast_to([P, 2 * NJ, HL]),
                                inv.unsqueeze(2).broadcast_to([P, 2 * NJ, HL]), ALU.mult).then_inc(s["v_step"], 1)
                return step()

            def blocks(dst, u, norm):
                return v.tensor_tensor(dst.rearrange("p b (g d) -> p b g d", d=DH), u[:, :, 0:D].rearrange("p b (g d) -> p b g d", d=DH),
                                       norm.rearrange("p b j h -> p b (j h)").unsqueeze(3).broadcast_to([P, 2, H, DH]),
                                       ALU.mult)

            for n, h in ((0, 0), (0, 1), (1, slice(0, 4))):
                b = bs(h) if n == 0 else h
                v.wait_ge(s["q12_mm"], n + 1)
                spread(qb[:, n, b], PS[:, 6 + n, b.start * L:b.stop * L]).then_inc(s["qb"], 1)
            for k in range(4):
                n, h = divmod(k, 2)
                v.wait_ge(s["s1_mm"], min(k + 1, 3))
                softmax_in(ex[:, n, bs(h)], mx[:, n, gs(h)], PS[:, S_BANK[k], h * 2 * P:(h + 1) * 2 * P]).then_inc(s["ex1_sub"], 1)
            v.wait_ge(s["row_in"], 16)
            lamb = row[:, R_LAMB:R_LAMB + 1]
            v.tensor_scalar(oml[:], lamb, -1.0, 1.0, ALU.mult, ALU.add).then_inc(s["oml"], 1)
            v.tensor_scalar(mask2[:], mask_q, lamb, -1.0, ALU.mult, ALU.mult).then_inc(s["mask2"], 1)
            v.wait_ge(s["oml"], 1)
            v.tensor_scalar(gl[:], row[:, R_GAMMA:R_GAMMA + D], oml[:], None, ALU.mult).then_inc(s["gl"], 1)
            v.wait_ge(s["mask2"], 1)

            def inverse1(k):
                n, h = divmod(k, 2)
                v.wait_ge(s["u1_mm"], k + 1)
                return inverse(rc[:, n, gs(h)], products(U_BANK[k])[:, :, D:D + NJ])

            done = inverse1(0)
            for k in range(4):
                n, h = divmod(k, 2)
                ready = normaliser(rm[:, n, bs(h)], rc[:, n, gs(h)], done, mask_q if n == 0 else mask2[:])
                if k < 3:
                    done = inverse1(k + 1)
                v.wait_ge(s["v_step"], ready)
                blocks(um[:, n, bs(h)], products(U_BANK[k]), rm[:, n, bs(h)]).then_inc(s["um1"], 1)
            v.scalar_tensor_tensor(xb[:], row[:, R_BETA:R_BETA + D], oml[:, 0:1], xs[1][:], ALU.mult, ALU.add).then_inc(s["xb"], 1)
            v.wait_ge(s["a1_mm"], 1)
            a1 = PS[:, 2, 0:D]
            v.bn_stats(st6[:, 5, :], a1).then_inc(s["v_step"], 1)
            v.wait_ge(s["v_step"], step())
            v.bn_aggr(mv[:, 5, :], st6[:, 5, :]).then_inc(s["v_step"], 1)
            v.wait_ge(s["v_step"], step())
            v.tensor_scalar(ve[:, 2:3], mv[:, 5, 1:2], EPS, None, ALU.add).then_inc(s["var"], 1)
            v.wait_ge(s["gl"], 1)
            v.scalar_tensor_tensor(tz[:], a1, mv[:, 5, 0:1], gl[:], ALU.subtract, ALU.mult).then_inc(s["v_step"], 1)
            v.wait_ge(s["v_step"], step())
            v.wait_ge(s["xb"], 1)
            v.wait_ge(s["rstd"], 3)
            v.scalar_tensor_tensor(xs[2][:], tz[:], rs[:, 2:3], xb[:], ALU.mult, ALU.add).then_inc(s["x"], 1)

            v.wait_ge(s["x"], 2)
            v.bn_stats(st6[:, 2, :], xs[2][:]).then_inc(s["v_step"], 1)
            v.wait_ge(s["v_step"], step())
            v.bn_aggr(mv[:, 2, :], st6[:, 2, :]).then_inc(s["v_step"], 1)
            v.wait_ge(s["v_step"], step())
            v.tensor_scalar(ve[:, 3:4], mv[:, 2, 1:2], 1.0 + RMS_EPS, RMS_EPS * EPS, ALU.mult, ALU.add).then_inc(s["var"], 1)
            v.wait_ge(s["rstd"], 4)
            v.wait_ge(s["yN_turned"], 2)
            v.tensor_scalar(yN[:], xs[2][:], mv[:, 2, 0:1], rs[:, 3:4], ALU.subtract, ALU.mult).then_inc(s["yN"], 1)
            v.wait_ge(s["yN_turned"], 3)
            v.tensor_scalar(yT[:], PS[:, 7, 0:P], cv(C_LNW), None, ALU.mult).then_inc(s["yT"], 1)

            def route(n, bias):
                v.wait_ge(s["lg_mm"], n + 1)
                lgp = PS[:, 6, 0:E0N]
                if bias is None:
                    v.tensor_copy(lg[:, n], lgp).then_inc(s["lg"], 1)
                else:
                    v.tensor_tensor(lg[:, n], lgp, bias, ALU.add).then_inc(s["lg"], 1)
                v.wait_ge(s["lg"], n + 1)
                v.max(top[:, n], lg[:, n]).then_inc(s["v_step"], 1)
                v.wait_ge(s["v_step"], step())
                v.max_index(idx[:, n], top[:, n], lg[:, n]).then_inc(s["v_step"], 1)
                v.wait_ge(s["v_step"], step())
                v.tensor_copy(idf[:, n], idx[:, n]).then_inc(s["idf"], 1)

            def gate0(e, f):
                n = e * FC0 + f
                v.wait_ge(s["ab_mm"], ab_ready(e, f))
                v.wait_ge(s["sa"], n + 1)
                if e >= 2 and f == 0:
                    v.wait_ge(s["y_mm"], e - 1)
                v.scalar_tensor_tensor(hT[:, e % 2, f], PS[:, ab_banks(e, f)[1], f * P:(f + 1) * P],
                                       cv(C_B1B + n), sa[:, n % 4], ALU.add, ALU.mult).then_inc(s["hT"], 1)

            def add0(e):
                v.wait_ge(s["y_mm"], e + 1)
                v.wait_ge(s["acc"], e + 1)
                v.scalar_tensor_tensor(acc[:, (e + 1) % 2] if e < E0N - 1 else xs[3][:],
                                       PS[:, y0_bank(e), 0:D], oh[:, 2, e:e + 1], acc[:, e % 2],
                                       ALU.mult, ALU.add).then_inc(s["acc"], 1)

            for f in range(FC0):
                gate0(0, f)
            route(0, row[:, R_BG:R_BG + E0N])
            v.tensor_tensor(tw[:, 0:1], top[:, 0, 1:2], top[:, 0, 0:1], ALU.subtract).then_inc(s["tw_d"], 1)
            for f in range(FC0):
                gate0(1, f)
            v.wait_ge(s["tw_e"], 1)
            v.tensor_scalar(tw[:, 2:3], tw[:, 1:2], 1.0, None, ALU.add).then_inc(s["v_step"], 1)
            v.wait_ge(s["v_step"], step())
            v.reciprocal(tw[:, 3:4], tw[:, 2:3]).then_inc(s["v_step"], 1)
            v.wait_ge(s["v_step"], step())
            v.tensor_tensor(tw[:, 4:5], tw[:, 1:2], tw[:, 3:4], ALU.mult).then_inc(s["v_step"], 1)
            v.wait_ge(s["v_step"], step())
            v.wait_ge(s["idf"], 1)
            v.tensor_scalar(oh[:, 0], iota, idf[:, 0, 0:1], tw[:, 3:4], ALU.is_equal, ALU.mult).then_inc(s["oh"], 1)
            v.tensor_scalar(oh[:, 1], iota, idf[:, 0, 1:2], tw[:, 4:5], ALU.is_equal, ALU.mult).then_inc(s["oh"], 1)
            v.wait_ge(s["oh"], 2)
            v.tensor_tensor(oh[:, 2], oh[:, 0], oh[:, 1], ALU.add).then_inc(s["we"], 1)

            v.wait_ge(s["we_turned"], 1)
            v.tensor_copy(weT[:], PS[0:E0N, 6, 0:P]).then_inc(s["weT"], 1)
            for e in range(2, E0N):
                if e == 3:
                    v.wait_ge(s["b2_mm"], 1)
                    v.tensor_tensor(acc[:, 0], PS[:, 6, 0:P], xs[2][:], ALU.add).then_inc(s["acc"], 1)
                    add0(0)
                for f in range(FC0):
                    gate0(e, f)
                if e == 3:
                    add0(1)
                if e >= 3:
                    add0(e - 1)
            add0(E0N - 1)

            v.wait_ge(s["acc"], E0N + 1)
            layernorm(4, 3)
            v.wait_ge(s["yN_turned"], 4)
            v.tensor_copy(yT[:], PS[:, 7, 0:P]).then_inc(s["yT"], 1)
            v.wait_ge(s["qx_mm"], 1)
            for h in (slice(0, HL), slice(HL, H)):
                n_heads = h.stop - h.start
                v.scalar_tensor_tensor(qbx[0][:, h], PS[:, 7, 0:L].unsqueeze(1).broadcast_to([P, n_heads, L]), cv(C_BQ1),
                                       mask_h[:, h].unsqueeze(2).broadcast_to([P, n_heads, L]),
                                       ALU.add, ALU.mult).then_inc(s["qbx0"], 1)
            v.tensor_scalar(qxT[:], PS[:, 7, 0:P], cv(C_BQ1), None, ALU.add).then_inc(s["qxT"], 1)

            def peak(n):
                v.wait_ge(s["sx_mm"], n + 1)
                v.tensor_reduce(nmx[:, n:n + 1], PS[:, n % NJ, :], AX, ALU.max, negate=True).then_inc(s["nmx"], 1)

            def turned(n):
                v.wait_ge(s["xe_turned"], n + 1)
                if n >= 2 * NJ:
                    v.wait_ge(s["ux_mm"], n // NJ - 1)
                w = slice(0, NCTX if n < B * NJ - 1 else NCTX // 2)
                v.tensor_copy(xeT[n % (2 * NJ)][:, w], PS[:, 5 if n < B * NJ - 1 else 0, w]).then_inc(s["xeT_odd"], 1)

            def norm(b):
                v.wait_ge(s["xe"], NJ * (b + 1))
                v.reciprocal(rx[:, b], smx[:, b * NJ:(b + 1) * NJ]).then_inc(s["v_step"], 1)
                v.wait_ge(s["v_step"], step())
                over_heads(rmx[:, b % 2], rx[:, b]).then_inc(s["rmx"], 1)

            def over_heads(dst, inv):
                return v.tensor_tensor(dst.rearrange("p (j h d) -> p j h d", j=NJ, h=HL),
                                       inv.unsqueeze(2).unsqueeze(3).broadcast_to([P, NJ, HL, DH]),
                                       mask_q.unsqueeze(1).unsqueeze(3).broadcast_to([P, NJ, HL, DH]), ALU.mult)

            def keep_own(b):
                if b < B - 1:
                    v.wait_ge(s["ux_mm"], b + 1)
                else:
                    v.wait_ge(s["rmx_turned"], 1)
                v.tensor_copy(rmT[:, b % 2], PS[:, RX_BANK[b], P:2 * P]).then_inc(s["v_step"], 1)
                v.wait_ge(s["v_step"], step())
                v.wait_ge(s["ux_mm"], b + 1)
                v.tensor_tensor(umx[:, b], PS[:, 6 + b % 2, 0:P], rmT[:, b % 2], ALU.mult).then_inc(s["umx"], 1)

            def fold_heads(b):
                v.wait_ge(s["umx"], b + 1)
                v.tensor_reduce(aTx[:, b * L:(b + 1) * L], umx[:, b].rearrange("p (h t) -> p t h", h=HL), AX,
                                ALU.add).then_inc(s["aTx"], 1)

            v.tensor_tensor(tz[:], xs[3][:], row[:, R_BO:R_BO + D], ALU.add).then_inc(s["x3b"], 1)
            for n in range(B * NJ):
                peak(n)
                if 3 <= n and n % 2:
                    turned(n - 2)
                for part, k in ((norm, 4), (keep_own, 8), (fold_heads, 9)):
                    b = (n - k) // NJ
                    if (n - k) % NJ == 0 and 0 <= b < B - 1:
                        part(b)
            norm(B - 1)
            turned(B * NJ - 1)
            keep_own(B - 2)
            fold_heads(B - 2)
            keep_own(B - 1)
            fold_heads(B - 1)
            v.wait_ge(s["ox_mm"], 1)
            v.wait_ge(s["x3b"], 1)
            v.tensor_tensor(xs[4][:], PS[:, 5, 0:P], tz[:], ALU.add).then_inc(s["x"], 1)

            v.wait_ge(s["x"], 3)
            layernorm(5, 4)
            v.wait_ge(s["yN_turned"], 5)
            v.tensor_copy(yT[:], PS[:, 7, 0:P]).then_inc(s["yT"], 1)
            v.wait_ge(s["q3_mm"], 1)
            for h in range(2):
                spread(qb3[:, bs(h)], PS[:, 6, h * 2 * L:(h + 1) * 2 * L]).then_inc(s["qb3"], 1)
            v.wait_ge(s["s3_mm"], 1)
            for h in range(2):
                v.wait_ge(s["s3_mm"], h + 1)
                softmax_in(ex3[:, bs(h)], mx3[:, gs(h)], PS[:, h, 0:2 * P]).then_inc(s["ex3_sub"], 1)
            ready = [0, 0]
            for h in range(2):
                v.wait_ge(s["ex3"], h + 1)
                v.tensor_reduce(sm3[:, gs(h)], ex3[:, bs(h)].rearrange("p b (j s) -> p (b j) s", s=L), AX, ALU.add).then_inc(s["v_step"], 1)
                v.wait_ge(s["v_step"], step())
                done = inverse(rc3[:, gs(h)], sm3[:, gs(h)].rearrange("p (b j) -> p b j", b=2))
                ready[h] = normaliser(rm3[:, bs(h)], rc3[:, gs(h)], done, mask_q)
            for h in range(2):
                v.wait_ge(s["u3_mm"], h + 1)
                v.wait_ge(s["v_step"], ready[h])
                blocks(um3[:, bs(h)], products(5 + h), rm3[:, bs(h)]).then_inc(s["um3"], 1)
            v.wait_ge(s["a3_mm"], 1)
            v.tensor_copy(aT3[:], PS[:, 4, 0:P]).then_inc(s["aT3"], 1)
            v.tensor_tensor(tz[:], xs[4][:], row[:, R_BPROJ:R_BPROJ + D], ALU.add).then_inc(s["v_step"], 1)
            v.wait_ge(s["v_step"], step())
            v.wait_ge(s["o3_mm"], 1)
            v.tensor_tensor(xs[5][:], PS[:, 7, 0:P], tz[:], ALU.add).then_inc(s["x"], 1)

            v.wait_ge(s["x"], 4)
            layernorm(6, 5)
            v.wait_ge(s["yN_turned"], 6)
            v.tensor_copy(yT[:], PS[:, 7, 0:P]).then_inc(s["yT"], 1)
            route(1, None)
            v.wait_ge(s["idf"], 2)
            v.tensor_scalar(oh[:, 3], iota, idf[:, 1, 0:1], None, ALU.is_equal).then_inc(s["oh3"], 1)

            def gate1(n):
                v.wait_ge(s["sa1"], n + 1)
                if n >= 3:
                    v.wait_ge(s["y1_mm"], n - 2)
                v.tensor_tensor(hT1[:, n % 3], PS[:, n % 4, 256:512].rearrange("p (f t) -> p f t", f=FC1),
                                sa1[:, n % 3], ALU.mult).then_inc(s["hT1"], 1)

            def add1(n):
                v.wait_ge(s["y1_mm"], n + 1)
                src = PS[:, y1_bank(n), 0:D]
                if n == 0:
                    v.tensor_tensor(acc1[:, 0], src, xs[5][:], ALU.add).then_inc(s["acc1"], 1)
                else:
                    v.wait_ge(s["acc1"], n)
                    v.wait_ge(s["oh3"], 1)
                    last = v.scalar_tensor_tensor(acc1[:, n % 2] if n < E1N else xs[6][:], src, oh[:, 3, n - 1:n],
                                                  acc1[:, (n - 1) % 2], ALU.mult, ALU.add)
                    last.then_inc(s["acc1"] if n < E1N else s["x"], 1)

            gate1(0)
            for n in range(1, E1N - 1):
                gate1(n)
                add1(n - 1)
            gate1(E1N - 1)
            gate1(E1N)
            add1(E1N - 2)
            add1(E1N - 1)
            add1(E1N)

        @block.scalar
        def _(a):
            def bg_out(u):
                a.wait_ge(s["bg_mm"], u + 1)
                src = PS[:, bg_bank(u), :]
                if u < B:
                    a.activation(kx[:, u], src, ACT.Identity, bias=cv(C_BK1)).then_inc(s["bg_out"], 1)
                else:
                    a.activation(vx[:, u - B].rearrange("p c k -> p (c k)"), src, ACT.Copy).then_inc(s["bg_out"], 1)

            values = vb[:, :, 0:D].rearrange("p b (j w) -> p b j w", j=NJ)

            def diagonal(dst, src):
                for q in range(NJ):
                    r = slice(q * QW, (q + 1) * QW)
                    last = a.activation(dst[r, :, q], src[r], ACT.Copy)
                return last

            a.wait_ge(s["half"], 1)
            a.activation(warm[:], half[:], ACT.Exp)
            a.wait_ge(s["col_in"], 16)
            a.wait_ge(s["kc_mm"], 1)
            a.activation(kcT[:], PS[:, 6, 0:P], ACT.Identity, bias=cv(C_BKC)).then_inc(s["kcT"], 1)
            a.wait_ge(s["m0b"], 1)
            a.activation(e0[:], PS[:, 0, :], ACT.Exp, bias=m0[:, 1:2], accum_out=m0[:, 2:3]).then_inc(s["e0"], 1)
            a.wait_ge(s["qs_mm"], 1)
            a.activation(qsT[:].rearrange("p r t -> p (r t)"), PS[:, 3, 0:2 * P], ACT.Identity, bias=cv(C_BQS)).then_inc(s["qsT"], 1)
            a.wait_ge(s["p0_turned"], 1)
            a.activation(p0T[:, 2:4, :], PS[:, 6, 0:2 * P].rearrange("p (c k) -> p c k", c=2), ACT.Copy).then_inc(s["p0T_b"], 1)
            a.wait_ge(s["vc_mm"], 1)
            a.activation(vc[:], PS[:, 7, 0:P], ACT.Copy).then_inc(s["vc"], 1)
            a.wait_ge(s["s2"], 1)
            a.activation(e2[:], s2[:], ACT.Exp, scale=SC0).then_inc(s["e2"], 1)
            a.wait_ge(s["g_mm"], 1)
            a.wait_ge(s["hbg"], 1)
            a.activation(th[:], PS[:, 6, 0:P], ACT.Tanh, bias=hbg[:, 0:1], scale=0.5).then_inc(s["th"], 1)
            for u in range(3):
                bg_out(u)

            a.wait_ge(s["zeros"], 1)
            for n in range(2):
                a.wait_ge(s["k12_mm"], n + 1)
                diagonal(kb[:, n], PS[:, 5 - n, 0:P].rearrange("p (b s) -> p b s", b=B)).then_inc(s["kb"], 1)

            def exp1(k):
                n, h = divmod(k, 2)
                part = ex[:, n, bs(h)].rearrange("p b k -> p (b k)")
                a.wait_ge(s["ex1_sub"], k + 1)
                a.activation(part, part, ACT.Exp, scale=SCH).then_inc(s["ex1"], 1)

            def turned1(k):
                n, h = divmod(k, 2)
                a.wait_ge(s["e1_turned"], k + 1)
                a.activation(eT[:, n, bs(h)].rearrange("p b k -> p (b k)"), PS[:, T_BANK[k], 0:2 * P], ACT.Copy).then_inc(s["eT"], 1)

            exp1(0)
            a.wait_ge(s["v1_mm"], 1)
            diagonal(values, PS[:, 0, 0:P].rearrange("p (b w) -> p b w", b=B)).then_inc(s["vb"], 1)
            for k in range(3):
                exp1(k + 1)
                turned1(k)
            turned1(3)
            a.activation(warm[:], half[:], ACT.Silu)
            bg_out(3)

            for e in range(E0N):
                for f in range(FC0):
                    n = e * FC0 + f
                    a.wait_ge(s["ab_mm"], ab_ready(e, f))
                    if n >= 4:
                        a.wait_ge(s["hT"], n - 3)
                    a.activation(sa[:, n % 4], PS[:, ab_banks(e, f)[0], f * P:(f + 1) * P], ACT.Silu, bias=cv(C_B1A + n)).then_inc(s["sa"], 1)

            def ex_tile(n):
                a.wait_ge(s["nmx"], n + 1)
                if n >= 3:
                    a.wait_ge(s["xe_turned"], n - 2)
                a.activation(xe[:, n % 3], PS[:, n % NJ, :], ACT.Exp, bias=nmx[:, n:n + 1],
                             accum_out=smx[:, n:n + 1]).then_inc(s["xe"], 1)

            def turned(n):
                a.wait_ge(s["xe_turned"], n + 1)
                if n >= 2 * NJ:
                    a.wait_ge(s["ux_mm"], n // NJ - 1)
                a.activation(xeT[n % (2 * NJ)], PS[:, 4, :], ACT.Copy).then_inc(s["xeT_even"], 1)

            for u in range(B, 2 * B):
                bg_out(u)
            for n in range(B * NJ + 1):
                if n < B * NJ:
                    ex_tile(n)
                if n % 2:
                    turned(n - 1)
            a.wait_ge(s["xe_turned"], B * NJ)
            half_tile = slice(NCTX // 2, NCTX)
            a.activation(xeT[2 * NJ - 1][:, half_tile], PS[:, 1, half_tile], ACT.Copy).then_inc(s["xeT_last"], 1)

            a.wait_ge(s["k3_mm"], 1)
            diagonal(kb3, PS[:, 5, 0:P].rearrange("p (b s) -> p b s", b=B)).then_inc(s["kb"], 1)
            a.wait_ge(s["v3_mm"], 1)
            diagonal(values, PS[:, 4, 0:P].rearrange("p (b w) -> p b w", b=B)).then_inc(s["vb3"], 1)
            for h in range(2):
                part = ex3[:, 2 * h:2 * h + 2].rearrange("p b k -> p (b k)")
                a.wait_ge(s["ex3_sub"], h + 1)
                a.activation(part, part, ACT.Exp, scale=SCH).then_inc(s["ex3"], 1)
            for h in range(2):
                a.wait_ge(s["e3_turned"], h + 1)
                a.activation(eT3[:, 2 * h:2 * h + 2].rearrange("p b k -> p (b k)"), PS[:, 2 + h, 0:2 * P], ACT.Copy).then_inc(s["eT3"], 1)

            for n in range(E1N + 1):
                a.wait_ge(s["gu_mm"], n + 1)
                if n >= 3:
                    a.wait_ge(s["hT1"], n - 2)
                a.activation(sa1[:, n % 3], PS[:, n % 4, 0:256].rearrange("p (f t) -> p f t", f=FC1), ACT.Silu).then_inc(s["sa1"], 1)

        @block.tensor
        def _(t):
            def mm(o, lhsT, rhs, start=True, stop=True):
                return t.matmul(o, lhsT, rhs, start=start, stop=stop, skip_group_check=True)

            def turn_y(n):
                t.wait_ge(s["yN"], n)
                t.transpose(PS[:, 7, 0:P], yN[:], ident).then_inc(s["yN_turned"], 1)

            def fill(bank, n):
                for _ in range(n):
                    mm(PS[:, bank, 0:P], blank[:], blank[:])

            piece = [0]

            def bg(n):
                for k in range(piece[0], piece[0] + n):
                    u, c = divmod(k, KC)
                    if k == 0:
                        t.wait_ge(s["w2_in"], 16)
                    if 2 <= u < B and c == 0:
                        t.wait_ge(s["bg_out"], u - 1)
                    part = ctxT[:, (u % B) * NCTX + c * P:(u % B) * NCTX + (c + 1) * P]
                    o = PS[:, bg_bank(u), c * P:(c + 1) * P]
                    last = mm(o, w2[:, 1], part) if u < B else mm(o, part, w2[:, 2])
                    if c == KC - 1:
                        last.then_inc(s["bg_mm"], 1)
                piece[0] += n

            t.wait_ge(s["blank"], 1)
            fill(1, FILL["start"])
            t.wait_ge(s["con_in"], 16)
            turn_y(1)
            fill(1, FILL["y1"])
            t.wait_ge(s["w0_in"], 16)
            t.wait_ge(s["yT"], 1)
            mm(PS[:, 7, 0:P], w0[:, 0], yT[:]).then_inc(s["qc_mm"], 1)
            fill(1, FILL["qc"])
            t.wait_ge(s["qcT"], 1)
            mm(PS[:, 7, 0:P], w0[:, 1], qcT[:])
            mm(PS[:, 7, P:P + 1], qcT[:], cv(C_BKS)).then_inc(s["qp_mm"], 1)
            fill(1, FILL["qp"])
            t.wait_ge(s["ctxT_in"], 16)
            t.wait_ge(s["qpT"], 1)
            for b in range(B):
                last = mm(PS[b * L:(b + 1) * L, 0, :], qpT[:, b * L:(b + 1) * L], ctxT[:, b * NCTX:(b + 1) * NCTX])
            last.then_inc(s["s0_mm"], 1)
            t.wait_ge(s["w0_rest_in"], 16)
            mm(PS[:, 6, 0:P], w0[:, 4], yT[:]).then_inc(s["kc_mm"], 1)
            near = ctxT[:].rearrange("c (b i r) -> c r b i", b=B, r=R)
            for r in range(2):
                last = mm(PS[:, 3, r * P:(r + 1) * P], w0[:, 3], near[:, LO + r])
            last.then_inc(s["qs_mm"], 1)
            t.wait_ge(s["qbk"], 1)
            mm(PS[:, 7, 0:P], yT[:], w0[:, 5]).then_inc(s["vc_mm"], 1)
            fill(1, FILL["s2"])
            t.wait_ge(s["e0"], 1)
            for c in range(KC):
                last = t.transpose(PS[:, 4 + 2 * (c // 2), (c % 2) * P:(c % 2 + 1) * P], e0[:, c * P:(c + 1) * P], ident)
            last.then_inc(s["p0_turned"], 1)
            t.wait_ge(s["qsT"], 1)
            t.wait_ge(s["kcT"], 1)
            for r in range(2):
                for b in range(B):
                    last = mm(PS[b * L:(b + 1) * L, 5, 256 + r * L:256 + (r + 1) * L],
                              qsT[:, r, b * L:(b + 1) * L], kcT[:, b * L:(b + 1) * L])
            last.then_inc(s["s2_mm"], 1)
            fill(1, FILL["p0"])
            t.wait_ge(s["p0T_a"], 1)
            t.wait_ge(s["p0T_b"], 1)
            t.wait_ge(s["ctxN_in"], 16)
            for c in range(KC):
                for b in range(B):
                    last = mm(PS[b * L:(b + 1) * L, 0, 0:D], p0T[:, c, b * L:(b + 1) * L], ctxN[:, b * KC + c],
                              start=(c == 0), stop=(c == KC - 1))
            last.then_inc(s["pc_mm"], 1)
            fill(1, FILL["pc"])
            t.wait_ge(s["pcN"], 1)
            t.transpose(PS[:, 1, 0:P], pcN[:], ident).then_inc(s["pc_turned"], 1)
            t.wait_ge(s["paBD"], 1)
            t.wait_ge(s["vc"], 1)
            mm(PS[:, 5, 384:384 + P], vc[:], paBD[:]).then_inc(s["s2c_mm"], 1)
            t.wait_ge(s["pcT"], 1)
            mm(PS[:, 7, 0:P], w0[:, 2], pcT[:]).then_inc(s["c2s_mm"], 1)
            fill(1, FILL["c2s"])
            t.wait_ge(s["s2cT"], 1)
            t.wait_ge(s["c2sT"], 1)
            mm(PS[:, 6, 0:P], w0[:, 7], s2cT[:], stop=False)
            mm(PS[:, 6, 0:P], w0[:, 6], c2sT[:], start=False).then_inc(s["g_mm"], 1)
            bg(PIECES["g"])
            fill(1, FILL["g"])
            t.wait_ge(s["oT0"], 1)
            t.transpose(PS[:, 4, 0:P], oT0[:], ident).then_inc(s["o0_turned"], 1)
            bg(PIECES["o0"])

            turn_y(2)
            fill(1, FILL["y2"])
            t.wait_ge(s["yT"], 2)
            t.wait_ge(s["w1_in"], 16)
            mm(PS[:, 5, 0:P], w1[:, 1], yT[:]).then_inc(s["k12_mm"], 1)
            mm(PS[:, 6, 0:P], w1[:, 0], yT[:]).then_inc(s["q12_mm"], 1)
            mm(PS[:, 7, 0:P], w1[:, 2], yT[:]).then_inc(s["q12_mm"], 1)
            mm(PS[:, 4, 0:P], w1[:, 3], yT[:]).then_inc(s["k12_mm"], 1)

            def values_mm(bank, w):
                for b in range(B):
                    for q in range(NJ):
                        last = mm(PS[q * L:(q + 1) * L, bank, b * QW:(b + 1) * QW], yT[:, b * L:(b + 1) * L], w[:, q * QW:(q + 1) * QW])
                return last

            def score1(k, batches):
                n = k // 2
                for b in batches:
                    last = mm(PS[:, S_BANK[k], b * P:(b + 1) * P], qb[:, n, b].rearrange("p h t -> p (h t)"),
                              kb[:, n, b].rearrange("p j s -> p (j s)"))
                last.then_inc(s["s1_mm"], 1)

            t.wait_ge(s["qb"], 1)
            t.wait_ge(s["kb"], 1)
            score1(0, (0, 1))
            t.wait_ge(s["qb"], 2)
            score1(1, (2, 3))
            values_mm(0, w1[:, 4]).then_inc(s["v1_mm"], 1)
            t.wait_ge(s["qb"], 3)
            t.wait_ge(s["kb"], 2)
            score1(2, range(B))
            bg(PIECES["s1"])

            def turn1(k):
                n, h = divmod(k, 2)
                t.wait_ge(s["ex1"], k + 1)
                if k == 3:
                    t.wait_ge(s["eT"], 1)
                for b in range(2):
                    last = t.transpose(PS[:, T_BANK[k], b * P:(b + 1) * P], ex[:, n, 2 * h + b], ident)
                last.then_inc(s["e1_turned"], 1)

            def products(bank, eT_of, h):
                for b in range(2):
                    last = mm(PS[:, bank, b * (D + NJ):(b + 1) * (D + NJ)], eT_of[:, 2 * h + b], vb[:, 2 * h + b])
                return last

            def value1(k):
                t.wait_ge(s["eT"], k + 1)
                products(U_BANK[k], eT[:, k // 2], k % 2).then_inc(s["u1_mm"], 1)

            turn1(0)
            turn1(1)
            fill(1, FILL["e1"])
            t.wait_ge(s["vb"], 1)
            t.wait_ge(s["vb_ones"], 1)
            value1(0)
            turn1(2)
            value1(1)
            turn1(3)
            value1(2)
            value1(3)
            t.wait_ge(s["bg_out"], 3)
            for k in range(4):
                n, h = divmod(k, 2)
                t.wait_ge(s["um1"], k + 1)
                for b in (2 * h, 2 * h + 1):
                    last = mm(PS[b * L:(b + 1) * L, 2, 0:D], sel, um[:, n, b], start=(n == 0), stop=(n == 1))
            last.then_inc(s["a1_mm"], 1)
            bg(B * KC - piece[0])
            fill(1, FILL["a1"])

            turn_y(3)
            fill(1, FILL["y3"])
            t.wait_ge(s["yT"], 3)

            def up0(e):
                if e % 2 == 0:
                    t.wait_ge(s[f"wab{e}_in"], 16)
                if e < 2:
                    t.wait_ge(s["bg_out"], 3 + e)
                else:
                    t.wait_ge(s["hT"], FC0 * (e - 1))
                for f in range(FC0):
                    bank_a, bank_b = ab_banks(e, f)
                    mm(PS[:, bank_a, f * P:(f + 1) * P], wab[:, e, 0, f * P:(f + 1) * P], yT[:])
                    last = mm(PS[:, bank_b, f * P:(f + 1) * P], wab[:, e, 1, f * P:(f + 1) * P], yT[:])
                    if f == FC0 - 1 or (e == E0N - 1 and f == FC0 // 2 - 1):
                        last.then_inc(s["ab_mm"], 1)

            def down0(e):
                if e % 2 == 0:
                    t.wait_ge(s[f"wdn{e}_in"], 16)
                if e >= 3:
                    t.wait_ge(s["acc"], e if e > 4 else e - 1)
                for f in range(FC0):
                    t.wait_ge(s["hT"], FC0 * e + f + 1)
                    last = mm(PS[:, y0_bank(e), 0:D], hT[:, e % 2, f], wdn[:, e, f], start=(f == 0), stop=(f == FC0 - 1))
                last.then_inc(s["y_mm"], 1)

            up0(0)
            t.wait_ge(s["wr_in"], 16)
            mm(PS[:, 6, 0:E0N], yT[:], wr[:, 0]).then_inc(s["lg_mm"], 1)
            for e in range(E0N):
                if e + 1 < E0N:
                    up0(e + 1)
                if e == 2:
                    t.wait_ge(s["weT"], 1)
                    t.wait_ge(s["b2_in"], 16)
                    mm(PS[:, 6, 0:P], weT[:], b2[:]).then_inc(s["b2_mm"], 1)
                down0(e)
                if e == 1:
                    t.wait_ge(s["we"], 1)
                    t.transpose(PS[0:E0N, 6, 0:P], oh[:, 2], ident).then_inc(s["we_turned"], 1)

            bg(PIECES["x"])
            turn_y(4)
            bg(PIECES["y4"])
            t.wait_ge(s["yT"], 4)
            mm(PS[:, 7, 0:P], w2[:, 0], yT[:]).then_inc(s["qx_mm"], 1)
            bg(2 * B * KC - piece[0])
            t.wait_ge(s["acc"], E0N + 1)

            def score(n):
                b, j = divmod(n, NJ)
                if n < 2:
                    t.wait_ge(s["qbx0"], n + 1)
                if b and j == 0:
                    t.wait_ge(s["qbx"], b)
                if n < NJ:
                    t.wait_ge(s["bg_out"], B + n + 1)
                else:
                    t.wait_ge(s["xe"], n - NJ + 1)
                mm(PS[:, j, :], qbx[b][:, j * HL:(j + 1) * HL].rearrange("p h t -> p (h t)"), kx[:, b]).then_inc(s["sx_mm"], 1)

            def copied(n):
                if n == B * NJ - 1:
                    t.wait_ge(s["xeT_last"], 1)
                t.wait_ge(s["xeT_odd"] if n % 2 else s["xeT_even"], n // 2 + 1)

            def turn(n):
                t.wait_ge(s["xe"], n + 1)
                if 2 <= n < B * NJ - 1:
                    copied(n - 2)
                for c in range(KC):
                    bank = 4 + n % 2 if n < B * NJ - 1 else 2 * c // KC
                    last = t.transpose(PS[:, bank, c * P:(c + 1) * P], xe[:, n % 3, c * P:(c + 1) * P], ident)
                last.then_inc(s["xe_turned"], 1)

            def values(b):
                if b >= 2:
                    t.wait_ge(s["umx"], b - 1)
                t.wait_ge(s["rmx"], b + 1)
                last = t.transpose(PS[:, RX_BANK[b], P:2 * P], rmx[:, b % 2], ident)
                if b == B - 1:
                    last.then_inc(s["rmx_turned"], 1)
                for n in range(NJ * b, NJ * (b + 1)):
                    copied(n)
                for c in range(KC):
                    for j in range(NJ):
                        q = slice(j * QW, (j + 1) * QW)
                        last = mm(PS[q, 6 + b % 2, 0:P], vx[:, b, c, q], xeT[(NJ * b + j) % (2 * NJ)][:, c * P:(c + 1) * P],
                                  start=(c == 0), stop=(c == KC - 1))
                last.then_inc(s["ux_mm"], 1)

            score(0)
            score(1)
            for n in range(B * NJ):
                if n + 2 < B * NJ:
                    score(n + 2)
                if n:
                    turn(n - 1)
                if (n - 5) % NJ == 0 and n >= 5:
                    values((n - 5) // NJ)
            turn(B * NJ - 1)
            values(B - 1)
            mm(PS[:, 5, 0:P], cv(C_BV1).broadcast_to([P, P]), w2[:, 3], stop=False)
            fill(3, FILL["un"])
            t.wait_ge(s["aTx"], B)
            mm(PS[:, 5, 0:P], aTx[:], w2[:, 3], start=False).then_inc(s["ox_mm"], 1)

            for h in range(2):
                mm(PS[:, h, 0:2 * P].rearrange("p (b k) -> p b k", b=2), ident, alibi.unsqueeze(1).broadcast_to([P, 2, NJ * L]),
                   stop=False)
            fill(3, FILL["ox"])
            turn_y(5)
            fill(3, FILL["y5"])
            t.wait_ge(s["yT"], 5)
            mm(PS[:, 5, 0:P], w2[:, 5], yT[:]).then_inc(s["k3_mm"], 1)
            mm(PS[:, 6, 0:P], w2[:, 4], yT[:]).then_inc(s["q3_mm"], 1)
            values_mm(4, w2[:, 6]).then_inc(s["v3_mm"], 1)
            fill(3, FILL["v3"])
            t.wait_ge(s["kb"], 3)
            for b in range(B):
                if b % 2 == 0:
                    t.wait_ge(s["qb3"], b // 2 + 1)
                last = mm(PS[:, b // 2, b % 2 * P:(b % 2 + 1) * P], qb3[:, b].rearrange("p h t -> p (h t)"),
                          kb3[:, b].rearrange("p j s -> p (j s)"), start=False)
                if b % 2:
                    last.then_inc(s["s3_mm"], 1)
            fill(3, FILL["s3"])
            for b in range(B):
                if b % 2 == 0:
                    t.wait_ge(s["ex3"], b // 2 + 1)
                last = t.transpose(PS[:, 2 + b // 2, b % 2 * P:(b % 2 + 1) * P], ex3[:, b], ident)
                if b % 2:
                    last.then_inc(s["e3_turned"], 1)
            t.wait_ge(s["vb3"], 1)
            for h in range(2):
                t.wait_ge(s["eT3"], h + 1)
                products(5 + h, eT3, h).then_inc(s["u3_mm"], 1)
            for b in range(B):
                if b % 2 == 0:
                    t.wait_ge(s["um3"], b // 2 + 1)
                last = mm(PS[:, 4, b * L:(b + 1) * L], um3[:, b], sel)
            last.then_inc(s["a3_mm"], 1)
            fill(3, FILL["a3"])
            t.wait_ge(s["aT3"], 1)
            mm(PS[:, 7, 0:P], aT3[:], w2[:, 7]).then_inc(s["o3_mm"], 1)

            fill(3, FILL["o3"])
            turn_y(6)
            fill(3, FILL["y6"])
            t.wait_ge(s["yT"], 6)
            t.wait_ge(s["wgu_in"], 16)
            t.wait_ge(s["wdo_in"], 16)

            def up1(n):
                if n >= 4:
                    t.wait_ge(s["hT1"], n - 3)
                for k in range(2):
                    for f in range(FC1):
                        last = mm(PS[:, n % 4, (k * FC1 + f) * P:(k * FC1 + f + 1) * P], wgu[:, n, k, f * P:(f + 1) * P], yT[:])
                last.then_inc(s["gu_mm"], 1)

            def down1(n):
                if 2 <= n < E1N:
                    t.wait_ge(s["acc1"], n - 1)
                t.wait_ge(s["hT1"], n + 1)
                for f in range(FC1):
                    last = mm(PS[:, y1_bank(n), 0:D], hT1[:, n % 3, f], wdo[:, n, f], start=(f == 0), stop=(f == FC1 - 1))
                last.then_inc(s["y1_mm"], 1)

            up1(0)
            mm(PS[:, 6, 0:E0N], yT[:], wr[:, 1]).then_inc(s["lg_mm"], 1)
            up1(1)
            for n in range(E1N + 1):
                if n + 2 <= E1N:
                    up1(n + 2)
                down1(n)


def kernel(**inputs):
    import concourse.bacc as bacc
    from concourse.bass_utils import run_bass_kernel_spmd

    I = {k: np.asarray(a) for k, a in inputs.items()}
    ctx = I["ctx_1024"].reshape(B * NCTX, D)

    def stack(*ws):
        return np.stack(ws, 1)

    def heads(w):
        return w.transpose(1, 0, 2).reshape(D, D)

    def chunks(w):
        return w.reshape(w.shape[0], -1, P, w.shape[2]).transpose(2, 0, 1, 3)

    x0, x1 = "L0_xattn_", "L1_xattn_"
    cols = [I[x0 + n] for n in ("bq_c", "bk_s", "bv_s", "bq_s", "bk_c", "bv_c", "bg")]
    cols += [I["L0_ffn_ln_w"], I[x1 + "bq"], I[x1 + "bk"], I[x1 + "bv"]]
    cols += list(I["L0_ffn_b1a"].reshape(-1, P)) + list(I["L0_ffn_b1b"].reshape(-1, P))
    up = np.concatenate([I["L1_ffn_w_up_s"][None], I["L1_ffn_up"]])
    gate = np.concatenate([I["L1_ffn_w_gate_s"][None], I["L1_ffn_gate"]])
    down = np.concatenate([I["L1_ffn_w_down_s"][None], I["L1_ffn_down"]])
    arrays = {
        "x": I["x"].reshape(P, D),
        "con": shape_constants(),
        "col": np.stack(cols, 1),
        "row": np.concatenate([I["L0_attn_ln_gamma"], I["L0_attn_ln_beta"], I[x1 + "bo"], I["L1_attn_b_proj"],
                               I["L0_ffn_bg"], I["L0_attn_lamb"].reshape(1)]),
        "w0": stack(I[x0 + "Wq_c"].T, I[x0 + "Wk_s"], I[x0 + "Wv_s"].T, I[x0 + "Wq_s"].T, I[x0 + "Wk_c"].T,
                    I[x0 + "Wv_c"].T, I[x0 + "Wg"][:, :D].T, I[x0 + "Wg"][:, D:].T),
        "w1": stack(*[heads(I["L0_attn_" + n]) for n in ("wq1", "wk1", "wq2", "wk2", "wv")]),
        "w2": stack(I[x1 + "Wq"].T, I[x1 + "Wk"].T, I[x1 + "Wv"].T, I[x1 + "Wo"].T, I["L1_attn_W_query"],
                    I["L1_attn_W_key"], I["L1_attn_W_value"], I["L1_attn_W_proj"]),
        "wr": stack(I["L0_ffn_Wg"], I["L1_ffn_router"].T),
        "b2": I["L0_ffn_b2"],
        "ctxT": ctx.T,
        "ctxN": ctx.reshape(B * KC, P, D).transpose(1, 0, 2),
        "wab": np.stack([I["L0_ffn_W1a"], I["L0_ffn_W1b"]]).transpose(2, 1, 0, 3),
        "wdn": chunks(I["L0_ffn_W2"]),
        "wgu": np.stack([gate, up]).transpose(3, 1, 0, 2),
        "wdo": chunks(down.transpose(0, 2, 1)),
    }
    nc = bacc.Bacc("TRN2", target_bir_lowering=False, num_devices=1)
    A = {}
    for name, a in arrays.items():
        arrays[name] = a = np.ascontiguousarray(a)
        A[name] = nc.dram_tensor(f"in_{name}", a.shape, mybir.dt.from_np(a.dtype), kind="ExternalInput").ap()
    out = nc.dram_tensor("out_x", (P, D), F32, kind="ExternalOutput").ap()
    build(nc, A, out)
    r = run_bass_kernel_spmd(nc, [{f"in_{k}": a for k, a in arrays.items()}], core_ids=[0])
    return r.results[0]["out_x"].reshape(B, L, D)
```
